# Optimizing a Trainium2 kernel written in Bass

```python
import numpy as np
import jax
import jax.numpy as jnp

def _softmax(x, axis=-1):
    return jax.nn.softmax(x, axis=axis)

def _gelu(x):
    return jax.nn.gelu(x, approximate=True)

def _silu(x):
    return jax.nn.silu(x)

def _sigmoid(x):
    return jax.nn.sigmoid(x)

def _layernorm(x, axis=-1, eps=1e-05):
    m = jnp.mean(x, axis=axis, keepdims=True)
    v = jnp.var(x, axis=axis, keepdims=True)
    return (x - m) / jnp.sqrt(v + eps)

def _scatter_add(tgt, idx, src, axis=0):
    return tgt.at[idx].add(src)

def _segment_sum(src, seg, n):
    return jax.ops.segment_sum(src, seg, n)
kernel_name = 'mk_flamingo_gated_d1_seqx_r8_895510'

def setup_inputs(seed: int=0):
    np.random.seed(seed)
    _w = jnp.asarray

    def _rec_inputs():
        import jax
        import jax.numpy as jnp
        _rk = jax.random.key(seed)
        x = -0.0002928 + 1 * jax.random.normal(jax.random.fold_in(_rk, 1), (32, 64, 256), jnp.float32)
        _lenS = 64 - jax.random.randint(jax.random.fold_in(_rk, 7), (32,), 0, max(1, 64 // 4) + 1, jnp.int32)
        _lenS2 = 64 - jax.random.randint(jax.random.fold_in(_rk, 8), (32,), 0, max(1, 64 // 4) + 1, jnp.int32)
        _ctx_2048P = jax.random.normal(jax.random.fold_in(_rk, 11), (32, 16, 256), jnp.float32)
        _ctx_2048c = jax.random.dirichlet(jax.random.fold_in(_rk, 511), 0.3 * jnp.ones((16,), jnp.float32), (32, 64))
        _ctx_2048t = jnp.einsum('bsk,bkd->bsd', _ctx_2048c, _ctx_2048P)
        _ctx_2048t = _ctx_2048t * jax.lax.rsqrt(jnp.mean(jnp.square(_ctx_2048t)) + 1e-12) * 0.953939
        ctx_2048 = -1.39393e-06 + 0.999914 * (_ctx_2048t + 0.3 * jax.random.normal(jax.random.fold_in(_rk, 611), (32, 64, 256), jnp.float32))
        _g = jax.random.normal(jax.random.fold_in(_rk, 9001), (2, 1), jnp.float32)
        _g = jnp.sign(_g) * jnp.maximum(jnp.abs(_g), 1.0) + (_g == 0) * 1.0
        g_xattn = _g[0]
        g_ffn = _g[1]
        return (x, ctx_2048, g_xattn, g_ffn)
    x, ctx_2048, g_xattn, g_ffn = _rec_inputs()

    def _L0_xattn_setup():
        import jax, jax.numpy as jnp
        import numpy as np
        B, S, E, NH = (2, 128, 256, 16)
        DH = E // NH
        EPS = 1e-06

        def _mlstm_forward(q, k, v, Wi, bi, Wf, bf, ln_scale):
            b, s, e = q.shape
            nh = Wi.shape[1]
            dh = e // nh
            x = jnp.concatenate([q, k, v], axis=-1)
            ig = (x @ Wi + bi).transpose(0, 2, 1)[..., None]
            fg = (x @ Wf + bf).transpose(0, 2, 1)[..., None]
            split = lambda t: t.reshape(b, s, nh, dh).transpose(0, 2, 1, 3)
            qh, kh, vh = (split(q), split(k), split(v))
            log_f = jax.nn.log_sigmoid(fg)
            log_f_cum = jnp.concatenate([jnp.zeros((b, nh, 1, 1), q.dtype), jnp.cumsum(log_f, axis=2)], axis=2)
            fg_mat = log_f_cum - jnp.transpose(log_f_cum, (0, 1, 3, 2))
            ltr = jnp.tril(jnp.ones((s, s), dtype=bool))
            log_fg = jnp.where(ltr, fg_mat[:, :, 1:, 1:], -jnp.inf)
            log_D = log_fg + jnp.transpose(ig, (0, 1, 3, 2))
            max_log_D = jnp.max(log_D, axis=-1, keepdims=True)
            D = jnp.exp(log_D - max_log_D)
            qk = jnp.einsum('bhsd,bhtd->bhst', qh, kh) / jnp.sqrt(jnp.asarray(dh, q.dtype))
            C = qk * D
            normalizer = jnp.maximum(jnp.abs(C.sum(-1, keepdims=True)), jnp.exp(-max_log_D))
            Cn = C / (normalizer + EPS)
            h = jnp.einsum('bhst,bhtd->bhsd', Cn, vh)
            mu = h.mean(-1, keepdims=True)
            var = ((h - mu) ** 2).mean(-1, keepdims=True)
            hn = (h - mu) * jax.lax.rsqrt(var + EPS)
            hn = hn * ln_scale.reshape(1, nh, 1, dh)
            return hn.transpose(0, 2, 1, 3).reshape(b, s, e)
        key = jax.random.key(seed)
        ks = jax.random.split(key, 6)
        q = jax.random.normal(ks[0], (B, S, E), dtype=jnp.float32)
        k = jax.random.normal(ks[1], (B, S, E), dtype=jnp.float32)
        v = jax.random.normal(ks[2], (B, S, E), dtype=jnp.float32)
        Wi = jax.random.normal(ks[3], (3 * E, NH), dtype=jnp.float32) * 0.02
        bi = jax.random.normal(ks[4], (NH,), dtype=jnp.float32) * 0.1
        Wf = jax.random.normal(ks[5], (3 * E, NH), dtype=jnp.float32) * 0.02
        bf = jnp.linspace(3.0, 6.0, NH, dtype=jnp.float32)
        ln_scale = jnp.ones((E,), dtype=jnp.float32)
        return {'q': q, 'k': k, 'v': v, 'Wi': Wi, 'bi': bi, 'Wf': Wf, 'bf': bf, 'ln_scale': ln_scale}
    _L0_xattn_all = _L0_xattn_setup()
    _L0_xattn_in = {k: v for k, v in _L0_xattn_all.items() if k in ('Wi', 'bi', 'Wf', 'bf', 'ln_scale')}
    del _L0_xattn_all

    def _L0_ffn_setup():
        import jax, jax.numpy as jnp
        import numpy as np
        TOP_K = 4
        key = jax.random.key(seed)
        ks = jax.random.split(key, 8)
        B, S, H = (1, 128, 256)
        E, I = (60, 176)
        I_SH = 704
        s = 0.02
        return {'hidden_states': jax.random.normal(ks[0], (B, S, H), jnp.float32), 'gate_w': jax.random.normal(ks[1], (E, H), jnp.float32) * s, 'shared_gate_w': jax.random.normal(ks[2], (1, H), jnp.float32) * s, 'w13': jax.random.normal(ks[3], (E, 2 * I, H), jnp.float32) * s, 'w2': jax.random.normal(ks[4], (E, H, I), jnp.float32) * s, 'se_gate_up_w': jax.random.normal(ks[5], (2 * I_SH, H), jnp.float32) * s, 'se_down_w': jax.random.normal(ks[6], (H, I_SH), jnp.float32) * s}
    _L0_ffn_all = _L0_ffn_setup()
    _L0_ffn_in = {k: v for k, v in _L0_ffn_all.items() if k in ('gate_w', 'shared_gate_w', 'w13', 'w2', 'se_gate_up_w', 'se_down_w')}
    del _L0_ffn_all
    return {'x': x, 'ctx_2048': ctx_2048, 'g_xattn': g_xattn, 'g_ffn': g_ffn, 'L0_xattn_Wi': _L0_xattn_in['Wi'], 'L0_xattn_bi': _L0_xattn_in['bi'], 'L0_xattn_Wf': _L0_xattn_in['Wf'], 'L0_xattn_bf': _L0_xattn_in['bf'], 'L0_xattn_ln_scale': _L0_xattn_in['ln_scale'], 'L0_ffn_gate_w': _L0_ffn_in['gate_w'], 'L0_ffn_shared_gate_w': _L0_ffn_in['shared_gate_w'], 'L0_ffn_w13': _L0_ffn_in['w13'], 'L0_ffn_w2': _L0_ffn_in['w2'], 'L0_ffn_se_gate_up_w': _L0_ffn_in['se_gate_up_w'], 'L0_ffn_se_down_w': _L0_ffn_in['se_down_w']}

def reference(x, ctx_2048, g_xattn, g_ffn, L0_xattn_Wi, L0_xattn_bi, L0_xattn_Wf, L0_xattn_bf, L0_xattn_ln_scale, L0_ffn_gate_w, L0_ffn_shared_gate_w, L0_ffn_w13, L0_ffn_w2, L0_ffn_se_gate_up_w, L0_ffn_se_down_w):
    import jax
    import jax.numpy as jnp

    def _L0_xattn_ref(q, k, v, Wi, bi, Wf, bf, ln_scale):
        import jax, jax.numpy as jnp
        import numpy as np
        B, S, E, NH = (2, 128, 256, 16)
        DH = E // NH
        EPS = 1e-06

        def _mlstm_forward(q, k, v, Wi, bi, Wf, bf, ln_scale):
            b, s, e = q.shape
            nh = Wi.shape[1]
            dh = e // nh
            x = jnp.concatenate([q, k, v], axis=-1)
            ig = (x @ Wi + bi).transpose(0, 2, 1)[..., None]
            fg = (x @ Wf + bf).transpose(0, 2, 1)[..., None]
            split = lambda t: t.reshape(b, s, nh, dh).transpose(0, 2, 1, 3)
            qh, kh, vh = (split(q), split(k), split(v))
            log_f = jax.nn.log_sigmoid(fg)
            log_f_cum = jnp.concatenate([jnp.zeros((b, nh, 1, 1), q.dtype), jnp.cumsum(log_f, axis=2)], axis=2)
            fg_mat = log_f_cum - jnp.transpose(log_f_cum, (0, 1, 3, 2))
            ltr = jnp.tril(jnp.ones((s, s), dtype=bool))
            log_fg = jnp.where(ltr, fg_mat[:, :, 1:, 1:], -jnp.inf)
            log_D = log_fg + jnp.transpose(ig, (0, 1, 3, 2))
            max_log_D = jnp.max(log_D, axis=-1, keepdims=True)
            D = jnp.exp(log_D - max_log_D)
            qk = jnp.einsum('bhsd,bhtd->bhst', qh, kh) / jnp.sqrt(jnp.asarray(dh, q.dtype))
            C = qk * D
            normalizer = jnp.maximum(jnp.abs(C.sum(-1, keepdims=True)), jnp.exp(-max_log_D))
            Cn = C / (normalizer + EPS)
            h = jnp.einsum('bhst,bhtd->bhsd', Cn, vh)
            mu = h.mean(-1, keepdims=True)
            var = ((h - mu) ** 2).mean(-1, keepdims=True)
            hn = (h - mu) * jax.lax.rsqrt(var + EPS)
            hn = hn * ln_scale.reshape(1, nh, 1, dh)
            return hn.transpose(0, 2, 1, 3).reshape(b, s, e)
        return _mlstm_forward(q, k, v, Wi, bi, Wf, bf, ln_scale)

    def _L0_ffn_ref(hidden_states, gate_w, shared_gate_w, w13, w2, se_gate_up_w, se_down_w):
        import jax, jax.numpy as jnp
        import numpy as np
        TOP_K = 4
        orig_shape = hidden_states.shape
        E, H = gate_w.shape
        I = w2.shape[2]
        x = hidden_states.reshape(-1, H)
        M = x.shape[0]
        gu = x @ se_gate_up_w.T
        I_sh = se_down_w.shape[1]
        shared = jax.nn.silu(gu[:, :I_sh]) * gu[:, I_sh:] @ se_down_w.T
        shared = shared * jax.nn.sigmoid(x @ shared_gate_w.T)
        logits = x @ gate_w.T
        probs = jax.nn.softmax(logits.astype(jnp.float32), axis=-1)
        weights, sel = jax.lax.top_k(probs, TOP_K)
        cw = jnp.zeros((M, E), jnp.float32).at[jnp.arange(M)[:, None], sel].add(weights)

        def step(acc, ews):
            w13_e, w2_e, cw_e = ews
            gu_e = x @ w13_e.T
            h = jax.nn.silu(gu_e[:, :I]) * gu_e[:, I:]
            return (acc + cw_e[:, None] * (h @ w2_e.T), None)
        sparse, _ = jax.lax.scan(step, jnp.zeros((M, H), jnp.float32), (w13, w2, cw.T))
        return (shared + sparse).reshape(orig_shape)
    x = x + jnp.tanh(g_xattn[0]) * _L0_xattn_ref(_layernorm(x, axis=-1), ctx_2048, ctx_2048, L0_xattn_Wi, L0_xattn_bi, L0_xattn_Wf, L0_xattn_bf, L0_xattn_ln_scale)
    x = x + jnp.tanh(g_ffn[0]) * _L0_ffn_ref(_layernorm(x, axis=-1), L0_ffn_gate_w, L0_ffn_shared_gate_w, L0_ffn_w13, L0_ffn_w2, L0_ffn_se_gate_up_w, L0_ffn_se_down_w)
    return x

_drawn_inputs = setup_inputs


def setup_inputs(seed=0):
    import zlib

    import numpy as np

    out = dict(_drawn_inputs(seed))
    spreads = {'L0_xattn_ln_scale': (1.0, 0.2)}
    factors = {'L0_xattn_bi': 64.0,
     'L0_xattn_Wf': 4.55,
     'L0_ffn_gate_w': 8.0,
     'L0_ffn_shared_gate_w': 8.0,
     'L0_ffn_w13': 8.0,
     'L0_ffn_w2': 8.0,
     'L0_ffn_se_gate_up_w': 6.647,
     'L0_ffn_se_down_w': 6.644}
    for name, (base, spread) in spreads.items():
        noise = np.random.default_rng([zlib.crc32(name.encode()), seed]).standard_normal(out[name].shape)
        drawn = base * np.exp(spread * noise) if base else spread * noise
        out[name] = jnp.asarray(drawn.astype(out[name].dtype))
    for name, factor in factors.items():
        out[name] = (out[name] * factor).astype(out[name].dtype)
    return out
```

```python
import concourse.bass as bass
from concourse import mybir
from contextlib import ExitStack


def flamingo_layer(nc, x, ctx, w_i, b_i, w_f, b_f, ln_scale, g_x, g_f,
                   router_w, w13, w2, se_w13, se_w2, consts, out):
    fp32, bf16, i32, u32 = mybir.dt.float32, mybir.dt.bfloat16, mybir.dt.int32, mybir.dt.uint32
    ALU, ACT, AX = mybir.AluOpType, mybir.ActivationFunctionType, mybir.AxisListType
    P = 128
    N, E = x.shape
    S = 64
    T = N // P
    NH = w_i.shape[1]
    DH = E // NH
    KC = E // P
    TG = P // NH
    G = T // TG
    NG = 2 * NH
    VW = DH + 1
    PAD = S // 2
    DEPTH = 2
    NEG = -3.0e38
    NR = router_w.shape[1]
    NE = NR - 1
    K4 = 4
    I2 = w13.shape[1] // KC
    I = I2 // 2
    IH = I // 2
    SUB = se_w13.shape[0] // P
    WB = 4
    NB = (N * K4 - NE) // P + NE
    NB += -NB % WB

    def done(t):
        return t + 1 + DEPTH

    def freed(t):
        return t + 1

    g_dram = nc.dram_tensor("g_dram", (2 * T, NH * S), fp32).ap()
    xT_dram = nc.dram_tensor("xT_dram", (T * P, E), fp32).ap()
    slot_x = nc.dram_tensor("slot_x", (NB * P, E), fp32).ap()
    slot_y = nc.dram_tensor("slot_y", (NB * P, E), fp32).ap()

    with ExitStack() as stack:
        def sb(name, shape, dt=fp32):
            return stack.enter_context(nc.sbuf_tensor(name, shape, dt))

        def sem(name):
            return stack.enter_context(nc.semaphore(name))

        bank = stack.enter_context(nc.psum_tensor("bank", [P, 8, 512], fp32))

        cst = sb("cst", [P, consts.shape[1]])
        at = 0
        ident, at = cst[:, at:at + P], at + P
        tri_seq, at = cst[:, at:at + P], at + P
        tri_all, at = cst[:, at:at + P], at + P
        HC = P // DH
        head_mask, at = cst[:, at:at + HC], at + HC
        neg_mask, at = cst[:, at:at + S], at + S

        iota_e, at = cst[:, at:at + NE], at + NE
        iota_p, at = cst[:, at:at + 1], at + 1
        fills, at = cst[:, at:at + T], at + T

        wi_sb = sb("wi_sb", [P, 3 * KC, NG])
        wctx = sb("wctx", [P, KC, NG])
        bias_bc = sb("bias_bc", [P, NG])
        lnsc = sb("lnsc", [P, E])
        gx = sb("gx", [P, 1])
        x_all = sb("x_all", [P, T * E])
        ctx_all = sb("ctx_all", [P, T * E])
        stats = sb("stats", [P, T, 6])
        mv = sb("mv", [P, T * 2])
        rstd = sb("rstd", [P, T])
        gates = sb("gates", [P, T * NG])
        s_all = sb("s_all", [P, T * NH * S])
        qn = [sb(f"qn{p}", [P, E]) for p in range(2)]
        ct = [sb(f"ct{p}", [P, E]) for p in range(2)]
        qkT = [sb(f"qkT{p}", [P, 2 * KC, P]) for p in range(2)]
        qbd = [sb(f"qbd{p}", [P, KC, HC, P]) for p in range(2)]
        lf = sb("lf", [P, T * NH])
        fcum = sb("fcum", [P, T * NH])
        a_all = sb("a_all", [P, T * NH])
        m_all = sb("m_all", [P, T * NH])
        scan = [sb(f"scan{p}", [P, 2 * G, PAD + S]) for p in range(2)]
        gcum = sb("gcum", [P, 2 * G, S])
        gb = [sb(f"gb{p}", [P, NH * S]) for p in range(2)]
        dd = [sb(f"dd{p}", [P, NH * S]) for p in range(2)]
        vt = [sb(f"vt{p}", [P, NH, VW]) for p in range(2)]
        h_all = sb("h_all", [P, T * NH * VW])
        CT = 4
        hh = sb("hh", [P, CT * NH * DH])
        hq = sb("hq", [P, CT * NH * DH])
        hs = sb("hs", [P, 2, CT * NH])

        ZW = NB * E // 31
        zeros = sb("zeros", [P, ZW])
        ones_b = sb("ones_b", [P, P], bf16)
        tri_b = sb("tri_b", [P, P], bf16)
        rw = sb("rw", [P, KC, NR])
        gf = sb("gf", [P, 1])
        used = {}

        def within(big, n, rows=P):
            lo = used.get(big.name, 0)
            used[big.name] = lo + n
            assert lo + n <= big.shape[1]
            return big[0:rows, lo:lo + n]

        def old(n):
            return within(s_all, n)
        xn_all = old(T * E)
        lg_all = old(T * NR)
        prob = old(T * NE)
        pos = old(T * NE)
        tcum = [old(8 * NE + T * NE) for _ in range(2)]
        oh = [within(b, T * NE // 2).bitcast(bf16) for b in (gb[1], gb[1], dd[0], dd[0])]
        top = sb("top", [P, T, 8])
        topi = sb("topi", [P, T, 8], u32)
        topf = sb("topf", [P, T, K4])
        wk = sb("wk", [P, T * K4])
        zsum = sb("zsum", [P, T])
        sgate = sb("sgate", [P, T])
        cnt = sb("cnt", [P, NE])
        cmp = within(gb[0], NE * T).rearrange("p (n t) -> p n t", t=T)
        nblk = sb("nblk", [P, NE])
        EP = 32
        ecum = [sb(f"ecum{p}", [P, EP + NE]) for p in range(2)]
        slotf = sb("slotf", [P, T, K4])
        slotu = sb("slotu", [P, T * K4], u32)
        eob = sb("eob", [P, 1])
        eob_row = sb("eob_row", [1, P], i32)
        se13 = sb("se13", [P, SUB, KC * I2])
        se2 = sb("se2", [IH, SUB, 2 * E])
        wa = [within(ctx_all, KC * I2) for _ in range(WB)]
        wb = [within(h_all, 2 * E, IH) for _ in range(WB)]
        xg = [within(h_all, E) for _ in range(WB)]
        xT = [within(hq, E).rearrange("p (c s) -> p c s", s=P) for _ in range(2)]
        sg = [within(dd[1], I) for _ in range(2)]
        hb = [within(dd[1], I) for _ in range(2)]
        hT = [within(hh, 2 * P, IH).rearrange("p (c s) -> p c s", s=P) for _ in range(2)]
        yb = [within(h_all, E) for _ in range(WB)]

        s_x, s_w, s_c = sem("s_x"), sem("s_w"), sem("s_c")
        pool_step, dve_step, act_step, pe_step = sem("pool_step"), sem("dve_step"), sem("act_step"), sem("pe_step")
        zeros_ready, cleared, s_se = sem("zeros_ready"), sem("cleared"), sem("s_se")
        ctx_in = [sem(f"ctx_in{p}") for p in range(2)]
        rstd_in, rstd_sq = sem("rstd_in"), sem("rstd_sq")
        wctx_ready = sem("wctx_ready")
        qn_ready, tr_done, qkT_ready, qbd_ready = sem("qn_ready"), sem("tr_done"), sem("qkT_ready"), sem("qbd_ready")
        gates_done, scores_done = sem("gates_done"), sem("scores_done")
        gates_out, scores_out = sem("gates_out"), sem("scores_out")

        steps = {}

        def after(eng, step_sem, ins):
            steps[step_sem.name] = steps.get(step_sem.name, 0) + 1
            ins.then_inc(step_sem, 1)
            eng.wait_ge(step_sem, steps[step_sem.name])

        def paired(eng, step, first=0, last=T):
            with eng.Fori(first // 2, last // 2) as it:
                for p in range(2):
                    step(it * 2 + p, p)

        with nc.Block() as block:
            @block.sync
            def _(sp):
                sp.dma_start(cst[:, :], consts).then_inc(s_c, 16)
                xr = x.rearrange("(t p) e -> p t e", p=P)
                cr = ctx.rearrange("(t p) e -> p t e", p=P)
                for h in range(4):
                    r = slice(h * T // 4, (h + 1) * T // 4)
                    c = slice(h * T * E // 4, (h + 1) * T * E // 4)
                    sp.dma_start(x_all[:, c].rearrange("p (t e) -> p t e", e=E), xr[:, r, :]).then_inc(s_x, 16)
                for h in range(4):
                    r = slice(h * T // 4, (h + 1) * T // 4)
                    c = slice(h * T * E // 4, (h + 1) * T * E // 4)
                    sp.dma_start(ctx_all[:, c].rearrange("p (t e) -> p t e", e=E), cr[:, r, :]).then_inc(s_w, 16)

                def load_ctx(t, p):
                    sp.wait_ge(tr_done, freed(t))
                    sp.dma_start(ct[p][:, :], ctx[bass.ds(t * P, P), :]).then_inc(ctx_in[p], 16)
                paired(sp, load_ctx)

            @block.gpsimd
            def _(pool):
                pool.memset(zeros[:, :], 0.0).then_inc(zeros_ready, 1)
                pool.memset(ones_b[:, :], 1.0)
                pool.memset(vt[0][:, :, DH:VW], 1.0)
                pool.memset(vt[1][:, :, DH:VW], 1.0)
                pool.memset(scan[0][:, :, 0:PAD], NEG)
                pool.memset(scan[1][:, :, 0:PAD], NEG)

            @block.vector
            def _(dve):
                dve.sem_inc(qn_ready, DEPTH)
                dve.sem_inc(qbd_ready, DEPTH)
                dve.wait_ge(s_w, 16 * 10)
                nc.vector.tensor_tensor(wctx[:, :, :], wi_sb[:, KC:2 * KC, :], wi_sb[:, 2 * KC:3 * KC, :], ALU.add).then_inc(wctx_ready, 1)
                dve.wait_ge(s_x, 64)
                for t in range(T):
                    ins = nc.vector.bn_stats(out=stats[:, t, :], in_=x_all[:, t * E:(t + 1) * E])
                after(dve, dve_step, ins)
                for t in range(T):
                    ins = nc.vector.bn_aggr(out=mv[:, 2 * t:2 * t + 2], in_=stats[:, t, :])
                after(dve, dve_step, ins)
                var = mv[:, :].rearrange("p (t c) -> p t c", c=2)[:, :, 1]
                nc.vector.tensor_scalar(rstd[:, :], var, 1.0e-5, None, ALU.add).then_inc(rstd_in, 1)
                dve.wait_ge(rstd_sq, 1)
                after(dve, dve_step, nc.vector.reciprocal(rstd[:, :], rstd[:, :]))

                def norm(t, p):
                    dve.wait_ge(tr_done, freed(t))
                    nc.vector.tensor_scalar(qn[p][:, :], x_all[:, bass.ds(t * E, E)], mv[:, bass.ds(t * 2, 1)],
                                            rstd[:, bass.ds(t, 1)], ALU.subtract, ALU.mult).then_inc(qn_ready, 1)

                def spread(t, p):
                    dve.wait_ge(qkT_ready, done(t))
                    dve.wait_ge(scores_done, freed(t))
                    nc.vector.tensor_tensor(qbd[p][:, :, :, :],
                                            qkT[p][:, 0:KC, :].unsqueeze(2).to_broadcast([P, KC, HC, P]),
                                            head_mask.unsqueeze(1).unsqueeze(3).to_broadcast([P, KC, HC, P]),
                                            ALU.mult).then_inc(qbd_ready, 1)

                def step(t, p):
                    norm(t + 1, 1 - p)
                    spread(t, p)
                dve.wait_ge(s_c, 16)
                norm(0, 0)
                paired(dve, step, 0, T - 2)
                step(T - 2, 0)
                spread(T - 1, 1)

            @block.scalar
            def _(act):
                act.sem_inc(qkT_ready, DEPTH)
                act.sem_inc(gates_out, DEPTH)
                act.sem_inc(scores_out, DEPTH)
                act.dma_start(wi_sb[:, :, 0:NH], w_i.rearrange("(c p) h -> p c h", p=P)).then_inc(s_w, 16)
                act.dma_start(wi_sb[:, :, NH:NG], w_f.rearrange("(c p) h -> p c h", p=P)).then_inc(s_w, 16)
                act.dma_start(bias_bc[:, 0:NH], b_i.partition_broadcast(P)).then_inc(s_w, 16)
                act.dma_start(bias_bc[:, NH:NG], b_f.partition_broadcast(P)).then_inc(s_w, 16)
                act.dma_start(lnsc[:, :], ln_scale.partition_broadcast(P)).then_inc(s_w, 16)
                act.dma_start(gx[:, :], g_x.partition_broadcast(P)).then_inc(s_w, 16)
                act.dma_start(gf[:, :], g_f.partition_broadcast(P)).then_inc(s_se, 16)
                act.dma_start(rw[:, :, :], router_w.rearrange("(c p) n -> p c n", p=P)).then_inc(s_se, 16)
                act.dma_start(se13[:, :, :], se_w13.rearrange("(j p) n -> p j n", p=P)).then_inc(s_se, 16)
                act.dma_start(se2[:, :, :], se_w2.rearrange("(j p) n -> p j n", p=IH)).then_inc(s_se, 16)
                act.wait_ge(zeros_ready, 1)
                clear = slot_x.rearrange("(p n) e -> p (n e)", p=P)
                for z in range(31):
                    act.dma_start(clear[:, z * ZW:(z + 1) * ZW], zeros[:, :]).then_inc(cleared, 16)
                act.wait_ge(rstd_in, 1)
                nc.scalar.activation(rstd[:, :], rstd[:, :], ACT.Sqrt).then_inc(rstd_sq, 1)

                def copy_qkT(t, p):
                    act.wait_ge(tr_done, done(t))
                    act.wait_ge(scores_done, freed(t))
                    nc.scalar.activation(qkT[p][:, :, :], bank[:, 4 + p, :].rearrange("p (c s) -> p c s", s=P),
                                         ACT.Copy).then_inc(qkT_ready, 1)

                def copy_out(t, p):
                    act.wait_ge(gates_done, done(t))
                    nc.scalar.activation(gates[:, bass.ds(t * NG, NG)], bank[:, 6 + p, 0:NG], ACT.Copy).then_inc(gates_out, 1)
                    act.wait_ge(scores_done, done(t))
                    dst = s_all[:, bass.ds(t * NH * S, NH * S)].rearrange("p (c m) -> p c m", c=KC)
                    nc.scalar.activation(dst, bank[:, 2 * p:2 * p + 2, :], ACT.Copy).then_inc(scores_out, 1)

                def step(t, p):
                    copy_qkT(t + 1, 1 - p)
                    copy_out(t, p)
                copy_qkT(0, 0)
                paired(act, step, 0, T - 2)
                step(T - 2, 0)
                copy_out(T - 1, 1)

            @block.tensor
            def _(pe):
                pe.sem_inc(tr_done, DEPTH)
                pe.sem_inc(gates_done, DEPTH)
                pe.sem_inc(scores_done, DEPTH)
                pe.wait_ge(s_c, 16)
                pe.wait_ge(wctx_ready, 1)

                def transposes(t, p, rounds):
                    pe.wait_ge(qn_ready, done(t))
                    pe.wait_ge(ctx_in[p], rounds * 16)
                    pe.wait_ge(qkT_ready, freed(t))
                    for k, src in enumerate((qn[p], ct[p])):
                        for c in range(KC):
                            ins = nc.tensor.transpose(bank[:, 4 + p, (2 * k + c) * P:(2 * k + c + 1) * P],
                                                      src[:, c * P:(c + 1) * P], ident)
                    ins.then_inc(tr_done, 1)

                def products(t, p):
                    pe.wait_ge(qkT_ready, done(t))
                    pe.wait_ge(gates_out, freed(t))
                    for k in range(2 * KC):
                        w = wi_sb[:, k, :] if k < KC else wctx[:, k - KC, :]
                        ins = nc.tensor.matmul(bank[:, 6 + p, 0:NG], qkT[p][:, k, :], w, start=(k == 0), stop=(k == 2 * KC - 1))
                    ins.then_inc(gates_done, 1)
                    pe.wait_ge(qbd_ready, done(t))
                    pe.wait_ge(scores_out, freed(t))
                    for c in range(KC):
                        for b in range(2):
                            r = slice(b * S, (b + 1) * S)
                            ins = nc.tensor.matmul(bank[r, 2 * p + c, :], qkT[p][:, KC + c, r], qbd[p][:, c, :, r],
                                                   start=True, stop=True)
                    ins.then_inc(scores_done, 1)

                transposes(0, 0, 1)
                with pe.Fori(0, T // 2 - 1) as it:
                    transposes(it * 2 + 1, 1, it + 1)
                    products(it * 2, 0)
                    transposes(it * 2 + 2, 0, it + 2)
                    products(it * 2 + 1, 1)
                transposes(T - 1, 1, T // 2)
                products(T - 2, 0)
                products(T - 1, 1)

        gates3 = gates[:, :].rearrange("p (t g) -> p t g", g=NG)

        def th(v):
            return v.rearrange("p (t h) -> p t h", h=NH)

        z_ready, l_ready, lf_ready, f_done, a_ready, aT_done, g_ready, gT_done, g_out, m_ready, em_ready = (
            sem(n) for n in ("z_ready", "l_ready", "lf_ready", "f_done", "a_ready", "aT_done", "g_ready", "gT_done",
                             "g_out", "m_ready", "em_ready"))
        sc = hq[:, 0:T * NH]
        with nc.Block() as block:
            @block.vector
            def _(dve):
                dve.wait_ge(s_w, 16 * 10)
                after(dve, dve_step, nc.vector.tensor_tensor(gates3, gates3, bias_bc[:, :].unsqueeze(1).to_broadcast([P, T, NG]), ALU.add))
                f = gates3[:, :, NH:NG]
                nc.vector.scalar_tensor_tensor(th(sc), f, -1.0, f, ALU.mult, ALU.min).then_inc(z_ready, 1)
                dve.wait_ge(l_ready, 1)
                nc.vector.scalar_tensor_tensor(th(lf[:, :]), f, 0.0, th(sc), ALU.min, ALU.subtract).then_inc(lf_ready, 1)
                dve.wait_ge(f_done, 1)
                nc.vector.tensor_tensor(th(a_all[:, :]), gates3[:, :, 0:NH], th(bank[:, 0, 0:T * NH]), ALU.subtract).then_inc(a_ready, 1)
                nc.vector.tensor_copy(fcum[:, :], bank[:, 0, 0:T * NH])
                dve.wait_ge(aT_done, 1)
                after(dve, dve_step, nc.vector.tensor_copy(scan[0][:, :, PAD:PAD + S], bank[:, 1, 0:2 * G * S].rearrange("p (g s) -> p g s", s=S)))
                k, sh = 0, 1
                while sh < S:
                    to = scan[1 - k][:, :, PAD:PAD + S] if 2 * sh < S else gcum[:, :, :]
                    ins = nc.vector.tensor_tensor(to, scan[k][:, :, PAD:PAD + S],
                                                  scan[k][:, :, PAD - sh:PAD + S - sh], ALU.max)
                    k, sh = 1 - k, 2 * sh
                    if sh < S:
                        after(dve, dve_step, ins)
                ins.then_inc(g_ready, 1)
                dve.wait_ge(gT_done, 1)
                nc.vector.tensor_tensor(m_all[:, :], fcum[:, :], bank[:, 2, 0:T * NH], ALU.add).then_inc(m_ready, 1)

            @block.scalar
            def _(act):
                act.wait_ge(z_ready, 1)
                after(act, act_step, nc.scalar.activation(sc, sc, ACT.Exp))
                nc.scalar.activation(sc, sc, ACT.Ln, bias=1.0).then_inc(l_ready, 1)
                act.wait_ge(m_ready, 1)
                nc.scalar.activation(m_all[:, :], m_all[:, :], ACT.Exp, scale=-1.0).then_inc(em_ready, 1)
                nc.scalar.activation(gx[:, :], gx[:, :], ACT.Tanh)

            @block.tensor
            def _(pe):
                pe.wait_ge(lf_ready, 1)
                nc.tensor.matmul(bank[:, 0, 0:T * NH], tri_seq, lf[:, :], start=True, stop=True).then_inc(f_done, 1)
                pe.wait_ge(a_ready, 1)
                for g in range(G):
                    ins = nc.tensor.transpose(bank[:, 1, g * P:(g + 1) * P], a_all[:, g * P:(g + 1) * P], ident)
                ins.then_inc(aT_done, 1)
                pe.wait_ge(g_ready, 1)
                for g in range(G):
                    ins = nc.tensor.transpose(bank[:, 2, g * P:(g + 1) * P], gcum[:, 2 * g:2 * g + 2, :].rearrange("p b s -> p (b s)"), ident)
                ins.then_inc(gT_done, 1)

            @block.sync
            def _(sp):
                sp.wait_ge(g_ready, 1)
                gd = g_dram.rearrange("(g t b) (h s) -> g b t h s", g=G, b=2, s=S)
                for g in range(G):
                    for b in range(2):
                        for t in range(TG):
                            sp.dma_start(gd[g, b, t, :, :], gcum[t * NH:(t + 1) * NH, 2 * g + b, :]).then_inc(g_out, 16)
                sp.wait_ge(g_out, 16 * 2 * T)

        gb_in = [sem(f"gb_in{p}") for p in range(2)]
        d_ready, dm_ready, e_ready, c_ready, vt_ready, h_done, h_out = (
            sem(n) for n in ("d_ready", "dm_ready", "e_ready", "c_ready", "vt_ready", "h_done", "h_out"))
        hd = [dd[0], dd[1]]

        def hs3(v):
            return v.rearrange("p (h s) -> p h s", s=S)

        with nc.Block() as block:
            @block.sync
            def _(sp):
                def load_g(t, p):
                    sp.wait_ge(d_ready, freed(t))
                    for b in range(2):
                        sp.dma_start(gb[p][b * S:(b + 1) * S, :], g_dram[bass.ds(t * 2 + b, 1), :].to_broadcast([S, NH * S])).then_inc(gb_in[p], 16)
                paired(sp, load_g)

            @block.gpsimd
            def _(pool):
                pool.sem_inc(d_ready, DEPTH)
                pool.sem_inc(vt_ready, DEPTH)
                with pool.Fori(0, T // 2) as it:
                    for p in range(2):
                        t = it * 2 + p
                        pool.wait_ge(gb_in[p], it * 32 + 32)
                        pool.wait_ge(h_done, freed(t))
                        pool.tensor_tensor(hs3(hd[p][:, :]), a_all[:, bass.ds(t * NH, NH)].unsqueeze(2).to_broadcast([P, NH, S]),
                                           hs3(gb[p][:, :]), ALU.subtract).then_inc(d_ready, 1)
                        pool.tensor_copy(vt[p][:, :, 0:DH], ctx_all[:, bass.ds(t * E, E)].rearrange("p (h d) -> p h d", d=DH)).then_inc(vt_ready, 1)

            @block.vector
            def _(dve):
                dve.sem_inc(dm_ready, DEPTH)
                dve.sem_inc(c_ready, DEPTH)

                def clip(t, p):
                    dve.wait_ge(d_ready, done(t))
                    nc.vector.scalar_tensor_tensor(hs3(hd[p][:, :]), hs3(hd[p][:, :]), 0.0,
                                                   neg_mask.unsqueeze(1).to_broadcast([P, NH, S]), ALU.min, ALU.add).then_inc(dm_ready, 1)

                def weigh(t, p):
                    dve.wait_ge(e_ready, done(t))
                    nc.vector.tensor_tensor(hd[p][:, :], hd[p][:, :], s_all[:, bass.ds(t * NH * S, NH * S)], ALU.mult).then_inc(c_ready, 1)

                def step(t, p):
                    clip(t + 1, 1 - p)
                    weigh(t, p)
                clip(0, 0)
                paired(dve, step, 0, T - 2)
                step(T - 2, 0)
                weigh(T - 1, 1)

            @block.scalar
            def _(act):
                act.sem_inc(e_ready, DEPTH)
                act.sem_inc(h_out, DEPTH)

                def expo(t, p):
                    act.wait_ge(dm_ready, done(t))
                    nc.scalar.activation(hd[p][:, :], hd[p][:, :], ACT.Exp).then_inc(e_ready, 1)

                def copy_h(t, p):
                    act.wait_ge(h_done, done(t))
                    for b in range(2):
                        ins = nc.scalar.activation(h_all[b * S:(b + 1) * S, bass.ds(t * NH * VW, NH * VW)],
                                                   bank[b * S:(b + 1) * S, 2 * p + b, 0:NH * VW], ACT.Copy)
                    ins.then_inc(h_out, 1)

                def step(t, p):
                    expo(t + 1, 1 - p)
                    copy_h(t, p)
                expo(0, 0)
                paired(act, step, 0, T - 2)
                step(T - 2, 0)
                copy_h(T - 1, 1)

            @block.tensor
            def _(pe):
                pe.sem_inc(h_done, DEPTH)

                def product(t, p):
                    pe.wait_ge(c_ready, done(t))
                    pe.wait_ge(vt_ready, done(t))
                    pe.wait_ge(h_out, freed(t))
                    pe.sem_inc(pe_step, 1)
                    for h in range(NH):
                        for b in range(2):
                            r = slice(b * S, (b + 1) * S)
                            ins = nc.tensor.matmul(bank[r, 2 * p + b, h * VW:(h + 1) * VW], hd[p][r, h * S:(h + 1) * S],
                                                   vt[p][r, h, :], start=True, stop=True)
                    ins.then_inc(h_done, 1)
                paired(pe, product)

        var_ready, var_sq = sem("var_ready"), sem("var_sq")
        with nc.Block() as block:
            @block.vector
            def _(dve):
                after(dve, dve_step, nc.vector.tensor_scalar(lnsc[:, :], lnsc[:, :], gx[:, 0:1], None, ALU.mult))
                base = steps[dve_step.name]
                NCH = CT * NH
                PER = 13
                with dve.Fori(0, T // CT) as q:
                    n = [0]

                    def link(ins):
                        n[0] += 1
                        ins.then_inc(dve_step, 1)
                        dve.wait_ge(dve_step, q * PER + base + n[0])

                    h4 = h_all[:, bass.ds(q * (NCH * VW), NCH * VW)].rearrange("p (h d) -> p h d", d=VW)
                    r0, r1 = hs[:, 0, :], hs[:, 1, :]
                    hh3 = hh[:, :].rearrange("p (h d) -> p h d", d=DH)
                    hq3 = hq[:, :].rearrange("p (h d) -> p h d", d=DH)
                    link(nc.vector.scalar_tensor_tensor(r0, h4[:, :, DH], -1.0, h4[:, :, DH], ALU.mult, ALU.max))
                    link(nc.vector.tensor_tensor(r0, r0, m_all[:, bass.ds(q * NCH, NCH)], ALU.max))
                    link(nc.vector.tensor_scalar(r0, r0, 1.0e-6, None, ALU.add))
                    link(nc.vector.reciprocal(r0, r0))
                    link(nc.vector.tensor_tensor(hh3, h4[:, :, 0:DH], r0.unsqueeze(2).to_broadcast([P, NCH, DH]), ALU.mult))
                    link(nc.vector.tensor_reduce(r1, hh3, AX.X, ALU.add))
                    link(nc.vector.scalar_tensor_tensor(hh3, r1.unsqueeze(2).to_broadcast([P, NCH, DH]), -1.0 / DH, hh3, ALU.mult, ALU.add))
                    link(nc.vector.tensor_tensor(hq[:, :], hh[:, :], hh[:, :], ALU.mult))
                    link(nc.vector.tensor_reduce(r1, hq3, AX.X, ALU.add))
                    nc.vector.tensor_scalar(r1, r1, 1.0 / DH, 1.0e-6, ALU.mult, ALU.add).then_inc(var_ready, 1)
                    dve.wait_ge(var_sq, q + 1)
                    link(nc.vector.reciprocal(r1, r1))
                    link(nc.vector.tensor_tensor(hh3, hh3, r1.unsqueeze(2).to_broadcast([P, NCH, DH]), ALU.mult))
                    xs = x_all[:, bass.ds(q * (CT * E), CT * E)]
                    link(nc.vector.tensor_tensor(hh[:, :].rearrange("p (t e) -> p t e", e=E), hh[:, :].rearrange("p (t e) -> p t e", e=E),
                                                 lnsc[:, :].unsqueeze(1).to_broadcast([P, CT, E]), ALU.mult))
                    link(nc.vector.tensor_tensor(xs, xs, hh[:, :], ALU.add))
                    assert n[0] == PER
                steps[dve_step.name] += PER * (T // CT)

            @block.scalar
            def _(act):
                with act.Fori(0, T // CT) as q:
                    act.wait_ge(var_ready, q + 1)
                    nc.scalar.activation(hs[:, 1, :], hs[:, 1, :], ACT.Sqrt).then_inc(var_sq, 1)

        xn_ready, xT_done, xT_copied, lg_done, lg_out, xn_kept, r5_in, r5_sq = (
            sem(n) for n in ("xn_ready", "xT_done", "xT_copied", "lg_done", "lg_out", "xn_kept", "r5_in", "r5_sq"))
        xT_st = [sem(f"xT_st{p}") for p in range(2)]
        with nc.Block() as block:
            @block.vector
            def _(dve):
                dve.sem_inc(xn_ready, DEPTH)
                for t in range(T):
                    ins = nc.vector.bn_stats(out=stats[:, t, :], in_=x_all[:, t * E:(t + 1) * E])
                after(dve, dve_step, ins)
                for t in range(T):
                    ins = nc.vector.bn_aggr(out=mv[:, 2 * t:2 * t + 2], in_=stats[:, t, :])
                after(dve, dve_step, ins)
                var = mv[:, :].rearrange("p (t c) -> p t c", c=2)[:, :, 1]
                nc.vector.tensor_scalar(rstd[:, :], var, 1.0e-5, None, ALU.add).then_inc(r5_in, 1)
                nc.vector.tensor_copy(tri_b[:, :], tri_all)
                dve.wait_ge(r5_sq, 1)
                after(dve, dve_step, nc.vector.reciprocal(rstd[:, :], rstd[:, :]))

                def norm(t, p):
                    dve.wait_ge(xT_done, freed(t))
                    dve.wait_ge(xn_kept, freed(t))
                    nc.vector.tensor_scalar(qn[p][:, :], x_all[:, bass.ds(t * E, E)], mv[:, bass.ds(t * 2, 1)],
                                            rstd[:, bass.ds(t, 1)], ALU.subtract, ALU.mult).then_inc(xn_ready, 1)
                paired(dve, norm)

            @block.gpsimd
            def _(pool):
                pool.sem_inc(xn_kept, DEPTH)

                def keep(t, p):
                    pool.wait_ge(xn_ready, done(t))
                    pool.tensor_copy(xn_all[:, bass.ds(t * E, E)], qn[p][:, :]).then_inc(xn_kept, 1)
                paired(pool, keep)

            @block.scalar
            def _(act):
                act.sem_inc(xT_copied, DEPTH)
                act.sem_inc(lg_out, DEPTH)
                act.wait_ge(r5_in, 1)
                nc.scalar.activation(rstd[:, :], rstd[:, :], ACT.Sqrt).then_inc(r5_sq, 1)
                with act.Fori(0, T // 2) as it:
                    for p in range(2):
                        t = it * 2 + p
                        act.wait_ge(xT_done, done(t))
                        act.wait_ge(lg_done, freed(t))
                        act.wait_ge(xT_st[p], it * 16)
                        nc.scalar.activation(qkT[p][:, 0:KC, :], bank[:, 4 + p, 0:E].rearrange("p (c s) -> p c s", s=P),
                                             ACT.Copy).then_inc(xT_copied, 1)
                        act.wait_ge(lg_done, done(t))
                        nc.scalar.activation(lg_all[:, bass.ds(t * NR, NR)], bank[:, 6 + p, 0:NR], ACT.Copy).then_inc(lg_out, 1)

            @block.sync
            def _(sp):
                with sp.Fori(0, T // 2) as it:
                    for p in range(2):
                        t = it * 2 + p
                        sp.wait_ge(xT_copied, done(t))
                        sp.dma_start(xT_dram[bass.ds(t * P, P), :], qkT[p][:, 0:KC, :].rearrange("p c s -> p (c s)")).then_inc(xT_st[p], 16)

            @block.tensor
            def _(pe):
                pe.sem_inc(xT_done, DEPTH)
                pe.sem_inc(lg_done, DEPTH)
                pe.wait_ge(s_se, 64)

                def transposes(t, p):
                    pe.wait_ge(xn_ready, done(t))
                    pe.wait_ge(xT_copied, freed(t))
                    for c in range(KC):
                        ins = nc.tensor.transpose(bank[:, 4 + p, c * P:(c + 1) * P], qn[p][:, c * P:(c + 1) * P], ident)
                    ins.then_inc(xT_done, 1)

                def logits(t, p):
                    pe.wait_ge(xT_copied, done(t))
                    pe.wait_ge(lg_out, freed(t))
                    for c in range(KC):
                        ins = nc.tensor.matmul(bank[:, 6 + p, 0:NR], qkT[p][:, c, :], rw[:, c, :], start=(c == 0), stop=(c == KC - 1))
                    ins.then_inc(lg_done, 1)

                def step(t, p):
                    transposes(t + 1, 1 - p)
                    logits(t, p)
                transposes(0, 0)
                paired(pe, step, 0, T - 2)
                step(T - 2, 0)
                logits(T - 1, 1)

        def tn(v, n=NE):
            return v.rearrange("p (t n) -> p t n", n=n)

        e_in, e_out, oh_ready, rank_done, eob_ready, eobT_done, slots_ready = (
            sem(n) for n in ("e_in", "e_out", "oh_ready", "rank_done", "eob_ready", "eobT_done", "slots_ready"))
        HB = T // 2
        with nc.Block() as block:
            @block.vector
            def _(dve):
                step = lambda ins: after(dve, dve_step, ins)
                lg = tn(lg_all, NR)
                for t in range(T):
                    ins = nc.vector.max(top[:, t, :], lg_all[:, t * NR:t * NR + NE])
                step(ins)
                for t in range(T):
                    ins = nc.vector.max_index(topi[:, t, :], top[:, t, :], lg_all[:, t * NR:t * NR + NE])
                step(ins)
                nc.vector.tensor_tensor(tn(prob), lg[:, :, 0:NE], top[:, :, 0].unsqueeze(2).to_broadcast([P, T, NE]), ALU.subtract)
                step(nc.vector.tensor_copy(topf[:, :, :], topi[:, :, 0:K4]))
                nc.vector.tensor_copy(sgate[:, :], lg[:, :, NE])
                nc.vector.tensor_tensor(tn(wk[:, :], K4), top[:, :, 0:K4], top[:, :, 0].unsqueeze(2).to_broadcast([P, T, K4]), ALU.subtract).then_inc(e_in, 1)
                for k in range(K4):
                    ins = nc.vector.tensor_tensor(tn(oh[k]), iota_e.unsqueeze(1).to_broadcast([P, T, NE]),
                                                  topf[:, :, k].unsqueeze(2).to_broadcast([P, T, NE]), ALU.is_equal)
                ins.then_inc(oh_ready, 1)
                dve.wait_ge(e_out, 1)
                step(nc.vector.tensor_reduce(zsum[:, :], tn(prob), AX.X, ALU.add))
                nc.vector.tensor_scalar(sgate[:, :], sgate[:, :], 1.0, None, ALU.add)
                step(nc.vector.reciprocal(zsum[:, :], zsum[:, :]))
                nc.vector.tensor_scalar(zsum[:, :], zsum[:, :], gf[:, 0:1], None, ALU.mult)
                step(nc.vector.reciprocal(sgate[:, :], sgate[:, :]))
                nc.vector.tensor_scalar(sgate[:, :], sgate[:, :], gf[:, 0:1], None, ALU.mult)
                step(nc.vector.tensor_tensor(tn(wk[:, :], K4), tn(wk[:, :], K4), zsum[:, :].unsqueeze(2).to_broadcast([P, T, K4]), ALU.mult))
                dve.wait_ge(rank_done, 1)
                pad = 8 * NE
                for b in range(2):
                    nc.vector.tensor_copy(tcum[0][:, pad + (1 + b * HB) * NE:pad + min((1 + (b + 1) * HB), T) * NE] if b == 0 else
                                          tcum[0][:, pad + (1 + HB) * NE:pad + T * NE],
                                          bank[:, 2 + b, 0:HB * NE] if b == 0 else bank[:, 2 + b, 0:(HB - 1) * NE])
                nc.vector.tensor_copy(cnt[:, :], bank[:, 3, (HB - 1) * NE:HB * NE])
                nc.vector.memset(ecum[0][:, 0:EP], 0.0)
                nc.vector.memset(ecum[1][:, 0:EP], 0.0)
                nc.vector.memset(tcum[1][:, 0:pad], 0.0)
                step(nc.vector.memset(tcum[0][:, 0:pad + NE], 0.0))
                k, sh = 0, 1
                while sh < T:
                    step(nc.vector.tensor_tensor(tcum[1 - k][:, pad:], tcum[k][:, pad:], tcum[k][:, pad - sh * NE:pad + (T - sh) * NE], ALU.add))
                    k, sh = 1 - k, 2 * sh
                tex = tcum[k][:, pad:]
                step(nc.vector.tensor_tensor(cnt[:, :], cnt[:, :], tex[:, (T - 1) * NE:T * NE], ALU.add))
                step(nc.vector.tensor_tensor(cmp[:, :, :], cnt[:, :].unsqueeze(2).to_broadcast([P, NE, T]),
                                             fills.unsqueeze(1).to_broadcast([P, NE, T]), ALU.is_gt))
                step(nc.vector.tensor_reduce(nblk[:, :], cmp[:, :, :], AX.X, ALU.add))
                step(nc.vector.tensor_copy(ecum[0][:, EP:], nblk[:, :]))
                k, sh = 0, 1
                while sh < NE:
                    step(nc.vector.tensor_tensor(ecum[1 - k][:, EP:], ecum[k][:, EP:], ecum[k][:, EP - sh:EP + NE - sh], ALU.add))
                    k, sh = 1 - k, 2 * sh
                ends = ecum[k][:, EP:]
                nc.vector.tensor_tensor(nblk[:, :], ends, nblk[:, :], ALU.subtract)
                step(nc.vector.tensor_scalar(cmp[:, :, 0], ends, iota_p, None, ALU.is_le))
                step(nc.vector.tensor_reduce(eob[:, :], cmp[:, :, 0], AX.X, ALU.add))
                nc.vector.tensor_scalar(eob[:, :], eob[:, :], float(NE - 1), None, ALU.min).then_inc(eob_ready, 1)
                step(nc.vector.tensor_scalar(nblk[:, :], nblk[:, :], float(P), None, ALU.mult))
                step(nc.vector.tensor_tensor(tn(pos), tn(tex), nblk[:, :].unsqueeze(1).to_broadcast([P, T, NE]), ALU.add))
                for b in range(2):
                    r = slice(b * HB * NE, (b + 1) * HB * NE)
                    ins = nc.vector.tensor_tensor(pos[:, r], pos[:, r], bank[:, b, 0:HB * NE], ALU.add)
                step(ins)
                for kk in range(K4):
                    step(nc.vector.tensor_tensor(prob, pos, oh[kk], ALU.mult))
                    step(nc.vector.tensor_reduce(slotf[:, :, kk], tn(prob), AX.X, ALU.add))
                nc.vector.tensor_copy(tn(slotu[:, :], K4), slotf[:, :, :]).then_inc(slots_ready, 1)
                dve.wait_ge(eobT_done, 1)
                nc.vector.tensor_copy(eob_row[0:1, :], bank[0:1, 4, 0:P])

            @block.scalar
            def _(act):
                act.wait_ge(e_in, 1)
                nc.scalar.activation(prob, prob, ACT.Exp)
                nc.scalar.activation(wk[:, :], wk[:, :], ACT.Exp)
                nc.scalar.activation(sgate[:, :], sgate[:, :], ACT.Exp, scale=-1.0)
                nc.scalar.activation(gf[:, :], gf[:, :], ACT.Tanh).then_inc(e_out, 1)

            @block.tensor
            def _(pe):
                pe.wait_ge(oh_ready, 1)
                for b in range(2):
                    for k, lhs in enumerate((tri_b, ones_b)):
                        for q in range(K4):
                            ins = nc.tensor.matmul(bank[:, 2 * k + b, 0:HB * NE], lhs[:, :], oh[q][:, b * HB * NE:(b + 1) * HB * NE],
                                                   start=(q == 0), stop=(q == K4 - 1))
                ins.then_inc(rank_done, 1)
                pe.wait_ge(eob_ready, 1)
                nc.tensor.matmul(bank[0:1, 4, 0:P], eob[:, 0:1], ident, start=True, stop=True).then_inc(eobT_done, 1)

        scattered = sem("scattered")
        xs_in = [sem(f"xs_in{p}") for p in range(2)]
        sgu_done, ssg_ready, sh_ready, shT_done, shT_ready, sy_done, sy_out = (
            sem(n) for n in ("sgu_done", "ssg_ready", "sh_ready", "shT_done", "shT_ready", "sy_done", "sy_out"))

        def up(s, p, xt_buf, w, at_w):
            for c in range(KC):
                ins = nc.tensor.matmul(bank[:, p, 0:I2], xt_buf[:, c, :], w[:, at_w + c * I2:at_w + (c + 1) * I2],
                                       start=(c == 0), stop=(c == KC - 1))
            return ins

        def turn(p):
            for c in range(2):
                ins = nc.tensor.transpose(bank[0:IH, 4 + p, c * P:(c + 1) * P], hb[p][:, c * IH:(c + 1) * IH], ident)
            return ins

        def down(p, ybank, w, at_w, first, last):
            for c in range(2):
                ins = nc.tensor.matmul(bank[:, ybank, 0:E], hT[p][:, c, :], w[:, at_w + c * E:at_w + (c + 1) * E],
                                       start=(first and c == 0), stop=(last and c == 1))
            return ins

        NS = SUB * T
        with nc.Block() as block:
            @block.gpsimd
            def _(pool):
                pool.wait_ge(cleared, 16 * 31)
                pool.wait_ge(slots_ready, 1)
                for t in range(T):
                    for k in range(K4):
                        c = t * K4 + k
                        pool.indirect_dma_start(slot_x[:, :], bass.IndirectOffsetOnAxis(slotu[:, c:c + 1], 0),
                                                xn_all[:, t * E:(t + 1) * E], None).then_inc(scattered, 16)
                pool.wait_ge(scattered, 16 * T * K4)

            @block.sync
            def _(sp):
                def load(t, p):
                    sp.dma_start(xT[p][:, :, :].rearrange("p c s -> p (c s)"), xT_dram[bass.ds(t * P, P), :]).then_inc(xs_in[p], 16)
                load(0, 0)
                load(1, 1)
                with sp.Fori(1, T // 2) as it:
                    for p in range(2):
                        sp.wait_ge(sgu_done, (it - 1) * (2 * SUB) + p * SUB + SUB + DEPTH)
                        load(it * 2 + p, p)

            @block.tensor
            def _(pe):
                pe.sem_inc(sgu_done, DEPTH)
                pe.sem_inc(shT_done, DEPTH)
                pe.sem_inc(sy_done, DEPTH)

                def pe_up(s, j, rounds):
                    if j % SUB == 0:
                        pe.wait_ge(xs_in[j // SUB], rounds * 16)
                    pe.wait_ge(sh_ready, freed(s))
                    up(s, j % 2, xT[j // SUB], se13[:, j % SUB, :], 0).then_inc(sgu_done, 1)

                def pe_turn(s, j):
                    pe.wait_ge(sh_ready, done(s))
                    pe.wait_ge(shT_ready, freed(s))
                    turn(j % 2).then_inc(shT_done, 1)

                def pe_down(s, t, j):
                    if j % SUB == 0:
                        pe.wait_ge(sy_out, freed(t))
                    pe.wait_ge(shT_ready, done(s))
                    ins = down(j % 2, 6 + j // SUB, se2[:, j % SUB, :], 0, j % SUB == 0, j % SUB == SUB - 1)
                    ins.then_inc(sy_done, 1)

                R = 2 * SUB

                def body(it, lag):
                    for j in range(R):
                        s = it * R + j
                        pe_up(s, j, it + 1)
                        if lag or j >= 1:
                            pe_turn(s - 1, (j - 1) % R)
                        if lag or j >= 2:
                            t2 = it * 2 + (j - 2) // SUB if j >= 2 else it * 2 - 1
                            pe_down(s - 2, t2, (j - 2) % R)
                body(0, False)
                with pe.Fori(1, NS // R) as it:
                    body(it, True)
                pe_turn(NS - 1, R - 1)
                pe_down(NS - 2, T - 1, R - 2)
                pe_down(NS - 1, T - 1, R - 1)

            @block.scalar
            def _(act):
                act.sem_inc(ssg_ready, DEPTH)
                act.sem_inc(shT_ready, DEPTH)

                def silu(s, p):
                    act.wait_ge(sgu_done, done(s))
                    act.wait_ge(sh_ready, freed(s))
                    nc.scalar.activation(sg[p][:, :], bank[:, p, 0:I], ACT.Silu).then_inc(ssg_ready, 1)

                def copy_hT(s, p):
                    act.wait_ge(shT_done, done(s))
                    act.wait_ge(sy_done, freed(s))
                    nc.scalar.activation(hT[p][:, :, :], bank[0:IH, 4 + p, 0:2 * P].rearrange("p (c s) -> p c s", s=P),
                                         ACT.Copy).then_inc(shT_ready, 1)

                def step(s, p):
                    silu(s + 1, 1 - p)
                    copy_hT(s, p)
                silu(0, 0)
                paired(act, step, 0, NS - 2)
                step(NS - 2, 0)
                copy_hT(NS - 1, 1)

            @block.vector
            def _(dve):
                dve.sem_inc(sh_ready, DEPTH)
                dve.sem_inc(sy_out, DEPTH)

                def mul(s, p):
                    dve.wait_ge(ssg_ready, done(s))
                    dve.wait_ge(shT_done, freed(s))
                    nc.vector.tensor_tensor(hb[p][:, :], sg[p][:, :], bank[:, p, I:I2], ALU.mult).then_inc(sh_ready, 1)

                def keep(t, p):
                    dve.wait_ge(sy_done, done(t * SUB + SUB - 1))
                    xs = x_all[:, bass.ds(t * E, E)]
                    nc.vector.scalar_tensor_tensor(xs, bank[:, 6 + p, 0:E], sgate[:, bass.ds(t, 1)], xs, ALU.mult, ALU.add).then_inc(sy_out, 1)

                def tile(t, p, lag):
                    for j in range(SUB):
                        mul(t * SUB + j, j % 2)
                        if j == 2 and lag:
                            keep(t - 1, 1 - p)
                tile(0, 0, False)
                tile(1, 1, True)
                with dve.Fori(1, T // 2) as it:
                    for p in range(2):
                        tile(it * 2 + p, p, True)
                keep(T - 1, 1)

        w_in = [sem(f"w_in{b}") for b in range(WB)]
        v_in = [sem(f"v_in{b}") for b in range(WB)]
        r_in = [sem(f"r_in{b}") for b in range(WB)]
        y_st = [sem(f"y_st{b}") for b in range(WB)]
        bx_done, bx_ready, bgu_done, bsg_ready, bh_ready, bhT_done, bhT_ready, by_done, by_ready = (
            sem(n) for n in ("bx_done", "bx_ready", "bgu_done", "bsg_ready", "bh_ready", "bhT_done", "bhT_ready", "by_done", "by_ready"))
        with nc.Block() as block:
            @block.sync
            def _(sp):
                def load(i, b, again):
                    e = sp.value_load(eob_row[0:1, bass.ds(i, 1)], min_val=0, max_val=NE - 1)
                    if again:
                        sp.wait_ge(bx_done, i - WB + 1 + DEPTH)
                    sp.dma_start(xg[b][:, :], slot_x[bass.ds(i * P, P), :]).then_inc(r_in[b], 16)
                    if again:
                        sp.wait_ge(bgu_done, i - WB + 1 + DEPTH)
                    sp.dma_start(wa[b][:, :], w13[bass.ds(e * P, P), :]).then_inc(w_in[b], 16)
                for b in range(WB):
                    load(b, b, False)
                with sp.Fori(1, NB // WB) as it:
                    for b in range(WB):
                        load(it * WB + b, b, True)

            @block.gpsimd
            def _(pool):
                def load(i, b):
                    e = pool.value_load(eob_row[0:1, bass.ds(i, 1)], min_val=0, max_val=NE - 1)
                    pool.dma_start(wb[b][:, :], w2[bass.ds(e * IH, IH), :]).then_inc(v_in[b], 16)

                def store(i, b):
                    pool.wait_ge(by_ready, done(i))
                    pool.dma_start(slot_y[bass.ds(i * P, P), :], yb[b][:, :]).then_inc(y_st[b], 16)
                for b in range(WB):
                    load(b, b)
                with pool.Fori(1, NB // WB) as it:
                    for b in range(WB):
                        pool.wait_ge(by_done, (it - 1) * WB + b + 1 + DEPTH)
                        load(it * WB + b, b)
                        store((it - 1) * WB + b, b)
                for b in range(WB):
                    store(NB - WB + b, b)
                for b in range(WB):
                    pool.wait_ge(y_st[b], 16 * (NB // WB))

            @block.tensor
            def _(pe):
                pe.sem_inc(bx_done, DEPTH)
                pe.sem_inc(bgu_done, DEPTH)
                pe.sem_inc(bhT_done, DEPTH)
                pe.sem_inc(by_done, DEPTH)

                def rows(i, b, rounds):
                    pe.wait_ge(r_in[b], rounds * 16)
                    pe.wait_ge(bx_ready, freed(i))
                    for c in range(KC):
                        ins = nc.tensor.transpose(bank[:, 2 + b % 2, c * P:(c + 1) * P], xg[b][:, c * P:(c + 1) * P], ident)
                    ins.then_inc(bx_done, 1)

                def pe_up(i, b, rounds):
                    pe.wait_ge(w_in[b], rounds * 16)
                    pe.wait_ge(bx_ready, done(i))
                    pe.wait_ge(bh_ready, freed(i))
                    up(i, b % 2, xT[b % 2], wa[b], 0).then_inc(bgu_done, 1)

                def pe_turn(i, b):
                    pe.wait_ge(bh_ready, done(i))
                    pe.wait_ge(bhT_ready, freed(i))
                    turn(b % 2).then_inc(bhT_done, 1)

                def pe_down(i, b, rounds):
                    pe.wait_ge(v_in[b], rounds * 16)
                    pe.wait_ge(bhT_ready, done(i))
                    pe.wait_ge(by_ready, freed(i))
                    down(b % 2, 6 + b % 2, wb[b], 0, True, True).then_inc(by_done, 1)

                def body(it, lag, lead=True):
                    for b in range(WB):
                        i = it * WB + b
                        if lead or b < WB - 1:
                            rows(i + 1, (b + 1) % WB, it + 1 if b < WB - 1 else it + 2)
                        pe_up(i, b, it + 1)
                        if lag or b >= 1:
                            pe_turn(i - 1, (b - 1) % WB)
                        if lag or b >= 2:
                            pe_down(i - 2, (b - 2) % WB, it + 1 if b >= 2 else it)
                rows(0, 0, 1)
                body(0, False)
                with pe.Fori(1, NB // WB - 1) as it:
                    body(it, True)
                body(NB // WB - 1, True, False)
                pe_turn(NB - 1, WB - 1)
                pe_down(NB - 2, WB - 2, NB // WB)
                pe_down(NB - 1, WB - 1, NB // WB)

            @block.scalar
            def _(act):
                act.sem_inc(bsg_ready, DEPTH)
                act.sem_inc(bhT_ready, DEPTH)
                act.sem_inc(by_ready, DEPTH)

                def silu(i, b):
                    act.wait_ge(bgu_done, done(i))
                    act.wait_ge(bh_ready, freed(i))
                    nc.scalar.activation(sg[b % 2][:, :], bank[:, b % 2, 0:I], ACT.Silu).then_inc(bsg_ready, 1)

                def copy_hT(i, b):
                    act.wait_ge(bhT_done, done(i))
                    act.wait_ge(by_done, freed(i))
                    nc.scalar.activation(hT[b % 2][:, :, :], bank[0:IH, 4 + b % 2, 0:2 * P].rearrange("p (c s) -> p c s", s=P),
                                         ACT.Copy).then_inc(bhT_ready, 1)

                def copy_y(i, b, rounds):
                    act.wait_ge(by_done, done(i))
                    if rounds is not None:
                        act.wait_ge(y_st[b], rounds * 16)
                    nc.scalar.activation(yb[b][:, :], bank[:, 6 + b % 2, 0:E], ACT.Copy).then_inc(by_ready, 1)

                def body(it, lag, again):
                    for b in range(WB):
                        i = it * WB + b
                        silu(i, b)
                        if lag or b >= 1:
                            copy_hT(i - 1, (b - 1) % WB)
                        if lag or b >= 2:
                            rounds = (it if b >= 2 else it - 1) if again or b >= 2 and lag else None
                            copy_y(i - 2, (b - 2) % WB, rounds)
                body(0, False, False)
                body(1, True, False)
                with act.Fori(2, NB // WB) as it:
                    body(it, True, True)
                copy_hT(NB - 1, WB - 1)
                copy_y(NB - 2, WB - 2, NB // WB - 1)
                copy_y(NB - 1, WB - 1, NB // WB - 1)

            @block.vector
            def _(dve):
                dve.sem_inc(bx_ready, DEPTH)
                dve.sem_inc(bh_ready, DEPTH)

                def copy_x(i, b):
                    dve.wait_ge(bx_done, done(i))
                    dve.wait_ge(bgu_done, freed(i))
                    nc.vector.tensor_copy(xT[b % 2][:, :, :], bank[:, 2 + b % 2, 0:E].rearrange("p (c s) -> p c s", s=P)).then_inc(bx_ready, 1)

                def mul(i, b):
                    dve.wait_ge(bsg_ready, done(i))
                    dve.wait_ge(bhT_done, freed(i))
                    nc.vector.tensor_tensor(hb[b % 2][:, :], sg[b % 2][:, :], bank[:, b % 2, I:I2], ALU.mult).then_inc(bh_ready, 1)

                def step(i, p):
                    copy_x(i + 1, 1 - p)
                    mul(i, p)
                copy_x(0, 0)
                paired(dve, step, 0, NB - 2)
                step(NB - 2, 0)
                mul(NB - 1, 1)

        YB = 8
        yg = [old(E) for _ in range(YB)]
        yg_in = [sem(f"yg_in{b}") for b in range(YB)]
        added, s_out = sem("added"), sem("s_out")
        with nc.Block() as block:
            @block.gpsimd
            def _(pool):
                for c in range(T * K4):
                    if c >= YB:
                        pool.wait_ge(added, c - YB + 1)
                    pool.indirect_dma_start(yg[c % YB], None, slot_y[:, :],
                                            bass.IndirectOffsetOnAxis(slotu[:, c:c + 1], 0)).then_inc(yg_in[c % YB], 16)

            @block.vector
            def _(dve):
                for c in range(T * K4):
                    t = c // K4
                    dve.wait_ge(yg_in[c % YB], 16 * (c // YB + 1))
                    if c:
                        dve.wait_ge(added, c)
                    xs = x_all[:, t * E:(t + 1) * E]
                    nc.vector.scalar_tensor_tensor(xs, yg[c % YB], wk[:, c:c + 1], xs, ALU.mult, ALU.add).then_inc(added, 1)

            @block.sync
            def _(sp):
                for t in range(T):
                    sp.wait_ge(added, K4 * (t + 1))
                    sp.dma_start(out[t * P:(t + 1) * P, :], x_all[:, t * E:(t + 1) * E]).then_inc(s_out, 16)
                sp.wait_ge(s_out, 16 * T)


def kernel(x, ctx_2048, g_xattn, g_ffn, L0_xattn_Wi, L0_xattn_bi, L0_xattn_Wf, L0_xattn_bf, L0_xattn_ln_scale,
           L0_ffn_gate_w, L0_ffn_shared_gate_w, L0_ffn_w13, L0_ffn_w2, L0_ffn_se_gate_up_w, L0_ffn_se_down_w):
    import numpy as np
    import concourse.bacc as bacc
    from concourse.bass_utils import run_bass_kernel_spmd

    P, S, DH = 128, 64, 16
    row, col = np.arange(P)[:, None], np.arange(P)[None, :]
    same = row // S == col // S
    consts = np.concatenate([
        row == col,
        (row <= col) & same,
        row < col,
        (row // DH == np.arange(P // DH)[None, :]) * DH ** -0.5,
        np.where(row % S > np.arange(S)[None, :], -1.0e30, 0.0),
        np.arange(L0_ffn_w2.shape[0])[None, :] + 0 * row,
        row,
        P * np.arange(x.size // x.shape[-1] // P)[None, :] + 0 * row,
    ], axis=1).astype(np.float32)

    def swapped(a):
        return np.ascontiguousarray(np.swapaxes(a, -1, -2))

    def width_first(w):
        e, n, k = w.shape
        return swapped(w).reshape(e, k // P, P, n).transpose(0, 2, 1, 3).reshape(e * P, -1)

    def inner_first(w):
        e, k, n = w.shape
        return swapped(w).reshape(e, 2, n // 2, k).transpose(0, 2, 1, 3).reshape(e * n // 2, -1)

    I = L0_ffn_w2.shape[2]
    se_gu = L0_ffn_se_gate_up_w.reshape(2, -1, I, L0_ffn_se_gate_up_w.shape[1])
    se_d = L0_ffn_se_down_w

    arrays = {
        "x": np.ascontiguousarray(x).reshape(-1, x.shape[-1]),
        "ctx": np.ascontiguousarray(ctx_2048).reshape(-1, x.shape[-1]),
        "w_i": L0_xattn_Wi, "b_i": L0_xattn_bi, "w_f": L0_xattn_Wf, "b_f": L0_xattn_bf,
        "ln_scale": L0_xattn_ln_scale, "g_x": g_xattn, "g_f": g_ffn,
        "router_w": np.concatenate([swapped(L0_ffn_gate_w), swapped(L0_ffn_shared_gate_w)], axis=1),
        "w13": width_first(L0_ffn_w13), "w2": inner_first(L0_ffn_w2),
        "se_w13": width_first(np.concatenate([se_gu[0], se_gu[1]], axis=1)),
        "se_w2": inner_first(np.swapaxes(se_d.reshape(se_d.shape[0], -1, I), 0, 1)),
        "consts": consts,
    }
    nc = bacc.Bacc("TRN2", target_bir_lowering=False, num_devices=1)
    arrays = {k: np.ascontiguousarray(v) for k, v in arrays.items()}
    aps = {k: nc.dram_tensor(f"in_{k}", v.shape, mybir.dt.from_np(v.dtype), kind="ExternalInput").ap() for k, v in arrays.items()}
    out = nc.dram_tensor("out_0", arrays["x"].shape, mybir.dt.float32, kind="ExternalOutput").ap()
    flamingo_layer(nc, out=out, **aps)
    r = run_bass_kernel_spmd(nc, [{f"in_{k}": v for k, v in arrays.items()}], core_ids=[0])
    return r.results[0]["out_0"].reshape(x.shape)
```

```python
import concourse.bass as bass
from concourse import mybir
from contextlib import ExitStack


def flamingo_layer(nc, x, ctx, w_i, b_i, w_f, b_f, ln_scale, g_x, g_f,
                   router_w, w13, w2, se_w13, se_w2, consts, out):
    fp32, bf16, i32, u32 = mybir.dt.float32, mybir.dt.bfloat16, mybir.dt.int32, mybir.dt.uint32
    ALU, ACT, AX = mybir.AluOpType, mybir.ActivationFunctionType, mybir.AxisListType
    P = 128
    N, E = x.shape
    S = 64
    T = N // P
    NH = w_i.shape[1]
    DH = E // NH
    KC = E // P
    TG = P // NH
    G = T // TG
    NG = 2 * NH
    VW = DH + 1
    PAD = S // 2
    CT = 4
    DEPTH = 2
    NEG = -3.0e38
    NR = router_w.shape[1]
    NE = NR - 1
    K4 = 4
    I2 = w13.shape[1] // KC
    I = I2 // 2
    IH = I // 2
    SUB = se_w13.shape[0] // P
    WB = 4
    NB = (N * K4 - NE) // P + NE
    NB += -NB % WB

    def done(t):
        return t + 1 + DEPTH

    def freed(t):
        return t + 1

    g_dram = nc.dram_tensor("g_dram", (2 * T, NH * S), fp32).ap()
    xT_dram = nc.dram_tensor("xT_dram", (T * P, E), fp32).ap()
    slot_x = nc.dram_tensor("slot_x", (NB * P, E), fp32).ap()
    slot_y = nc.dram_tensor("slot_y", (NB * P, E), fp32).ap()

    with ExitStack() as stack:
        def sb(name, shape, dt=fp32):
            return stack.enter_context(nc.sbuf_tensor(name, shape, dt))

        def sem(name):
            return stack.enter_context(nc.semaphore(name))

        bank = stack.enter_context(nc.psum_tensor("bank", [P, 8, 512], fp32))

        cst = sb("cst", [P, consts.shape[1]])
        at = 0
        ident, at = cst[:, at:at + P], at + P
        tri_seq, at = cst[:, at:at + P], at + P
        tri_all, at = cst[:, at:at + P], at + P
        HC = P // DH
        head_mask, at = cst[:, at:at + HC], at + HC
        neg_mask, at = cst[:, at:at + S], at + S

        iota_e, at = cst[:, at:at + NE], at + NE
        iota_p, at = cst[:, at:at + 1], at + 1
        fills, at = cst[:, at:at + T], at + T
        seq_mask, at = cst[:, at:at + 2], at + 2

        wi_sb = sb("wi_sb", [P, 3 * KC, NG])
        wctx = sb("wctx", [P, KC, NG])
        bias_bc = sb("bias_bc", [P, NG])
        lnsc = sb("lnsc", [P, E])
        gx = sb("gx", [P, 1])
        x_all = sb("x_all", [P, T * E])
        ctx_all = sb("ctx_all", [P, T * E])
        stats = sb("stats", [P, T, 6])
        mv = sb("mv", [P, T * 2])
        rstd = sb("rstd", [P, T])
        gates = sb("gates", [P, T * NG])
        s_all = sb("s_all", [P, T * NH * S])
        qn = [sb(f"qn{p}", [P, E]) for p in range(2)]
        ct = [sb(f"ct{p}", [P, E]) for p in range(2)]
        qkT = [sb(f"qkT{p}", [P, 2 * KC, P]) for p in range(2)]
        qbd = [sb(f"qbd{p}", [P, KC, HC, P]) for p in range(2)]
        lf = sb("lf", [P, T * NH])
        fcum = sb("fcum", [P, T * NH])
        a_all = sb("a_all", [P, T * NH])
        m_all = sb("m_all", [P, T * NH])
        scan = [sb(f"scan{p}", [P, 2 * G, PAD + S]) for p in range(2)]
        gcum = sb("gcum", [P, 2 * G, S])
        gb = [sb(f"gb{p}", [P, NH * S]) for p in range(2)]
        dd = [sb(f"dd{b}", [P, NH * S]) for b in range(4)]
        vbd = [sb(f"vbd{p}", [P, NH // 2, 2, 2, VW]) for p in range(2)]
        half = sb("half", [P, CT * NH])
        h_all = sb("h_all", [P, T * NH * VW])
        hh = sb("hh", [P, CT * NH * DH])
        hq = sb("hq", [P, CT * NH * DH])
        hs = sb("hs", [P, 2, CT * NH])

        NZ = 31
        ZW = NB * E // NZ
        zeros = sb("zeros", [P, ZW])
        ones_b = sb("ones_b", [P, P], bf16)
        tri_b = sb("tri_b", [P, P], bf16)
        rw = sb("rw", [P, KC, NR])
        gf = sb("gf", [P, 1])
        used = {}

        def within(big, n, rows=P):
            lo = used.get(big.name, 0)
            used[big.name] = lo + n
            assert lo + n <= big.shape[1]
            return big[0:rows, lo:lo + n]

        def old(n):
            return within(s_all, n)
        xn_all = old(T * E)
        lg_all = old(T * NR)
        prob = old(T * NE)
        pos = old(T * NE)
        tcum = [old(8 * NE + T * NE) for _ in range(2)]
        oh = [within(b, T * NE // 2).bitcast(bf16) for b in (gb[1], gb[1], dd[0], dd[0])]
        top = sb("top", [P, T, 8])
        topi = sb("topi", [P, T, 8], u32)
        topf = sb("topf", [P, T, K4])
        wk = sb("wk", [P, T * K4])
        zsum = sb("zsum", [P, T])
        sgate = sb("sgate", [P, T])
        cnt = sb("cnt", [P, NE])
        cmp = within(gb[0], NE * T).rearrange("p (n t) -> p n t", t=T)
        nblk = sb("nblk", [P, NE])
        EP = 32
        ecum = [sb(f"ecum{p}", [P, EP + NE]) for p in range(2)]
        slotf = sb("slotf", [P, T, K4])
        slotu = sb("slotu", [P, T * K4], u32)
        eob = sb("eob", [P, 1])
        last_f = sb("last_f", [P, 1])
        eob_row = sb("eob_row", [1, P + 1], i32)
        se13 = old(SUB * KC * I2).rearrange("p (j n) -> p j n", j=SUB)
        se2 = within(s_all, SUB * 2 * E, IH).rearrange("p (j n) -> p j n", j=SUB)
        wa = [within(ctx_all, KC * I2) for _ in range(WB)]
        wb = [within(h_all, 2 * E, IH) for _ in range(WB)]
        xg = [within(h_all, E) for _ in range(WB)]
        xT = [within(hq, E).rearrange("p (c s) -> p c s", s=P) for _ in range(2)]
        sg = [within(dd[1], I) for _ in range(2)]
        hb = [within(dd[1], I) for _ in range(2)]
        hT = [within(hh, 2 * P, IH).rearrange("p (c s) -> p c s", s=P) for _ in range(2)]
        yb = [within(h_all, E) for _ in range(WB)]

        s_x, s_w, s_c = sem("s_x"), sem("s_w"), sem("s_c")
        pool_norm, dve_norm, dve_sum = sem("pool_norm"), sem("dve_norm"), sem("dve_sum")
        pool_step, dve_step, act_step, pe_step = sem("pool_step"), sem("dve_step"), sem("act_step"), sem("pe_step")
        zeros_ready, cleared, s_se, s_r = sem("zeros_ready"), sem("cleared"), sem("s_se"), sem("s_r")
        ctx_in = [sem(f"ctx_in{p}") for p in range(2)]
        rstd_in, rstd_sq = sem("rstd_in"), sem("rstd_sq")
        wctx_ready = sem("wctx_ready")
        qn_ready, tr_done, qkT_ready, qbd_ready = sem("qn_ready"), sem("tr_done"), sem("qkT_ready"), sem("qbd_ready")
        gates_done, scores_done = sem("gates_done"), sem("scores_done")
        gates_out, scores_out = sem("gates_out"), sem("scores_out")

        steps = {}

        def after(eng, step_sem, ins):
            steps[step_sem.name] = steps.get(step_sem.name, 0) + 1
            ins.then_inc(step_sem, 1)
            eng.wait_ge(step_sem, steps[step_sem.name])

        def paired(eng, step, first=0, last=T):
            with eng.Fori(first // 2, last // 2) as it:
                for p in range(2):
                    step(it * 2 + p, p)

        with nc.Block() as block:
            @block.sync
            def _(sp):
                sp.dma_start(cst[:, :], consts).then_inc(s_c, 16)
                xr = x.rearrange("(t p) e -> p t e", p=P)
                cr = ctx.rearrange("(t p) e -> p t e", p=P)
                for h in range(4):
                    r = slice(h * T // 4, (h + 1) * T // 4)
                    c = slice(h * T * E // 4, (h + 1) * T * E // 4)
                    sp.dma_start(x_all[:, c].rearrange("p (t e) -> p t e", e=E), xr[:, r, :]).then_inc(s_x, 16)
                for h in range(4):
                    r = slice(h * T // 4, (h + 1) * T // 4)
                    c = slice(h * T * E // 4, (h + 1) * T * E // 4)
                    sp.dma_start(ctx_all[:, c].rearrange("p (t e) -> p t e", e=E), cr[:, r, :]).then_inc(s_w, 16)

                def load_ctx(t, p):
                    sp.wait_ge(tr_done, freed(t))
                    sp.dma_start(ct[p][:, :], ctx[bass.ds(t * P, P), :]).then_inc(ctx_in[p], 16)
                paired(sp, load_ctx)

            @block.gpsimd
            def _(pool):
                pool.memset(zeros[:, :], 0.0).then_inc(zeros_ready, 1)
                pool.memset(ones_b[:, :], 1.0)
                pool.memset(half[:, :], -0.5)
                pool.wait_ge(s_c, 16)
                for p in range(2):
                    for b in range(2):
                        pool.tensor_copy(vbd[p][:, :, b, :, DH], seq_mask[:, b:b + 1].unsqueeze(2).to_broadcast([P, NH // 2, 2]))
                pool.memset(scan[0][:, :, 0:PAD], NEG)
                pool.memset(scan[1][:, :, 0:PAD], NEG)

            @block.vector
            def _(dve):
                dve.sem_inc(qn_ready, DEPTH)
                dve.sem_inc(qbd_ready, DEPTH)
                dve.wait_ge(s_w, 16 * 10)
                nc.vector.tensor_tensor(wctx[:, :, :], wi_sb[:, KC:2 * KC, :], wi_sb[:, 2 * KC:3 * KC, :], ALU.add).then_inc(wctx_ready, 1)
                dve.wait_ge(s_x, 64)
                for t in range(T):
                    ins = nc.vector.bn_stats(out=stats[:, t, :], in_=x_all[:, t * E:(t + 1) * E])
                after(dve, dve_step, ins)
                for t in range(T):
                    ins = nc.vector.bn_aggr(out=mv[:, 2 * t:2 * t + 2], in_=stats[:, t, :])
                after(dve, dve_step, ins)
                var = mv[:, :].rearrange("p (t c) -> p t c", c=2)[:, :, 1]
                nc.vector.tensor_scalar(rstd[:, :], var, 1.0e-5, None, ALU.add).then_inc(rstd_in, 1)
                dve.wait_ge(rstd_sq, 1)
                after(dve, dve_step, nc.vector.reciprocal(rstd[:, :], rstd[:, :]))

                def norm(t, p):
                    dve.wait_ge(tr_done, freed(t))
                    nc.vector.tensor_scalar(qn[p][:, :], x_all[:, bass.ds(t * E, E)], mv[:, bass.ds(t * 2, 1)],
                                            rstd[:, bass.ds(t, 1)], ALU.subtract, ALU.mult).then_inc(qn_ready, 1)

                def spread(t, p):
                    dve.wait_ge(qkT_ready, done(t))
                    dve.wait_ge(scores_done, freed(t))
                    nc.vector.tensor_tensor(qbd[p][:, :, :, :],
                                            qkT[p][:, 0:KC, :].unsqueeze(2).to_broadcast([P, KC, HC, P]),
                                            head_mask.unsqueeze(1).unsqueeze(3).to_broadcast([P, KC, HC, P]),
                                            ALU.mult).then_inc(qbd_ready, 1)

                def step(t, p):
                    norm(t + 1, 1 - p)
                    spread(t, p)
                dve.wait_ge(s_c, 16)
                norm(0, 0)
                paired(dve, step, 0, T - 2)
                step(T - 2, 0)
                spread(T - 1, 1)

            @block.scalar
            def _(act):
                act.sem_inc(qkT_ready, DEPTH)
                act.sem_inc(gates_out, DEPTH)
                act.sem_inc(scores_out, DEPTH)
                act.dma_start(wi_sb[:, :, 0:NH], w_i.rearrange("(c p) h -> p c h", p=P)).then_inc(s_w, 16)
                act.dma_start(wi_sb[:, :, NH:NG], w_f.rearrange("(c p) h -> p c h", p=P)).then_inc(s_w, 16)
                act.dma_start(bias_bc[:, 0:NH], b_i.partition_broadcast(P)).then_inc(s_w, 16)
                act.dma_start(bias_bc[:, NH:NG], b_f.partition_broadcast(P)).then_inc(s_w, 16)
                act.dma_start(lnsc[:, :], ln_scale.partition_broadcast(P)).then_inc(s_w, 16)
                act.dma_start(gx[:, :], g_x.partition_broadcast(P)).then_inc(s_w, 16)
                act.dma_start(gf[:, :], g_f.partition_broadcast(P)).then_inc(s_r, 16)
                act.dma_start(rw[:, :, :], router_w.rearrange("(c p) n -> p c n", p=P)).then_inc(s_r, 16)
                act.wait_ge(rstd_in, 1)
                nc.scalar.activation(rstd[:, :], rstd[:, :], ACT.Sqrt).then_inc(rstd_sq, 1)

                def copy_qkT(t, p):
                    act.wait_ge(tr_done, done(t))
                    act.wait_ge(scores_done, freed(t))
                    nc.scalar.activation(qkT[p][:, :, :], bank[:, 4 + p, :].rearrange("p (c s) -> p c s", s=P),
                                         ACT.Copy).then_inc(qkT_ready, 1)

                def copy_out(t, p):
                    act.wait_ge(gates_done, done(t))
                    nc.scalar.activation(gates[:, bass.ds(t * NG, NG)], bank[:, 6 + p, 0:NG], ACT.Copy).then_inc(gates_out, 1)
                    act.wait_ge(scores_done, done(t))
                    dst = s_all[:, bass.ds(t * NH * S, NH * S)].rearrange("p (c m) -> p c m", c=KC)
                    nc.scalar.activation(dst, bank[:, 2 * p:2 * p + 2, :], ACT.Copy).then_inc(scores_out, 1)

                def step(t, p):
                    copy_qkT(t + 1, 1 - p)
                    copy_out(t, p)
                copy_qkT(0, 0)
                paired(act, step, 0, T - 2)
                step(T - 2, 0)
                copy_out(T - 1, 1)

            @block.tensor
            def _(pe):
                pe.sem_inc(tr_done, DEPTH)
                pe.sem_inc(gates_done, DEPTH)
                pe.sem_inc(scores_done, DEPTH)
                pe.wait_ge(s_c, 16)
                pe.wait_ge(wctx_ready, 1)

                def transposes(t, p, rounds):
                    pe.wait_ge(qn_ready, done(t))
                    pe.wait_ge(ctx_in[p], rounds * 16)
                    pe.wait_ge(qkT_ready, freed(t))
                    for k, src in enumerate((qn[p], ct[p])):
                        for c in range(KC):
                            ins = nc.tensor.transpose(bank[:, 4 + p, (2 * k + c) * P:(2 * k + c + 1) * P],
                                                      src[:, c * P:(c + 1) * P], ident)
                    ins.then_inc(tr_done, 1)

                def products(t, p):
                    pe.wait_ge(qkT_ready, done(t))
                    pe.wait_ge(gates_out, freed(t))
                    for k in range(2 * KC):
                        w = wi_sb[:, k, :] if k < KC else wctx[:, k - KC, :]
                        ins = nc.tensor.matmul(bank[:, 6 + p, 0:NG], qkT[p][:, k, :], w, start=(k == 0), stop=(k == 2 * KC - 1))
                    ins.then_inc(gates_done, 1)
                    pe.wait_ge(qbd_ready, done(t))
                    pe.wait_ge(scores_out, freed(t))
                    for c in range(KC):
                        for b in range(2):
                            r = slice(b * S, (b + 1) * S)
                            ins = nc.tensor.matmul(bank[r, 2 * p + c, :], qkT[p][:, KC + c, r], qbd[p][:, c, :, r],
                                                   start=True, stop=True)
                    ins.then_inc(scores_done, 1)

                transposes(0, 0, 1)
                with pe.Fori(0, T // 2 - 1) as it:
                    transposes(it * 2 + 1, 1, it + 1)
                    products(it * 2, 0)
                    transposes(it * 2 + 2, 0, it + 2)
                    products(it * 2 + 1, 1)
                transposes(T - 1, 1, T // 2)
                products(T - 2, 0)
                products(T - 1, 1)

        gates3 = gates[:, :].rearrange("p (t g) -> p t g", g=NG)

        def th(v):
            return v.rearrange("p (t h) -> p t h", h=NH)

        z_ready, l_ready, lf_ready, f_done, a_ready, aT_done, g_ready, gT_done, g_out, m_ready, em_ready = (
            sem(n) for n in ("z_ready", "l_ready", "lf_ready", "f_done", "a_ready", "aT_done", "g_ready", "gT_done",
                             "g_out", "m_ready", "em_ready"))
        sc = hq[:, 0:T * NH]
        with nc.Block() as block:
            @block.vector
            def _(dve):
                dve.wait_ge(s_w, 16 * 10)
                after(dve, dve_step, nc.vector.tensor_tensor(gates3, gates3, bias_bc[:, :].unsqueeze(1).to_broadcast([P, T, NG]), ALU.add))
                f = gates3[:, :, NH:NG]
                nc.vector.scalar_tensor_tensor(th(sc), f, -1.0, f, ALU.mult, ALU.min).then_inc(z_ready, 1)
                dve.wait_ge(l_ready, 1)
                nc.vector.scalar_tensor_tensor(th(lf[:, :]), f, 0.0, th(sc), ALU.min, ALU.subtract).then_inc(lf_ready, 1)
                dve.wait_ge(f_done, 1)
                nc.vector.tensor_tensor(th(a_all[:, :]), gates3[:, :, 0:NH], th(bank[:, 0, 0:T * NH]), ALU.subtract).then_inc(a_ready, 1)
                nc.vector.tensor_copy(fcum[:, :], bank[:, 0, 0:T * NH])
                dve.wait_ge(aT_done, 1)
                after(dve, dve_step, nc.vector.tensor_copy(scan[0][:, :, PAD:PAD + S], bank[:, 1, 0:2 * G * S].rearrange("p (g s) -> p g s", s=S)))
                k, sh = 0, 1
                while sh < S:
                    to = scan[1 - k][:, :, PAD:PAD + S] if 2 * sh < S else gcum[:, :, :]
                    ins = nc.vector.tensor_tensor(to, scan[k][:, :, PAD:PAD + S],
                                                  scan[k][:, :, PAD - sh:PAD + S - sh], ALU.max)
                    k, sh = 1 - k, 2 * sh
                    if sh < S:
                        after(dve, dve_step, ins)
                ins.then_inc(g_ready, 1)
                dve.wait_ge(gT_done, 1)
                nc.vector.tensor_tensor(m_all[:, :], fcum[:, :], bank[:, 2, 0:T * NH], ALU.add).then_inc(m_ready, 1)

            @block.scalar
            def _(act):
                act.wait_ge(z_ready, 1)
                after(act, act_step, nc.scalar.activation(sc, sc, ACT.Exp))
                nc.scalar.activation(sc, sc, ACT.Ln, bias=1.0).then_inc(l_ready, 1)
                act.wait_ge(m_ready, 1)
                nc.scalar.activation(m_all[:, :], m_all[:, :], ACT.Exp, scale=-1.0).then_inc(em_ready, 1)
                nc.scalar.activation(gx[:, :], gx[:, :], ACT.Tanh)

            @block.tensor
            def _(pe):
                pe.wait_ge(lf_ready, 1)
                nc.tensor.matmul(bank[:, 0, 0:T * NH], tri_seq, lf[:, :], start=True, stop=True).then_inc(f_done, 1)
                pe.wait_ge(a_ready, 1)
                for g in range(G):
                    ins = nc.tensor.transpose(bank[:, 1, g * P:(g + 1) * P], a_all[:, g * P:(g + 1) * P], ident)
                ins.then_inc(aT_done, 1)
                pe.wait_ge(g_ready, 1)
                for g in range(G):
                    ins = nc.tensor.transpose(bank[:, 2, g * P:(g + 1) * P], gcum[:, 2 * g:2 * g + 2, :].rearrange("p b s -> p (b s)"), ident)
                ins.then_inc(gT_done, 1)

            @block.sync
            def _(sp):
                sp.wait_ge(g_ready, 1)
                gd = g_dram.rearrange("(g t b) (h s) -> g b t h s", g=G, b=2, s=S)
                for g in range(G):
                    for b in range(2):
                        for t in range(TG):
                            sp.dma_start(gd[g, b, t, :, :], gcum[t * NH:(t + 1) * NH, 2 * g + b, :]).then_inc(g_out, 16)
                sp.wait_ge(g_out, 16 * 2 * T)

        gb_in = [sem(f"gb_in{p}") for p in range(2)]
        d_ready, dm_ready, e_ready, c_ready, vt_ready, h_done, h_out = (
            sem(n) for n in ("d_ready", "dm_ready", "e_ready", "c_ready", "vt_ready", "h_done", "h_out"))
        hc_ready, sq_ready, var_ready, rs_ready, hn_ready, x_ready = (
            sem(n) for n in ("hc_ready", "sq_ready", "var_ready", "rs_ready", "hn_ready", "x_ready"))
        lnsc_ready = sem("lnsc_ready")
        NCH = CT * NH
        NQ = T // CT
        DB = len(dd)
        hh3 = hh[:, :].rearrange("p (h d) -> p h d", d=DH)
        hq3 = hq[:, :].rearrange("p (h d) -> p h d", d=DH)
        r0, r1 = hs[:, 0, :], hs[:, 1, :]

        def hs3(v):
            return v.rearrange("p (h s) -> p h s", s=S)

        with nc.Block() as block:
            @block.sync
            def _(sp):
                clear = slot_x.rearrange("(p n) e -> p (n e)", p=P)

                def load_g(t, p):
                    sp.wait_ge(d_ready, freed(t))
                    for b in range(2):
                        sp.dma_start(gb[p][b * S:(b + 1) * S, :], g_dram[bass.ds(t * 2 + b, 1), :].to_broadcast([S, NH * S])).then_inc(gb_in[p], 16)
                with sp.Fori(0, T // 2) as it:
                    for p in range(2):
                        load_g(it * 2 + p, p)
                        sp.dma_start(clear[:, bass.ds((it * 2 + p) * ZW, ZW)], zeros[:, :]).then_inc(cleared, 16)
                for z in range(T, NZ):
                    sp.dma_start(clear[:, z * ZW:(z + 1) * ZW], zeros[:, :]).then_inc(cleared, 16)

            @block.gpsimd
            def _(pool):
                pool.sem_inc(d_ready, DEPTH)
                pool.sem_inc(vt_ready, DEPTH)
                pool.sem_inc(x_ready, 1)

                def spread(t, p, d, rounds, first):
                    pool.wait_ge(gb_in[p], rounds * 32)
                    if not first:
                        pool.wait_ge(h_done, t - DB + 1 + DEPTH)
                    pool.tensor_tensor(hs3(dd[d][:, :]), a_all[:, bass.ds(t * NH, NH)].unsqueeze(2).to_broadcast([P, NH, S]),
                                       hs3(gb[p][:, :]), ALU.subtract).then_inc(d_ready, 1)
                    pool.wait_ge(h_done, freed(t))
                    for b in range(2):
                        ins = pool.tensor_tensor(vbd[p][:, :, b, :, 0:DH],
                                                 ctx_all[:, bass.ds(t * E, E)].rearrange("p (j h d) -> p j h d", h=2, d=DH),
                                                 seq_mask[:, b:b + 1].unsqueeze(2).unsqueeze(3).to_broadcast([P, NH // 2, 2, DH]), ALU.mult)
                    ins.then_inc(vt_ready, 1)

                def root(c):
                    pool.wait_ge(var_ready, c + 1)
                    pool.tensor_tensor(r1, r1, half[:, :], ALU.pow).then_inc(rs_ready, 1)

                def residual(c):
                    pool.wait_ge(hn_ready, c + 1)
                    pool.tensor_tensor(hh[:, :].rearrange("p (t e) -> p t e", e=E), hh[:, :].rearrange("p (t e) -> p t e", e=E),
                                       lnsc[:, :].unsqueeze(1).to_broadcast([P, CT, E]), ALU.mult).then_inc(pool_norm, 1)
                    pool.wait_ge(pool_norm, c + 1)
                    xs = x_all[:, bass.ds(c * (CT * E), CT * E)]
                    pool.tensor_tensor(xs, xs, hh[:, :], ALU.add).then_inc(x_ready, 1)

                def body(it, norm):
                    for u in range(CT):
                        spread(it * CT + u, u % 2, u, it * 2 + u // 2 + 1, not norm)
                        if norm and u == 2:
                            root(it - 1)
                        if norm and u == 3:
                            residual(it - 1)
                body(0, False)
                pool.wait_ge(lnsc_ready, 1)
                with pool.Fori(1, NQ) as it:
                    body(it, True)
                root(NQ - 1)
                residual(NQ - 1)

            @block.vector
            def _(dve):
                dve.sem_inc(dm_ready, DEPTH)
                dve.sem_inc(c_ready, DEPTH)
                nc.vector.tensor_scalar(lnsc[:, :], lnsc[:, :], gx[:, 0:1], None, ALU.mult).then_inc(lnsc_ready, 1)

                def clip(t, d):
                    dve.wait_ge(d_ready, done(t))
                    nc.vector.scalar_tensor_tensor(hs3(dd[d][:, :]), hs3(dd[d][:, :]), 0.0,
                                                   neg_mask.unsqueeze(1).to_broadcast([P, NH, S]), ALU.min, ALU.add).then_inc(dm_ready, 1)

                def weigh(t, d):
                    dve.wait_ge(e_ready, done(t))
                    nc.vector.tensor_tensor(dd[d][:, :], dd[d][:, :], s_all[:, bass.ds(t * NH * S, NH * S)], ALU.mult).then_inc(c_ready, 1)

                PER = 6

                def norm(c, part, n=[0]):
                    def link(ins):
                        n[0] += 1
                        ins.then_inc(dve_norm, 1)
                        dve.wait_ge(dve_norm, c * PER + n[0])
                    if part == 0:
                        n[0] = 0
                        h4 = h_all[:, bass.ds(c * (NCH * VW), NCH * VW)].rearrange("p (h d) -> p h d", d=VW)
                        dve.wait_ge(h_out, c * CT + CT + DEPTH)
                        link(nc.vector.scalar_tensor_tensor(r0, h4[:, :, DH], -1.0, h4[:, :, DH], ALU.mult, ALU.max))
                        link(nc.vector.tensor_tensor(r0, r0, m_all[:, bass.ds(c * NCH, NCH)], ALU.max))
                        link(nc.vector.tensor_scalar(r0, r0, 1.0e-6, None, ALU.add))
                        link(nc.vector.reciprocal(r0, r0))
                        dve.wait_ge(x_ready, c + 1)
                        link(nc.vector.tensor_tensor(hh3, h4[:, :, 0:DH], r0.unsqueeze(2).to_broadcast([P, NCH, DH]), ALU.mult))
                        link(nc.vector.tensor_reduce(r1, hh3, AX.X, ALU.add))
                        nc.vector.scalar_tensor_tensor(hh3, r1.unsqueeze(2).to_broadcast([P, NCH, DH]), -1.0 / DH, hh3, ALU.mult, ALU.add).then_inc(hc_ready, 1)
                        assert n[0] == PER
                    if part == 1:
                        dve.wait_ge(sq_ready, c + 1)
                        nc.vector.tensor_reduce(r1, hq3, AX.X, ALU.add).then_inc(dve_sum, 1)
                        dve.wait_ge(dve_sum, c + 1)
                        nc.vector.tensor_scalar(r1, r1, 1.0 / DH, 1.0e-6, ALU.mult, ALU.add).then_inc(var_ready, 1)
                    if part == 2:
                        dve.wait_ge(rs_ready, c + 1)
                        nc.vector.tensor_tensor(hh3, hh3, r1.unsqueeze(2).to_broadcast([P, NCH, DH]), ALU.mult).then_inc(hn_ready, 1)

                def body(it, first, last):
                    for u in range(CT):
                        if not (last and u == CT - 1):
                            clip(it * CT + u + 1, (u + 1) % CT)
                        if not first:
                            norm(it - 1, u)
                        weigh(it * CT + u, u)
                clip(0, 0)
                body(0, True, False)
                with dve.Fori(1, NQ - 1) as it:
                    body(it, False, False)
                body(NQ - 1, False, True)
                for part in range(3):
                    norm(NQ - 1, part)

            @block.scalar
            def _(act):
                act.sem_inc(e_ready, DEPTH)
                act.sem_inc(h_out, DEPTH)

                def expo(t, d):
                    act.wait_ge(dm_ready, done(t))
                    nc.scalar.activation(dd[d][:, :], dd[d][:, :], ACT.Exp).then_inc(e_ready, 1)

                def copy_h(t, p):
                    act.wait_ge(h_done, done(t))
                    for b in range(2):
                        dst = h_all[b * S:(b + 1) * S, bass.ds(t * NH * VW, NH * VW)].rearrange("p (k j h d) -> p k j h d", k=2, h=2, d=VW)
                        for h in range(2):
                            src = bank[h * S:(h + 1) * S, 2 * p:2 * p + 2, 0:NH * VW].rearrange("p k (j b h d) -> p k j b h d", b=2, h=2, d=VW)
                            ins = nc.scalar.activation(dst[:, :, :, h, :], src[:, :, :, b, h, :], ACT.Copy)
                    ins.then_inc(h_out, 1)

                def square(c):
                    act.wait_ge(hc_ready, c + 1)
                    nc.scalar.activation(hq[:, :], hh[:, :], ACT.Square).then_inc(sq_ready, 1)

                def body(it, first, last):
                    for u in range(CT):
                        if not (last and u == CT - 1):
                            expo(it * CT + u + 1, (u + 1) % CT)
                        if not first and u == 1:
                            square(it - 1)
                        copy_h(it * CT + u, u % 2)
                expo(0, 0)
                body(0, True, False)
                with act.Fori(1, NQ - 1) as it:
                    body(it, False, False)
                body(NQ - 1, False, True)
                square(NQ - 1)

            @block.tensor
            def _(pe):
                pe.sem_inc(h_done, DEPTH)
                with pe.Fori(0, NQ) as it:
                    for u in range(CT):
                        t, p = it * CT + u, u % 2
                        pe.wait_ge(c_ready, done(t))
                        pe.wait_ge(vt_ready, done(t))
                        pe.wait_ge(h_out, freed(t))
                        for j in range(NH // 2):
                            at = (j % 4) * 4 * VW
                            ins = nc.tensor.matmul(bank[:, 2 * p + j // 4, at:at + 4 * VW], dd[u][:, j * P:(j + 1) * P],
                                                   vbd[p][:, j, :, :, :].rearrange("p b h d -> p (b h d)"), start=True, stop=True)
                        ins.then_inc(h_done, 1)

        xn_ready, xT_done, xT_copied, lg_done, lg_out, xn_kept, r5_in, r5_sq = (
            sem(n) for n in ("xn_ready", "xT_done", "xT_copied", "lg_done", "lg_out", "xn_kept", "r5_in", "r5_sq"))
        xT_st = [sem(f"xT_st{p}") for p in range(2)]
        with nc.Block() as block:
            @block.vector
            def _(dve):
                dve.sem_inc(xn_ready, DEPTH)
                for t in range(T):
                    ins = nc.vector.bn_stats(out=stats[:, t, :], in_=x_all[:, t * E:(t + 1) * E])
                after(dve, dve_step, ins)
                for t in range(T):
                    ins = nc.vector.bn_aggr(out=mv[:, 2 * t:2 * t + 2], in_=stats[:, t, :])
                after(dve, dve_step, ins)
                var = mv[:, :].rearrange("p (t c) -> p t c", c=2)[:, :, 1]
                nc.vector.tensor_scalar(rstd[:, :], var, 1.0e-5, None, ALU.add).then_inc(r5_in, 1)
                nc.vector.tensor_copy(tri_b[:, :], tri_all)
                dve.wait_ge(r5_sq, 1)
                after(dve, dve_step, nc.vector.reciprocal(rstd[:, :], rstd[:, :]))

                def norm(t, p):
                    dve.wait_ge(xT_done, freed(t))
                    dve.wait_ge(xn_kept, freed(t))
                    nc.vector.tensor_scalar(qn[p][:, :], x_all[:, bass.ds(t * E, E)], mv[:, bass.ds(t * 2, 1)],
                                            rstd[:, bass.ds(t, 1)], ALU.subtract, ALU.mult).then_inc(xn_ready, 1)
                paired(dve, norm)

            @block.gpsimd
            def _(pool):
                pool.sem_inc(xn_kept, DEPTH)

                def keep(t, p):
                    pool.wait_ge(xn_ready, done(t))
                    pool.tensor_copy(xn_all[:, bass.ds(t * E, E)], qn[p][:, :]).then_inc(xn_kept, 1)
                paired(pool, keep)

            @block.scalar
            def _(act):
                act.sem_inc(xT_copied, DEPTH)
                act.sem_inc(lg_out, DEPTH)
                for p in range(2):
                    act.sem_inc(xT_st[p], 16)
                act.dma_start(se13[:, :, :], se_w13.rearrange("(j p) n -> p j n", p=P)).then_inc(s_se, 16)
                act.dma_start(se2[:, :, :], se_w2.rearrange("(j p) n -> p j n", p=IH)).then_inc(s_se, 16)
                act.wait_ge(r5_in, 1)
                nc.scalar.activation(rstd[:, :], rstd[:, :], ACT.Sqrt).then_inc(r5_sq, 1)
                with act.Fori(0, T // 2) as it:
                    for p in range(2):
                        t = it * 2 + p
                        act.wait_ge(xT_done, done(t))
                        act.wait_ge(lg_done, freed(t))
                        act.wait_ge(xT_st[p], it * 16 + 16)
                        nc.scalar.activation(qkT[p][:, 0:KC, :], bank[:, 4 + p, 0:E].rearrange("p (c s) -> p c s", s=P),
                                             ACT.Copy).then_inc(xT_copied, 1)
                        act.wait_ge(lg_done, done(t))
                        nc.scalar.activation(lg_all[:, bass.ds(t * NR, NR)], bank[:, 6 + p, 0:NR], ACT.Copy).then_inc(lg_out, 1)

            @block.sync
            def _(sp):
                with sp.Fori(0, T // 2) as it:
                    for p in range(2):
                        t = it * 2 + p
                        sp.wait_ge(xT_copied, done(t))
                        sp.dma_start(xT_dram[bass.ds(t * P, P), :], qkT[p][:, 0:KC, :].rearrange("p c s -> p (c s)")).then_inc(xT_st[p], 16)

            @block.tensor
            def _(pe):
                pe.sem_inc(xT_done, DEPTH)
                pe.sem_inc(lg_done, DEPTH)
                pe.wait_ge(s_r, 32)

                def transposes(t, p):
                    pe.wait_ge(xn_ready, done(t))
                    pe.wait_ge(xT_copied, freed(t))
                    for c in range(KC):
                        ins = nc.tensor.transpose(bank[:, 4 + p, c * P:(c + 1) * P], qn[p][:, c * P:(c + 1) * P], ident)
                    ins.then_inc(xT_done, 1)

                def logits(t, p):
                    pe.wait_ge(xT_copied, done(t))
                    pe.wait_ge(lg_out, freed(t))
                    for c in range(KC):
                        ins = nc.tensor.matmul(bank[:, 6 + p, 0:NR], qkT[p][:, c, :], rw[:, c, :], start=(c == 0), stop=(c == KC - 1))
                    ins.then_inc(lg_done, 1)

                def step(t, p):
                    transposes(t + 1, 1 - p)
                    logits(t, p)
                transposes(0, 0)
                paired(pe, step, 0, T - 2)
                step(T - 2, 0)
                logits(T - 1, 1)

        def tn(v, n=NE):
            return v.rearrange("p (t n) -> p t n", n=n)

        e_in, e_out, oh_ready, rank_done, eob_ready, eobT_done, slots_ready = (
            sem(n) for n in ("e_in", "e_out", "oh_ready", "rank_done", "eob_ready", "eobT_done", "slots_ready"))
        HB = T // 2
        with nc.Block() as block:
            @block.vector
            def _(dve):
                step = lambda ins: after(dve, dve_step, ins)
                lg = tn(lg_all, NR)
                for t in range(T):
                    ins = nc.vector.max(top[:, t, :], lg_all[:, t * NR:t * NR + NE])
                step(ins)
                for t in range(T):
                    ins = nc.vector.max_index(topi[:, t, :], top[:, t, :], lg_all[:, t * NR:t * NR + NE])
                step(ins)
                nc.vector.tensor_tensor(tn(prob), lg[:, :, 0:NE], top[:, :, 0].unsqueeze(2).to_broadcast([P, T, NE]), ALU.subtract)
                step(nc.vector.tensor_copy(topf[:, :, :], topi[:, :, 0:K4]))
                nc.vector.tensor_copy(sgate[:, :], lg[:, :, NE])
                nc.vector.tensor_tensor(tn(wk[:, :], K4), top[:, :, 0:K4], top[:, :, 0].unsqueeze(2).to_broadcast([P, T, K4]), ALU.subtract).then_inc(e_in, 1)
                for k in range(K4):
                    ins = nc.vector.tensor_tensor(tn(oh[k]), iota_e.unsqueeze(1).to_broadcast([P, T, NE]),
                                                  topf[:, :, k].unsqueeze(2).to_broadcast([P, T, NE]), ALU.is_equal)
                ins.then_inc(oh_ready, 1)
                dve.wait_ge(e_out, 1)
                step(nc.vector.tensor_reduce(zsum[:, :], tn(prob), AX.X, ALU.add))
                nc.vector.tensor_scalar(sgate[:, :], sgate[:, :], 1.0, None, ALU.add)
                step(nc.vector.reciprocal(zsum[:, :], zsum[:, :]))
                nc.vector.tensor_scalar(zsum[:, :], zsum[:, :], gf[:, 0:1], None, ALU.mult)
                step(nc.vector.reciprocal(sgate[:, :], sgate[:, :]))
                nc.vector.tensor_scalar(sgate[:, :], sgate[:, :], gf[:, 0:1], None, ALU.mult)
                step(nc.vector.tensor_tensor(tn(wk[:, :], K4), tn(wk[:, :], K4), zsum[:, :].unsqueeze(2).to_broadcast([P, T, K4]), ALU.mult))
                dve.wait_ge(rank_done, 1)
                pad = 8 * NE
                for b in range(2):
                    nc.vector.tensor_copy(tcum[0][:, pad + (1 + b * HB) * NE:pad + min((1 + (b + 1) * HB), T) * NE] if b == 0 else
                                          tcum[0][:, pad + (1 + HB) * NE:pad + T * NE],
                                          bank[:, 2 + b, 0:HB * NE] if b == 0 else bank[:, 2 + b, 0:(HB - 1) * NE])
                nc.vector.tensor_copy(cnt[:, :], bank[:, 3, (HB - 1) * NE:HB * NE])
                nc.vector.memset(ecum[0][:, 0:EP], 0.0)
                nc.vector.memset(ecum[1][:, 0:EP], 0.0)
                nc.vector.memset(tcum[1][:, 0:pad], 0.0)
                step(nc.vector.memset(tcum[0][:, 0:pad + NE], 0.0))
                k, sh = 0, 1
                while sh < T:
                    step(nc.vector.tensor_tensor(tcum[1 - k][:, pad:], tcum[k][:, pad:], tcum[k][:, pad - sh * NE:pad + (T - sh) * NE], ALU.add))
                    k, sh = 1 - k, 2 * sh
                tex = tcum[k][:, pad:]
                step(nc.vector.tensor_tensor(cnt[:, :], cnt[:, :], tex[:, (T - 1) * NE:T * NE], ALU.add))
                step(nc.vector.tensor_tensor(cmp[:, :, :], cnt[:, :].unsqueeze(2).to_broadcast([P, NE, T]),
                                             fills.unsqueeze(1).to_broadcast([P, NE, T]), ALU.is_gt))
                step(nc.vector.tensor_reduce(nblk[:, :], cmp[:, :, :], AX.X, ALU.add))
                step(nc.vector.tensor_copy(ecum[0][:, EP:], nblk[:, :]))
                k, sh = 0, 1
                while sh < NE:
                    step(nc.vector.tensor_tensor(ecum[1 - k][:, EP:], ecum[k][:, EP:], ecum[k][:, EP - sh:EP + NE - sh], ALU.add))
                    k, sh = 1 - k, 2 * sh
                ends = ecum[k][:, EP:]
                nc.vector.tensor_tensor(nblk[:, :], ends, nblk[:, :], ALU.subtract)
                step(nc.vector.tensor_scalar(cmp[:, :, 0], ends, iota_p, None, ALU.is_le))
                step(nc.vector.tensor_reduce(eob[:, :], cmp[:, :, 0], AX.X, ALU.add))
                nc.vector.tensor_scalar(eob[:, :], eob[:, :], float(NE - 1), None, ALU.min).then_inc(eob_ready, 1)
                step(nc.vector.tensor_scalar(last_f[:, :], ends[:, NE - 1:NE], 1.0 / WB, -1.0, ALU.mult, ALU.add))
                step(nc.vector.tensor_scalar(cmp[:, :, 1], iota_e, last_f[:, 0:1], None, ALU.is_lt))
                step(nc.vector.tensor_reduce(last_f[:, :], cmp[:, :, 1], AX.X, ALU.add))
                nc.vector.tensor_copy(eob_row[0:1, P:P + 1], last_f[0:1, :])
                step(nc.vector.tensor_scalar(nblk[:, :], nblk[:, :], float(P), None, ALU.mult))
                step(nc.vector.tensor_tensor(tn(pos), tn(tex), nblk[:, :].unsqueeze(1).to_broadcast([P, T, NE]), ALU.add))
                for b in range(2):
                    r = slice(b * HB * NE, (b + 1) * HB * NE)
                    ins = nc.vector.tensor_tensor(pos[:, r], pos[:, r], bank[:, b, 0:HB * NE], ALU.add)
                step(ins)
                for kk in range(K4):
                    step(nc.vector.tensor_tensor(prob, pos, oh[kk], ALU.mult))
                    step(nc.vector.tensor_reduce(slotf[:, :, kk], tn(prob), AX.X, ALU.add))
                nc.vector.tensor_copy(tn(slotu[:, :], K4), slotf[:, :, :]).then_inc(slots_ready, 1)
                dve.wait_ge(eobT_done, 1)
                nc.vector.tensor_copy(eob_row[0:1, 0:P], bank[0:1, 4, 0:P])

            @block.scalar
            def _(act):
                act.wait_ge(e_in, 1)
                nc.scalar.activation(prob, prob, ACT.Exp)
                nc.scalar.activation(wk[:, :], wk[:, :], ACT.Exp)
                nc.scalar.activation(sgate[:, :], sgate[:, :], ACT.Exp, scale=-1.0)
                nc.scalar.activation(gf[:, :], gf[:, :], ACT.Tanh).then_inc(e_out, 1)

            @block.tensor
            def _(pe):
                pe.wait_ge(oh_ready, 1)
                for b in range(2):
                    for k, lhs in enumerate((tri_b, ones_b)):
                        for q in range(K4):
                            ins = nc.tensor.matmul(bank[:, 2 * k + b, 0:HB * NE], lhs[:, :], oh[q][:, b * HB * NE:(b + 1) * HB * NE],
                                                   start=(q == 0), stop=(q == K4 - 1))
                ins.then_inc(rank_done, 1)
                pe.wait_ge(eob_ready, 1)
                nc.tensor.matmul(bank[0:1, 4, 0:P], eob[:, 0:1], ident, start=True, stop=True).then_inc(eobT_done, 1)

        scattered, rest_cleared = sem("scattered"), sem("rest_cleared")
        xs_in = [sem(f"xs_in{p}") for p in range(2)]
        sgu_done, ssg_ready, sh_ready, shT_done, shT_ready, sy_done, sy_out = (
            sem(n) for n in ("sgu_done", "ssg_ready", "sh_ready", "shT_done", "shT_ready", "sy_done", "sy_out"))

        def up(s, p, xt_buf, w, at_w):
            for c in range(KC):
                ins = nc.tensor.matmul(bank[:, p, 0:I2], xt_buf[:, c, :], w[:, at_w + c * I2:at_w + (c + 1) * I2],
                                       start=(c == 0), stop=(c == KC - 1))
            return ins

        def turn(p):
            for c in range(2):
                ins = nc.tensor.transpose(bank[0:IH, 4 + p, c * P:(c + 1) * P], hb[p][:, c * IH:(c + 1) * IH], ident)
            return ins

        def down(p, ybank, w, at_w, first, last):
            for c in range(2):
                ins = nc.tensor.matmul(bank[:, ybank, 0:E], hT[p][:, c, :], w[:, at_w + c * E:at_w + (c + 1) * E],
                                       start=(first and c == 0), stop=(last and c == 1))
            return ins

        NS = SUB * T
        with nc.Block() as block:
            @block.gpsimd
            def _(pool):
                pool.wait_ge(cleared, 16 * NZ)
                pool.wait_ge(slots_ready, 1)
                for t in range(T):
                    for k in range(K4):
                        c = t * K4 + k
                        pool.indirect_dma_start(slot_x[:, :], bass.IndirectOffsetOnAxis(slotu[:, c:c + 1], 0),
                                                xn_all[:, t * E:(t + 1) * E], None).then_inc(scattered, 16)
                pool.wait_ge(scattered, 16 * T * K4)

            @block.sync
            def _(sp):
                def load(t, p):
                    sp.dma_start(xT[p][:, :, :].rearrange("p c s -> p (c s)"), xT_dram[bass.ds(t * P, P), :]).then_inc(xs_in[p], 16)
                load(0, 0)
                load(1, 1)
                with sp.Fori(1, T // 2) as it:
                    for p in range(2):
                        sp.wait_ge(sgu_done, (it - 1) * (2 * SUB) + p * SUB + SUB + DEPTH)
                        load(it * 2 + p, p)
                last = sp.value_load(eob_row[0:1, P:P + 1], min_val=N * K4 // P // WB - 1, max_val=NB // WB - 1)
                with sp.Fori(N * K4 // P // WB, NB // WB) as it:
                    with sp.If(it <= last):
                        sp.sem_inc(rest_cleared, 16)
                    with sp.Else():
                        sp.dma_start(slot_y[bass.ds(it * (WB * P), WB * P), :].rearrange("(p n) e -> p (n e)", p=P),
                                     zeros[:, 0:WB * E]).then_inc(rest_cleared, 16)
                sp.wait_ge(rest_cleared, 16 * (NB - N * K4 // P) // WB)

            @block.tensor
            def _(pe):
                pe.sem_inc(sgu_done, DEPTH)
                pe.sem_inc(shT_done, DEPTH)
                pe.sem_inc(sy_done, DEPTH)
                pe.wait_ge(s_se, 32)

                def pe_up(s, j, rounds):
                    if j % SUB == 0:
                        pe.wait_ge(xs_in[j // SUB], rounds * 16)
                    pe.wait_ge(sh_ready, freed(s))
                    up(s, j % 2, xT[j // SUB], se13[:, j % SUB, :], 0).then_inc(sgu_done, 1)

                def pe_turn(s, j):
                    pe.wait_ge(sh_ready, done(s))
                    pe.wait_ge(shT_ready, freed(s))
                    turn(j % 2).then_inc(shT_done, 1)

                def pe_down(s, t, j):
                    if j % SUB == 0:
                        pe.wait_ge(sy_out, freed(t))
                    pe.wait_ge(shT_ready, done(s))
                    ins = down(j % 2, 6 + j // SUB, se2[:, j % SUB, :], 0, j % SUB == 0, j % SUB == SUB - 1)
                    ins.then_inc(sy_done, 1)

                R = 2 * SUB

                def body(it, lag):
                    for j in range(R):
                        s = it * R + j
                        pe_up(s, j, it + 1)
                        if lag or j >= 1:
                            pe_turn(s - 1, (j - 1) % R)
                        if lag or j >= 2:
                            t2 = it * 2 + (j - 2) // SUB if j >= 2 else it * 2 - 1
                            pe_down(s - 2, t2, (j - 2) % R)
                body(0, False)
                with pe.Fori(1, NS // R) as it:
                    body(it, True)
                pe_turn(NS - 1, R - 1)
                pe_down(NS - 2, T - 1, R - 2)
                pe_down(NS - 1, T - 1, R - 1)

            @block.scalar
            def _(act):
                act.sem_inc(ssg_ready, DEPTH)
                act.sem_inc(shT_ready, DEPTH)

                def silu(s, p):
                    act.wait_ge(sgu_done, done(s))
                    act.wait_ge(sh_ready, freed(s))
                    nc.scalar.activation(sg[p][:, :], bank[:, p, 0:I], ACT.Silu).then_inc(ssg_ready, 1)

                def copy_hT(s, p):
                    act.wait_ge(shT_done, done(s))
                    act.wait_ge(sy_done, freed(s))
                    nc.scalar.activation(hT[p][:, :, :], bank[0:IH, 4 + p, 0:2 * P].rearrange("p (c s) -> p c s", s=P),
                                         ACT.Copy).then_inc(shT_ready, 1)

                def step(s, p):
                    silu(s + 1, 1 - p)
                    copy_hT(s, p)
                silu(0, 0)
                paired(act, step, 0, NS - 2)
                step(NS - 2, 0)
                copy_hT(NS - 1, 1)

            @block.vector
            def _(dve):
                dve.sem_inc(sh_ready, DEPTH)
                dve.sem_inc(sy_out, DEPTH)

                def mul(s, p):
                    dve.wait_ge(ssg_ready, done(s))
                    dve.wait_ge(shT_done, freed(s))
                    nc.vector.tensor_tensor(hb[p][:, :], sg[p][:, :], bank[:, p, I:I2], ALU.mult).then_inc(sh_ready, 1)

                def keep(t, p):
                    dve.wait_ge(sy_done, done(t * SUB + SUB - 1))
                    xs = x_all[:, bass.ds(t * E, E)]
                    nc.vector.scalar_tensor_tensor(xs, bank[:, 6 + p, 0:E], sgate[:, bass.ds(t, 1)], xs, ALU.mult, ALU.add).then_inc(sy_out, 1)

                def tile(t, p, lag):
                    for j in range(SUB):
                        mul(t * SUB + j, j % 2)
                        if j == 2 and lag:
                            keep(t - 1, 1 - p)
                tile(0, 0, False)
                tile(1, 1, True)
                with dve.Fori(1, T // 2) as it:
                    for p in range(2):
                        tile(it * 2 + p, p, True)
                keep(T - 1, 1)

        w_in = [sem(f"w_in{b}") for b in range(WB)]
        v_in = [sem(f"v_in{b}") for b in range(WB)]
        r_in = [sem(f"r_in{b}") for b in range(WB)]
        y_st = [sem(f"y_st{b}") for b in range(WB)]
        bx_done, bx_ready, bgu_done, bsg_ready, bh_ready, bhT_done, bhT_ready, by_done, by_ready = (
            sem(n) for n in ("bx_done", "bx_ready", "bgu_done", "bsg_ready", "bh_ready", "bhT_done", "bhT_ready", "by_done", "by_ready"))
        def in_use(eng, first, step):
            last = eng.value_load(eob_row[0:1, P:P + 1], min_val=N * K4 // P // WB - 1, max_val=NB // WB - 1)
            with eng.Fori(first, NB // WB) as it:
                with eng.If(it <= last):
                    step(it, last)
            return last

        with nc.Block() as block:
            @block.sync
            def _(sp):
                def load(i, b, again):
                    e = sp.value_load(eob_row[0:1, bass.ds(i, 1)], min_val=0, max_val=NE - 1)
                    if again:
                        sp.wait_ge(bx_done, i - WB + 1 + DEPTH)
                    sp.dma_start(xg[b][:, :], slot_x[bass.ds(i * P, P), :]).then_inc(r_in[b], 16)
                    if again:
                        sp.wait_ge(bgu_done, i - WB + 1 + DEPTH)
                    sp.dma_start(wa[b][:, :], w13[bass.ds(e * P, P), :]).then_inc(w_in[b], 16)
                for b in range(WB):
                    load(b, b, False)

                def round_(it, _):
                    for b in range(WB):
                        load(it * WB + b, b, True)
                in_use(sp, 1, round_)

            @block.gpsimd
            def _(pool):
                def load(i, b):
                    e = pool.value_load(eob_row[0:1, bass.ds(i, 1)], min_val=0, max_val=NE - 1)
                    pool.dma_start(wb[b][:, :], w2[bass.ds(e * IH, IH), :]).then_inc(v_in[b], 16)

                def store(i, b):
                    pool.wait_ge(by_ready, done(i))
                    pool.dma_start(slot_y[bass.ds(i * P, P), :], yb[b][:, :]).then_inc(y_st[b], 16)
                for b in range(WB):
                    load(b, b)

                def round_(it, _):
                    for b in range(WB):
                        pool.wait_ge(by_done, (it - 1) * WB + b + 1 + DEPTH)
                        load(it * WB + b, b)
                        store((it - 1) * WB + b, b)
                last = in_use(pool, 1, round_)
                for b in range(WB):
                    store(last * WB + b, b)
                for b in range(WB):
                    pool.wait_ge(y_st[b], last * 16 + 16)

            @block.tensor
            def _(pe):
                pe.sem_inc(bx_done, DEPTH)
                pe.sem_inc(bgu_done, DEPTH)
                pe.sem_inc(bhT_done, DEPTH)
                pe.sem_inc(by_done, DEPTH)

                def rows(i, b, rounds):
                    pe.wait_ge(r_in[b], rounds * 16)
                    pe.wait_ge(bx_ready, freed(i))
                    for c in range(KC):
                        ins = nc.tensor.transpose(bank[:, 2 + b % 2, c * P:(c + 1) * P], xg[b][:, c * P:(c + 1) * P], ident)
                    ins.then_inc(bx_done, 1)

                def pe_up(i, b, rounds):
                    pe.wait_ge(w_in[b], rounds * 16)
                    pe.wait_ge(bx_ready, done(i))
                    pe.wait_ge(bh_ready, freed(i))
                    up(i, b % 2, xT[b % 2], wa[b], 0).then_inc(bgu_done, 1)

                def pe_turn(i, b):
                    pe.wait_ge(bh_ready, done(i))
                    pe.wait_ge(bhT_ready, freed(i))
                    turn(b % 2).then_inc(bhT_done, 1)

                def pe_down(i, b, rounds):
                    pe.wait_ge(v_in[b], rounds * 16)
                    pe.wait_ge(bhT_ready, done(i))
                    pe.wait_ge(by_ready, freed(i))
                    down(b % 2, 6 + b % 2, wb[b], 0, True, True).then_inc(by_done, 1)

                def body(it, lag, last):
                    for b in range(WB):
                        i = it * WB + b
                        if b < WB - 1:
                            rows(i + 1, b + 1, it + 1)
                        elif last is None:
                            rows(i + 1, 0, it + 2)
                        else:
                            with pe.If(it < last):
                                rows(i + 1, 0, it + 2)
                        pe_up(i, b, it + 1)
                        if lag or b >= 1:
                            pe_turn(i - 1, (b - 1) % WB)
                        if lag or b >= 2:
                            pe_down(i - 2, (b - 2) % WB, it + 1 if b >= 2 else it)
                rows(0, 0, 1)
                body(0, False, None)
                last = in_use(pe, 1, lambda it, last: body(it, True, last))
                pe_turn(last * WB + WB - 1, WB - 1)
                pe_down(last * WB + WB - 2, WB - 2, last + 1)
                pe_down(last * WB + WB - 1, WB - 1, last + 1)

            @block.scalar
            def _(act):
                act.sem_inc(bsg_ready, DEPTH)
                act.sem_inc(bhT_ready, DEPTH)
                act.sem_inc(by_ready, DEPTH)

                def silu(i, b):
                    act.wait_ge(bgu_done, done(i))
                    act.wait_ge(bh_ready, freed(i))
                    nc.scalar.activation(sg[b % 2][:, :], bank[:, b % 2, 0:I], ACT.Silu).then_inc(bsg_ready, 1)

                def copy_hT(i, b):
                    act.wait_ge(bhT_done, done(i))
                    act.wait_ge(by_done, freed(i))
                    nc.scalar.activation(hT[b % 2][:, :, :], bank[0:IH, 4 + b % 2, 0:2 * P].rearrange("p (c s) -> p c s", s=P),
                                         ACT.Copy).then_inc(bhT_ready, 1)

                def copy_y(i, b, rounds):
                    act.wait_ge(by_done, done(i))
                    if rounds is not None:
                        act.wait_ge(y_st[b], rounds * 16)
                    nc.scalar.activation(yb[b][:, :], bank[:, 6 + b % 2, 0:E], ACT.Copy).then_inc(by_ready, 1)

                def body(it, lag, again):
                    for b in range(WB):
                        i = it * WB + b
                        silu(i, b)
                        if lag or b >= 1:
                            copy_hT(i - 1, (b - 1) % WB)
                        if lag or b >= 2:
                            rounds = (it if b >= 2 else it - 1) if again or b >= 2 and lag else None
                            copy_y(i - 2, (b - 2) % WB, rounds)
                body(0, False, False)
                body(1, True, False)
                last = in_use(act, 2, lambda it, _: body(it, True, True))
                copy_hT(last * WB + WB - 1, WB - 1)
                copy_y(last * WB + WB - 2, WB - 2, last)
                copy_y(last * WB + WB - 1, WB - 1, last)

            @block.vector
            def _(dve):
                dve.sem_inc(bx_ready, DEPTH)
                dve.sem_inc(bh_ready, DEPTH)

                def copy_x(i, b):
                    dve.wait_ge(bx_done, done(i))
                    dve.wait_ge(bgu_done, freed(i))
                    nc.vector.tensor_copy(xT[b % 2][:, :, :], bank[:, 2 + b % 2, 0:E].rearrange("p (c s) -> p c s", s=P)).then_inc(bx_ready, 1)

                def mul(i, b):
                    dve.wait_ge(bsg_ready, done(i))
                    dve.wait_ge(bhT_done, freed(i))
                    nc.vector.tensor_tensor(hb[b % 2][:, :], sg[b % 2][:, :], bank[:, b % 2, I:I2], ALU.mult).then_inc(bh_ready, 1)

                def round_(it, last):
                    for b in range(WB):
                        i = it * WB + b
                        if b < WB - 1:
                            copy_x(i + 1, b + 1)
                        else:
                            with dve.If(it < last):
                                copy_x(i + 1, 0)
                        mul(i, b)
                copy_x(0, 0)
                in_use(dve, 0, round_)

        YB = 8
        yg = [b[:, i * E:(i + 1) * E] for b in (dd[2], dd[3]) for i in range(4)]
        yg_in = [sem(f"yg_in{b}") for b in range(YB)]
        added, s_out = sem("added"), sem("s_out")
        with nc.Block() as block:
            @block.gpsimd
            def _(pool):
                for c in range(T * K4):
                    if c >= YB:
                        pool.wait_ge(added, c - YB + 1)
                    pool.indirect_dma_start(yg[c % YB], None, slot_y[:, :],
                                            bass.IndirectOffsetOnAxis(slotu[:, c:c + 1], 0)).then_inc(yg_in[c % YB], 16)

            @block.vector
            def _(dve):
                for c in range(T * K4):
                    t = c // K4
                    dve.wait_ge(yg_in[c % YB], 16 * (c // YB + 1))
                    if c:
                        dve.wait_ge(added, c)
                    xs = x_all[:, t * E:(t + 1) * E]
                    nc.vector.scalar_tensor_tensor(xs, yg[c % YB], wk[:, c:c + 1], xs, ALU.mult, ALU.add).then_inc(added, 1)

            @block.sync
            def _(sp):
                for t in range(T):
                    sp.wait_ge(added, K4 * (t + 1))
                    sp.dma_start(out[t * P:(t + 1) * P, :], x_all[:, t * E:(t + 1) * E]).then_inc(s_out, 16)
                sp.wait_ge(s_out, 16 * T)


def kernel(x, ctx_2048, g_xattn, g_ffn, L0_xattn_Wi, L0_xattn_bi, L0_xattn_Wf, L0_xattn_bf, L0_xattn_ln_scale,
           L0_ffn_gate_w, L0_ffn_shared_gate_w, L0_ffn_w13, L0_ffn_w2, L0_ffn_se_gate_up_w, L0_ffn_se_down_w):
    import numpy as np
    import concourse.bacc as bacc
    from concourse.bass_utils import run_bass_kernel_spmd

    P, S, DH = 128, 64, 16
    row, col = np.arange(P)[:, None], np.arange(P)[None, :]
    same = row // S == col // S
    consts = np.concatenate([
        row == col,
        (row <= col) & same,
        row < col,
        (row // DH == np.arange(P // DH)[None, :]) * DH ** -0.5,
        np.where(row % S > np.arange(S)[None, :], -1.0e30, 0.0),
        np.arange(L0_ffn_w2.shape[0])[None, :] + 0 * row,
        row,
        P * np.arange(x.size // x.shape[-1] // P)[None, :] + 0 * row,
        row // S == np.arange(P // S)[None, :],
    ], axis=1).astype(np.float32)

    def swapped(a):
        return np.ascontiguousarray(np.swapaxes(a, -1, -2))

    def width_first(w):
        e, n, k = w.shape
        return swapped(w).reshape(e, k // P, P, n).transpose(0, 2, 1, 3).reshape(e * P, -1)

    def inner_first(w):
        e, k, n = w.shape
        return swapped(w).reshape(e, 2, n // 2, k).transpose(0, 2, 1, 3).reshape(e * n // 2, -1)

    I = L0_ffn_w2.shape[2]
    se_gu = L0_ffn_se_gate_up_w.reshape(2, -1, I, L0_ffn_se_gate_up_w.shape[1])
    se_d = L0_ffn_se_down_w

    arrays = {
        "x": np.ascontiguousarray(x).reshape(-1, x.shape[-1]),
        "ctx": np.ascontiguousarray(ctx_2048).reshape(-1, x.shape[-1]),
        "w_i": L0_xattn_Wi, "b_i": L0_xattn_bi, "w_f": L0_xattn_Wf, "b_f": L0_xattn_bf,
        "ln_scale": L0_xattn_ln_scale, "g_x": g_xattn, "g_f": g_ffn,
        "router_w": np.concatenate([swapped(L0_ffn_gate_w), swapped(L0_ffn_shared_gate_w)], axis=1),
        "w13": width_first(L0_ffn_w13), "w2": inner_first(L0_ffn_w2),
        "se_w13": width_first(np.concatenate([se_gu[0], se_gu[1]], axis=1)),
        "se_w2": inner_first(np.swapaxes(se_d.reshape(se_d.shape[0], -1, I), 0, 1)),
        "consts": consts,
    }
    nc = bacc.Bacc("TRN2", target_bir_lowering=False, num_devices=1)
    arrays = {k: np.ascontiguousarray(v) for k, v in arrays.items()}
    aps = {k: nc.dram_tensor(f"in_{k}", v.shape, mybir.dt.from_np(v.dtype), kind="ExternalInput").ap() for k, v in arrays.items()}
    out = nc.dram_tensor("out_0", arrays["x"].shape, mybir.dt.float32, kind="ExternalOutput").ap()
    flamingo_layer(nc, out=out, **aps)
    r = run_bass_kernel_spmd(nc, [{f"in_{k}": v for k, v in arrays.items()}], core_ids=[0])
    return r.results[0]["out_0"].reshape(x.shape)
```

```python
import concourse.bass as bass
from concourse import mybir
from contextlib import ExitStack


class SharedSems:

    def __init__(self, sem):
        self.xs_in = [sem(f"xs_in{p}") for p in range(2)]
        self.sgu_done = sem("sgu_done")
        self.ssg_ready = sem("ssg_ready")
        self.sh_ready = sem("sh_ready")
        self.shT_done = sem("shT_done")
        self.shT_ready = sem("shT_ready")
        self.sy_done = sem("sy_done")
        self.sy_out = sem("sy_out")


def flamingo_layer(nc, x, ctx, w_i, b_i, w_f, b_f, ln_scale, g_x, g_f,
                   router_w, w13, w2, se_w13, se_w2, consts, out):
    fp32, bf16, i32, u32 = mybir.dt.float32, mybir.dt.bfloat16, mybir.dt.int32, mybir.dt.uint32
    ALU, ACT, AX = mybir.AluOpType, mybir.ActivationFunctionType, mybir.AxisListType
    P = 128
    N, E = x.shape
    S = 64
    T = N // P
    NH = w_i.shape[1]
    DH = E // NH
    KC = E // P
    TG = P // NH
    G = T // TG
    NG = 2 * NH
    VW = DH + 1
    PAD = S // 2
    CT = 4
    DEPTH = 2
    NEG = -3.0e38
    NR = router_w.shape[1]
    NE = NR - 1
    K4 = 4
    I2 = w13.shape[1] // KC
    I = I2 // 2
    IH = I // 2
    SUB = se_w13.shape[0] // P
    WB = 4
    NB = (N * K4 - NE) // P + NE
    NB += -NB % WB

    def done(t):
        return t + 1 + DEPTH

    def freed(t):
        return t + 1

    g_dram = nc.dram_tensor("g_dram", (2 * T * NH, S), fp32).ap()
    slot_x = nc.dram_tensor("slot_x", (NB * P, E), fp32).ap()
    slot_y = nc.dram_tensor("slot_y", (NB * P, E), fp32).ap()

    with ExitStack() as stack:
        def sb(name, shape, dt=fp32):
            return stack.enter_context(nc.sbuf_tensor(name, shape, dt))

        def sem(name):
            return stack.enter_context(nc.semaphore(name))

        bank = stack.enter_context(nc.psum_tensor("bank", [P, 8, 512], fp32))

        cst = sb("cst", [P, consts.shape[1]])
        at = 0
        ident, at = cst[:, at:at + P], at + P
        tri_seq, at = cst[:, at:at + P], at + P
        tri_all, at = cst[:, at:at + P], at + P
        HC = P // DH
        head_mask, at = cst[:, at:at + HC], at + HC
        neg_mask, at = cst[:, at:at + S], at + S

        iota_e, at = cst[:, at:at + NE], at + NE
        iota_p, at = cst[:, at:at + 1], at + 1
        fills, at = cst[:, at:at + T], at + T
        seq_mask, at = cst[:, at:at + 2], at + 2

        wi_sb = sb("wi_sb", [P, 3 * KC, NG])
        wctx = sb("wctx", [P, KC, NG])
        bias_bc = sb("bias_bc", [P, NG])
        lnsc = sb("lnsc", [P, E])
        gx = sb("gx", [P, 1])
        x_all = sb("x_all", [P, T * E])
        ctx_all = sb("ctx_all", [P, T * E])
        stats = sb("stats", [P, T, 6])
        mv = sb("mv", [P, T * 2])
        rstd = sb("rstd", [P, T])
        gates = sb("gates", [P, T * NG])
        s_all = sb("s_all", [P, T * NH * S])
        qn = [sb(f"qn{p}", [P, E]) for p in range(2)]
        ct = [sb(f"ct{p}", [P, E]) for p in range(2)]
        qkT = [sb(f"qkT{p}", [P, 2 * KC, P]) for p in range(2)]
        qbd_all = sb("qbd_all", [P, 2 * KC * HC * P])
        qbd = [qbd_all[:, p * KC * HC * P:(p + 1) * KC * HC * P].rearrange("p (c h s) -> p c h s", c=KC, h=HC) for p in range(2)]
        xT_all = qbd_all
        lf = sb("lf", [P, T * NH])
        fcum = sb("fcum", [P, T * NH])
        a_all = sb("a_all", [P, T * NH])
        m_all = sb("m_all", [P, T * NH])
        scan = [sb(f"scan{p}", [P, 2 * G, PAD + S]) for p in range(2)]
        gcum = sb("gcum", [P, 2 * G, S])
        gb = [sb(f"gb{p}", [P, NH * S]) for p in range(2)]
        dd = [sb(f"dd{b}", [P, NH * S]) for b in range(4)]
        VB = NH // 2 * 2 * 2 * VW
        vbd = [qbd_all[:, d * VB:(d + 1) * VB].rearrange("p (j b h d) -> p j b h d", j=NH // 2, b=2, h=2) for d in range(4)]
        h_all = sb("h_all", [P, T * NH * VW])
        hh = sb("hh", [P, CT * NH * DH])
        hq = sb("hq", [P, CT * NH * DH])
        hs = sb("hs", [P, 2, CT * NH])

        NZ = 31
        ZW = NB * E // NZ
        zeros = sb("zeros", [P, ZW])
        ones_b = sb("ones_b", [P, P], bf16)
        tri_b = sb("tri_b", [P, P], bf16)
        rw = sb("rw", [P, KC, NR])
        gf = sb("gf", [P, 1])
        used = {}

        def within(big, n, rows=P):
            lo = used.get(big.name, 0)
            used[big.name] = lo + n
            assert lo + n <= big.shape[1]
            return big[0:rows, lo:lo + n]

        def old(n):
            return within(s_all, n)
        xn_all = old(T * E)
        lg_all = old(T * NR)
        prob = old(T * NE)
        pos = old(T * NE)
        tcum = [old(8 * NE + T * NE) for _ in range(2)]
        oh = [within(b, T * NE // 2).bitcast(bf16) for b in (gb[1], gb[1], dd[0], dd[0])]
        top = sb("top", [P, T, 8])
        topi = sb("topi", [P, T, 8], u32)
        topf = sb("topf", [P, T, K4])
        wk = sb("wk", [P, T * K4])
        zsum = sb("zsum", [P, T])
        sgate = sb("sgate", [P, T])
        cnt = sb("cnt", [P, NE])
        cmp = within(gb[0], NE * T).rearrange("p (n t) -> p n t", t=T)
        nblk = sb("nblk", [P, NE])
        EP = 32
        ecum = [sb(f"ecum{p}", [P, EP + NE]) for p in range(2)]
        slotf = sb("slotf", [P, T, K4])
        slotu = sb("slotu", [P, T * K4], u32)
        eob = sb("eob", [P, 1])
        last_f = sb("last_f", [P, 1])
        eob_row = sb("eob_row", [1, P + 1], i32)
        se13 = old(SUB * KC * I2).rearrange("p (j n) -> p j n", j=SUB)
        se2 = within(s_all, SUB * 2 * E, IH).rearrange("p (j n) -> p j n", j=SUB)
        wa = [within(ctx_all, KC * I2) for _ in range(WB)]
        wb = [within(h_all, 2 * E, IH) for _ in range(WB)]
        xg = [within(h_all, E) for _ in range(WB)]
        xT = [within(hq, E).rearrange("p (c s) -> p c s", s=P) for _ in range(2)]
        sg = [within(dd[1], I) for _ in range(2)]
        hb = [within(dd[1], I) for _ in range(2)]
        hT = [within(hh, 2 * P, IH).rearrange("p (c s) -> p c s", s=P) for _ in range(2)]
        yb = [within(h_all, E) for _ in range(WB)]
        TA, TB, TC = 4, 6, 6
        assert TA + TB + TC == T
        ysh = within(ctx_all, TA * E)
        ub = [within(ct[p], I) for p in range(2)]

        s_x = [sem(f"s_x{h}") for h in range(4)]
        s_w, s_c, s_v = sem("s_w"), sem("s_c"), sem("s_v")
        pool_norm, dve_norm = sem("pool_norm"), sem("dve_norm")
        dve_step, act_step = sem("dve_step"), sem("act_step")
        zeros_ready, cleared, s_se, s_r = sem("zeros_ready"), sem("cleared"), sem("s_se"), sem("s_r")
        ctx_in = [sem(f"ctx_in{p}") for p in range(2)]
        rstd_in, rstd_sq = sem("rstd_in"), sem("rstd_sq")
        wctx_ready = sem("wctx_ready")
        qn_ready, tr_done, qkT_ready, qbd_ready = sem("qn_ready"), sem("tr_done"), sem("qkT_ready"), sem("qbd_ready")
        gates_done, scores_done, qbd1_ready = sem("gates_done"), sem("scores_done"), sem("qbd1_ready")
        gates_out, scores_out = sem("gates_out"), sem("scores_out")

        steps = {}

        def after(eng, step_sem, ins):
            steps[step_sem.name] = steps.get(step_sem.name, 0) + 1
            ins.then_inc(step_sem, 1)
            eng.wait_ge(step_sem, steps[step_sem.name])

        def paired(eng, step, first=0, last=T):
            with eng.Fori(first // 2, last // 2) as it:
                for p in range(2):
                    step(it * 2 + p, p)

        with nc.Block() as block:
            @block.sync
            def _(sp):
                sp.dma_start(cst[:, :], consts).then_inc(s_c, 16)
                xr = x.rearrange("(t p) e -> p t e", p=P)
                cr = ctx.rearrange("(t p) e -> p t e", p=P)

                def load_ctx(t, p, again=True):
                    if again:
                        sp.wait_ge(tr_done, freed(t))
                    sp.dma_start(ct[p][:, :], ctx[bass.ds(t * P, P), :]).then_inc(ctx_in[p], 16)
                for h in range(4):
                    r = slice(h * T // 4, (h + 1) * T // 4)
                    c = slice(h * T * E // 4, (h + 1) * T * E // 4)
                    sp.dma_start(x_all[:, c].rearrange("p (t e) -> p t e", e=E), xr[:, r, :]).then_inc(s_x[h], 16)
                load_ctx(0, 0, False)
                load_ctx(1, 1, False)
                paired(sp, load_ctx, 2)
                for h in range(4):
                    r = slice(h * T // 4, (h + 1) * T // 4)
                    c = slice(h * T * E // 4, (h + 1) * T * E // 4)
                    sp.dma_start(ctx_all[:, c].rearrange("p (t e) -> p t e", e=E), cr[:, r, :]).then_inc(s_v, 16)

            @block.gpsimd
            def _(pool):
                pool.memset(zeros[:, :], 0.0).then_inc(zeros_ready, 1)
                pool.memset(ones_b[:, :], 1.0)
                pool.memset(scan[0][:, :, 0:PAD], NEG)
                pool.memset(scan[1][:, :, 0:PAD], NEG)
                pool.sem_inc(qbd1_ready, DEPTH)

                def spread(t, p):
                    pool.wait_ge(qkT_ready, done(t))
                    pool.wait_ge(scores_done, freed(t))
                    pool.tensor_tensor(qbd[p][:, 1, :, :], qkT[p][:, 1:2, :].to_broadcast([P, HC, P]),
                                       head_mask.unsqueeze(2).to_broadcast([P, HC, P]), ALU.mult).then_inc(qbd1_ready, 1)
                pool.wait_ge(s_c, 16)
                paired(pool, spread)

            @block.vector
            def _(dve):
                dve.sem_inc(qn_ready, DEPTH)
                dve.sem_inc(qbd_ready, DEPTH)
                for t in range(T):
                    if t % (T // 4) == 0:
                        dve.wait_ge(s_x[t // (T // 4)], 16)
                    ins = nc.vector.bn_stats(out=stats[:, t, :], in_=x_all[:, t * E:(t + 1) * E])
                after(dve, dve_step, ins)
                for t in range(T):
                    ins = nc.vector.bn_aggr(out=mv[:, 2 * t:2 * t + 2], in_=stats[:, t, :])
                after(dve, dve_step, ins)
                var = mv[:, :].rearrange("p (t c) -> p t c", c=2)[:, :, 1]
                nc.vector.tensor_scalar(rstd[:, :], var, 1.0e-5, None, ALU.add).then_inc(rstd_in, 1)
                dve.wait_ge(s_w, 16 * 6)
                nc.vector.tensor_tensor(wctx[:, :, :], wi_sb[:, KC:2 * KC, :], wi_sb[:, 2 * KC:3 * KC, :], ALU.add).then_inc(wctx_ready, 1)
                dve.wait_ge(rstd_sq, 1)
                after(dve, dve_step, nc.vector.reciprocal(rstd[:, :], rstd[:, :]))

                def norm(t, p):
                    dve.wait_ge(tr_done, freed(t))
                    nc.vector.tensor_scalar(qn[p][:, :], x_all[:, bass.ds(t * E, E)], mv[:, bass.ds(t * 2, 1)],
                                            rstd[:, bass.ds(t, 1)], ALU.subtract, ALU.mult).then_inc(qn_ready, 1)

                def spread(t, p):
                    dve.wait_ge(qkT_ready, done(t))
                    dve.wait_ge(scores_done, freed(t))
                    nc.vector.tensor_tensor(qbd[p][:, 0, :, :], qkT[p][:, 0:1, :].to_broadcast([P, HC, P]),
                                            head_mask.unsqueeze(2).to_broadcast([P, HC, P]), ALU.mult).then_inc(qbd_ready, 1)

                def step(t, p):
                    norm(t + 1, 1 - p)
                    spread(t, p)
                dve.wait_ge(s_c, 16)
                norm(0, 0)
                paired(dve, step, 0, T - 2)
                step(T - 2, 0)
                spread(T - 1, 1)

            @block.scalar
            def _(act):
                act.sem_inc(qkT_ready, DEPTH)
                act.sem_inc(gates_out, DEPTH)
                act.sem_inc(scores_out, DEPTH)
                act.dma_start(wi_sb[:, :, 0:NH], w_i.rearrange("(c p) h -> p c h", p=P)).then_inc(s_w, 16)
                act.dma_start(wi_sb[:, :, NH:NG], w_f.rearrange("(c p) h -> p c h", p=P)).then_inc(s_w, 16)
                act.dma_start(bias_bc[:, 0:NH], b_i.partition_broadcast(P)).then_inc(s_w, 16)
                act.dma_start(bias_bc[:, NH:NG], b_f.partition_broadcast(P)).then_inc(s_w, 16)
                act.dma_start(lnsc[:, :], ln_scale.partition_broadcast(P)).then_inc(s_w, 16)
                act.dma_start(gx[:, :], g_x.partition_broadcast(P)).then_inc(s_w, 16)
                act.dma_start(gf[:, :], g_f.partition_broadcast(P)).then_inc(s_r, 16)
                act.dma_start(rw[:, :, :], router_w.rearrange("(c p) n -> p c n", p=P)).then_inc(s_r, 16)
                act.wait_ge(rstd_in, 1)
                nc.scalar.activation(rstd[:, :], rstd[:, :], ACT.Sqrt).then_inc(rstd_sq, 1)

                def copy_qkT(t, p):
                    act.wait_ge(tr_done, done(t))
                    act.wait_ge(scores_done, freed(t))
                    nc.scalar.activation(qkT[p][:, :, :], bank[:, 4 + p, :].rearrange("p (c s) -> p c s", s=P),
                                         ACT.Copy).then_inc(qkT_ready, 1)

                def copy_out(t, p):
                    act.wait_ge(gates_done, done(t))
                    nc.scalar.activation(gates[:, bass.ds(t * NG, NG)], bank[:, 6 + p, 0:NG], ACT.Copy).then_inc(gates_out, 1)
                    act.wait_ge(scores_done, done(t))
                    dst = s_all[:, bass.ds(t * NH * S, NH * S)].rearrange("p (c m) -> p c m", c=KC)
                    nc.scalar.activation(dst, bank[:, 2 * p:2 * p + 2, :], ACT.Copy).then_inc(scores_out, 1)

                def step(t, p):
                    copy_qkT(t + 2, p)
                    copy_out(t, p)
                copy_qkT(0, 0)
                copy_qkT(1, 1)
                paired(act, step, 0, T - 2)
                copy_out(T - 2, 0)
                copy_out(T - 1, 1)

            @block.tensor
            def _(pe):
                pe.sem_inc(tr_done, DEPTH)
                pe.sem_inc(gates_done, DEPTH)
                pe.sem_inc(scores_done, DEPTH)
                pe.wait_ge(s_c, 16)

                def transposes(t, p, rounds):
                    pe.wait_ge(qn_ready, done(t))
                    pe.wait_ge(ctx_in[p], rounds * 16)
                    pe.wait_ge(qkT_ready, freed(t))
                    for k, src in enumerate((qn[p], ct[p])):
                        for c in range(KC):
                            ins = nc.tensor.transpose(bank[:, 4 + p, (2 * k + c) * P:(2 * k + c + 1) * P],
                                                      src[:, c * P:(c + 1) * P], ident)
                    ins.then_inc(tr_done, 1)

                def products(t, p):
                    pe.wait_ge(qkT_ready, done(t))
                    pe.wait_ge(gates_out, freed(t))
                    for k in range(2 * KC):
                        w = wi_sb[:, k, :] if k < KC else wctx[:, k - KC, :]
                        ins = nc.tensor.matmul(bank[:, 6 + p, 0:NG], qkT[p][:, k, :], w, start=(k == 0), stop=(k == 2 * KC - 1))
                    ins.then_inc(gates_done, 1)
                    pe.wait_ge(qbd_ready, done(t))
                    pe.wait_ge(scores_out, freed(t))
                    for c in range(KC):
                        if c == 1:
                            pe.wait_ge(qbd1_ready, done(t))
                        for b in range(2):
                            r = slice(b * S, (b + 1) * S)
                            ins = nc.tensor.matmul(bank[r, 2 * p + c, :], qkT[p][:, KC + c, r], qbd[p][:, c, :, r],
                                                   start=True, stop=True)
                    ins.then_inc(scores_done, 1)

                transposes(0, 0, 1)
                pe.wait_ge(wctx_ready, 1)
                with pe.Fori(0, T // 2 - 1) as it:
                    transposes(it * 2 + 1, 1, it + 1)
                    products(it * 2, 0)
                    transposes(it * 2 + 2, 0, it + 2)
                    products(it * 2 + 1, 1)
                transposes(T - 1, 1, T // 2)
                products(T - 2, 0)
                products(T - 1, 1)

        gates3 = gates[:, :].rearrange("p (t g) -> p t g", g=NG)

        def th(v):
            return v.rearrange("p (t h) -> p t h", h=NH)

        z_ready, l_ready, lf_ready, f_done, a_ready, aT_done, g_ready, gT_done, g_out, m_ready, em_ready = (
            sem(n) for n in ("z_ready", "l_ready", "lf_ready", "f_done", "a_ready", "aT_done", "g_ready", "gT_done",
                             "g_out", "m_ready", "em_ready"))
        sc = hq[:, 0:T * NH]
        with nc.Block() as block:
            @block.vector
            def _(dve):
                dve.wait_ge(s_w, 16 * 6)
                after(dve, dve_step, nc.vector.tensor_tensor(gates3, gates3, bias_bc[:, :].unsqueeze(1).to_broadcast([P, T, NG]), ALU.add))
                f = gates3[:, :, NH:NG]
                nc.vector.scalar_tensor_tensor(th(sc), f, -1.0, f, ALU.mult, ALU.min).then_inc(z_ready, 1)
                dve.wait_ge(l_ready, 1)
                nc.vector.scalar_tensor_tensor(th(lf[:, :]), f, 0.0, th(sc), ALU.min, ALU.subtract).then_inc(lf_ready, 1)
                dve.wait_ge(f_done, 1)
                nc.vector.tensor_tensor(th(a_all[:, :]), gates3[:, :, 0:NH], th(bank[:, 0, 0:T * NH]), ALU.subtract).then_inc(a_ready, 1)
                nc.vector.tensor_copy(fcum[:, :], bank[:, 0, 0:T * NH])
                dve.wait_ge(aT_done, 1)
                after(dve, dve_step, nc.vector.tensor_copy(scan[0][:, :, PAD:PAD + S], bank[:, 1, 0:2 * G * S].rearrange("p (g s) -> p g s", s=S)))
                k, sh = 0, 1
                while sh < S:
                    to = scan[1 - k][:, :, PAD:PAD + S] if 2 * sh < S else gcum[:, :, :]
                    ins = nc.vector.tensor_tensor(to, scan[k][:, :, PAD:PAD + S],
                                                  scan[k][:, :, PAD - sh:PAD + S - sh], ALU.max)
                    k, sh = 1 - k, 2 * sh
                    if sh < S:
                        after(dve, dve_step, ins)
                ins.then_inc(g_ready, 1)
                dve.wait_ge(gT_done, 1)
                nc.vector.tensor_tensor(m_all[:, :], fcum[:, :], bank[:, 2, 0:T * NH], ALU.add).then_inc(m_ready, 1)

            @block.scalar
            def _(act):
                act.wait_ge(z_ready, 1)
                after(act, act_step, nc.scalar.activation(sc, sc, ACT.Exp))
                nc.scalar.activation(sc, sc, ACT.Ln, bias=1.0).then_inc(l_ready, 1)
                act.wait_ge(m_ready, 1)
                nc.scalar.activation(m_all[:, :], m_all[:, :], ACT.Exp, scale=-1.0).then_inc(em_ready, 1)
                nc.scalar.activation(gx[:, :], gx[:, :], ACT.Tanh)

            @block.tensor
            def _(pe):
                pe.wait_ge(lf_ready, 1)
                nc.tensor.matmul(bank[:, 0, 0:T * NH], tri_seq, lf[:, :], start=True, stop=True).then_inc(f_done, 1)
                pe.wait_ge(a_ready, 1)
                for g in range(G):
                    ins = nc.tensor.transpose(bank[:, 1, g * P:(g + 1) * P], a_all[:, g * P:(g + 1) * P], ident)
                ins.then_inc(aT_done, 1)
                pe.wait_ge(g_ready, 1)
                for g in range(G):
                    ins = nc.tensor.transpose(bank[:, 2, g * P:(g + 1) * P], gcum[:, 2 * g:2 * g + 2, :].rearrange("p b s -> p (b s)"), ident)
                ins.then_inc(gT_done, 1)

            @block.sync
            def _(sp):
                sp.wait_ge(g_ready, 1)
                for b in range(2):
                    sp.dma_start(g_dram.rearrange("(b g p) s -> p b g s", b=2, g=G)[:, b, :, :],
                                 gcum[:, :, :].rearrange("p (g b) s -> p g b s", b=2)[:, :, b, :]).then_inc(g_out, 16)
                sp.wait_ge(g_out, 16 * 2)

        gb_in = [sem(f"gb_in{p}") for p in range(2)]
        d_ready, dm_ready, e_ready, c_ready, vt_ready, h_done, h_out = (
            sem(n) for n in ("d_ready", "dm_ready", "e_ready", "c_ready", "vt_ready", "h_done", "h_out"))
        hc_ready, sq_ready, var_ready, sd_ready, hn_ready, x_ready = (
            sem(n) for n in ("hc_ready", "sq_ready", "var_ready", "sd_ready", "hn_ready", "x_ready"))
        lnsc_ready, ones_ready = sem("lnsc_ready"), sem("ones_ready")
        NCH = CT * NH
        NQ = T // CT
        DB = len(dd)
        hh3 = hh[:, :].rearrange("p (h d) -> p h d", d=DH)
        hq3 = hq[:, :].rearrange("p (h d) -> p h d", d=DH)
        r0, r1 = hs[:, 0, :], hs[:, 1, :]

        def hs3(v):
            return v.rearrange("p (h s) -> p h s", s=S)

        with nc.Block() as block:
            @block.sync
            def _(sp):
                g_rows = g_dram.rearrange("(r h) s -> r (h s)", h=NH)
                clear = slot_x.rearrange("(p n) e -> p (n e)", p=P)

                def load_g(t, p):
                    sp.wait_ge(d_ready, freed(t))
                    for b in range(2):
                        sp.dma_start(gb[p][b * S:(b + 1) * S, :], g_rows[bass.ds(t + b * T, 1), :].to_broadcast([S, NH * S])).then_inc(gb_in[p], 16)
                with sp.Fori(0, T // 2) as it:
                    for p in range(2):
                        load_g(it * 2 + p, p)
                        sp.dma_start(clear[:, bass.ds((it * 2 + p) * ZW, ZW)], zeros[:, :]).then_inc(cleared, 16)
                for z in range(T, NZ):
                    sp.dma_start(clear[:, z * ZW:(z + 1) * ZW], zeros[:, :]).then_inc(cleared, 16)

            @block.gpsimd
            def _(pool):
                pool.sem_inc(d_ready, DEPTH)
                pool.sem_inc(x_ready, 1)
                for d in range(DB):
                    for b in range(2):
                        ins = pool.tensor_copy(vbd[d][:, :, b, :, DH], seq_mask[:, b:b + 1].unsqueeze(2).to_broadcast([P, NH // 2, 2]))
                ins.then_inc(ones_ready, 1)

                def subtract(t, p, d, rounds, first):
                    pool.wait_ge(gb_in[p], rounds * 32)
                    if not first:
                        pool.wait_ge(h_done, t - DB + 1 + DEPTH)
                    pool.tensor_tensor(hs3(dd[d][:, :]), a_all[:, bass.ds(t * NH, NH)].unsqueeze(2).to_broadcast([P, NH, S]),
                                       hs3(gb[p][:, :]), ALU.subtract).then_inc(d_ready, 1)

                def scale(c):
                    pool.wait_ge(hn_ready, c + 1)
                    pool.tensor_tensor(hq[:, :].rearrange("p (t e) -> p t e", e=E), hq[:, :].rearrange("p (t e) -> p t e", e=E),
                                       lnsc[:, :].unsqueeze(1).to_broadcast([P, CT, E]), ALU.mult).then_inc(pool_norm, 1)

                def residual(c):
                    pool.wait_ge(pool_norm, c + 1)
                    xs = x_all[:, bass.ds(c * (CT * E), CT * E)]
                    pool.tensor_tensor(xs, xs, hq[:, :], ALU.add).then_inc(x_ready, 1)

                def body(it, before, before2):
                    for u in range(CT):
                        subtract(it * CT + u, u % 2, u, it * 2 + u // 2 + 1, not before)
                        if before2 and u == 1:
                            scale(it - 2)
                        if before2 and u == 2:
                            residual(it - 2)
                body(0, False, False)
                body(1, True, False)
                pool.wait_ge(lnsc_ready, 1)
                with pool.Fori(2, NQ) as it:
                    body(it, True, True)
                for c in (NQ - 2, NQ - 1):
                    scale(c)
                    residual(c)

            @block.vector
            def _(dve):
                dve.sem_inc(dm_ready, DEPTH)
                dve.sem_inc(c_ready, DEPTH)
                nc.vector.tensor_scalar(lnsc[:, :], lnsc[:, :], gx[:, 0:1], None, ALU.mult).then_inc(lnsc_ready, 1)

                def clip(t, d):
                    dve.wait_ge(d_ready, done(t))
                    nc.vector.scalar_tensor_tensor(hs3(dd[d][:, :]), hs3(dd[d][:, :]), 0.0,
                                                   neg_mask.unsqueeze(1).to_broadcast([P, NH, S]), ALU.min, ALU.add).then_inc(dm_ready, 1)

                def weigh(t, d):
                    dve.wait_ge(e_ready, done(t))
                    nc.vector.tensor_tensor(dd[d][:, :], dd[d][:, :], s_all[:, bass.ds(t * NH * S, NH * S)], ALU.mult).then_inc(c_ready, 1)

                PER = 8

                def link(c, k, ins):
                    ins.then_inc(dve_norm, 1)
                    dve.wait_ge(dve_norm, c * PER + k)

                def norm(c, part):
                    if part == 0:
                        h4 = h_all[:, bass.ds(c * (NCH * VW), NCH * VW)].rearrange("p (h d) -> p h d", d=VW)
                        dve.wait_ge(h_out, c * CT + CT + DEPTH)
                        link(c, 1, nc.vector.scalar_tensor_tensor(r0, h4[:, :, DH], -1.0, h4[:, :, DH], ALU.mult, ALU.max))
                        link(c, 2, nc.vector.tensor_tensor(r0, r0, m_all[:, bass.ds(c * NCH, NCH)], ALU.max))
                        link(c, 3, nc.vector.tensor_scalar(r0, r0, 1.0e-6, None, ALU.add))
                        link(c, 4, nc.vector.reciprocal(r0, r0))
                        link(c, 5, nc.vector.tensor_tensor(hh3, h4[:, :, 0:DH], r0.unsqueeze(2).to_broadcast([P, NCH, DH]), ALU.mult))
                    if part == 1:
                        link(c, 6, nc.vector.tensor_reduce(r1, hh3, AX.X, ALU.add))
                        nc.vector.scalar_tensor_tensor(hh3, r1.unsqueeze(2).to_broadcast([P, NCH, DH]), -1.0 / DH, hh3, ALU.mult, ALU.add).then_inc(hc_ready, 1)
                    if part == 2:
                        dve.wait_ge(sq_ready, c + 1)
                        link(c, 7, nc.vector.tensor_reduce(r1, hq3, AX.X, ALU.add))
                        nc.vector.tensor_scalar(r1, r1, 1.0 / DH, 1.0e-6, ALU.mult, ALU.add).then_inc(var_ready, 1)
                    if part == 3:
                        dve.wait_ge(sd_ready, c + 1)
                        link(c, 8, nc.vector.reciprocal(r1, r1))
                        nc.vector.tensor_tensor(hq3, hh3, r1.unsqueeze(2).to_broadcast([P, NCH, DH]), ALU.mult).then_inc(hn_ready, 1)

                def body(it, before, before2, last=False):
                    for u in range(CT):
                        weigh(it * CT + u, u)
                        if not (last and u == CT - 1):
                            clip(it * CT + u + 1, (u + 1) % CT)
                        if before2 and u == 0:
                            norm(it - 2, 3)
                        if before and u > 0:
                            norm(it - 1, u - 1)
                clip(0, 0)
                body(0, False, False)
                body(1, True, False)
                with dve.Fori(2, NQ - 1) as it:
                    body(it, True, True)
                body(NQ - 1, True, True, True)
                norm(NQ - 2, 3)
                for part in range(4):
                    norm(NQ - 1, part)
                dve.wait_ge(x_ready, NQ)
                for t in range(T - CT):
                    nc.vector.bn_stats(out=stats[:, t, :], in_=x_all[:, t * E:(t + 1) * E])

            @block.scalar
            def _(act):
                act.sem_inc(e_ready, DEPTH)
                act.sem_inc(h_out, DEPTH)

                def expo(t, d):
                    act.wait_ge(dm_ready, done(t))
                    nc.scalar.activation(dd[d][:, :], dd[d][:, :], ACT.Exp).then_inc(e_ready, 1)

                def spread(t, d, first=False):
                    if not first:
                        act.wait_ge(h_done, t - DB + 1 + DEPTH)
                    for b in range(2):
                        ins = nc.scalar.activation(vbd[d][:, :, b, :, 0:DH],
                                                   ctx_all[:, bass.ds(t * E, E)].rearrange("p (j h d) -> p j h d", h=2, d=DH),
                                                   ACT.Copy, scale=seq_mask[:, b:b + 1])
                    ins.then_inc(vt_ready, 1)

                def copy_h(t, p):
                    act.wait_ge(h_done, done(t))
                    for b in range(2):
                        dst = h_all[b * S:(b + 1) * S, bass.ds(t * NH * VW, NH * VW)].rearrange("p (k j h d) -> p k j h d", k=2, h=2, d=VW)
                        for h in range(2):
                            src = bank[h * S:(h + 1) * S, 2 * p:2 * p + 2, 0:NH * VW].rearrange("p k (j b h d) -> p k j b h d", b=2, h=2, d=VW)
                            ins = nc.scalar.activation(dst[:, :, :, h, :], src[:, :, :, b, h, :], ACT.Copy)
                    ins.then_inc(h_out, 1)

                def square(c):
                    act.wait_ge(hc_ready, c + 1)
                    act.wait_ge(x_ready, c + 1)
                    nc.scalar.activation(hq[:, :], hh[:, :], ACT.Square).then_inc(sq_ready, 1)

                def root(c):
                    act.wait_ge(var_ready, c + 1)
                    nc.scalar.activation(r1, r1, ACT.Sqrt).then_inc(sd_ready, 1)

                def body(it, before, last=False):
                    for u in range(CT):
                        if not (last and u == CT - 1):
                            expo(it * CT + u + 1, (u + 1) % CT)
                            spread(it * CT + u + 1, (u + 1) % CT, not before and u + 1 < CT)
                        copy_h(it * CT + u, u % 2)
                        if before and u == CT - 2:
                            square(it - 1)
                        if before and u == CT - 1:
                            root(it - 1)
                act.sem_inc(vt_ready, DEPTH)
                act.wait_ge(s_v, 16 * 4)
                act.wait_ge(ones_ready, 1)
                spread(0, 0, True)
                expo(0, 0)
                body(0, False)
                with act.Fori(1, NQ - 1) as it:
                    body(it, True)
                body(NQ - 1, True, True)
                square(NQ - 1)
                root(NQ - 1)

            @block.tensor
            def _(pe):
                pe.sem_inc(h_done, DEPTH)
                with pe.Fori(0, NQ) as it:
                    for u in range(CT):
                        t, p = it * CT + u, u % 2
                        pe.wait_ge(c_ready, done(t))
                        pe.wait_ge(vt_ready, done(t))
                        pe.wait_ge(h_out, freed(t))
                        for j in range(NH // 2):
                            at = (j % 4) * 4 * VW
                            ins = nc.tensor.matmul(bank[:, 2 * p + j // 4, at:at + 4 * VW], dd[u][:, j * P:(j + 1) * P],
                                                   vbd[u][:, j, :, :, :].rearrange("p b h d -> p (b h d)"), start=True, stop=True)
                        ins.then_inc(h_done, 1)

        xn_ready, xT_done, xT_copied, lg_done, lg_out, xn_kept, r5_in, r5_sq = (
            sem(n) for n in ("xn_ready", "xT_done", "xT_copied", "lg_done", "lg_out", "xn_kept", "r5_in", "r5_sq"))
        xT_st = [sem(f"xT_st{p}") for p in range(2)]
        with nc.Block() as block:
            @block.vector
            def _(dve):
                dve.sem_inc(xn_ready, DEPTH)
                for t in range(T - CT, T):
                    ins = nc.vector.bn_stats(out=stats[:, t, :], in_=x_all[:, t * E:(t + 1) * E])
                after(dve, dve_step, ins)
                for t in range(T):
                    ins = nc.vector.bn_aggr(out=mv[:, 2 * t:2 * t + 2], in_=stats[:, t, :])
                after(dve, dve_step, ins)
                var = mv[:, :].rearrange("p (t c) -> p t c", c=2)[:, :, 1]
                nc.vector.tensor_scalar(rstd[:, :], var, 1.0e-5, None, ALU.add).then_inc(r5_in, 1)
                nc.vector.tensor_copy(tri_b[:, :], tri_all)
                dve.wait_ge(r5_sq, 1)
                after(dve, dve_step, nc.vector.reciprocal(rstd[:, :], rstd[:, :]))

                def norm(t, p):
                    dve.wait_ge(xT_done, freed(t))
                    dve.wait_ge(xn_kept, freed(t))
                    nc.vector.tensor_scalar(qn[p][:, :], x_all[:, bass.ds(t * E, E)], mv[:, bass.ds(t * 2, 1)],
                                            rstd[:, bass.ds(t, 1)], ALU.subtract, ALU.mult).then_inc(xn_ready, 1)
                paired(dve, norm)

            @block.gpsimd
            def _(pool):
                pool.sem_inc(xn_kept, DEPTH)

                def keep(t, p):
                    pool.wait_ge(xn_ready, done(t))
                    pool.tensor_copy(xn_all[:, bass.ds(t * E, E)], qn[p][:, :]).then_inc(xn_kept, 1)
                paired(pool, keep)

            @block.scalar
            def _(act):
                act.sem_inc(xT_copied, DEPTH)
                act.sem_inc(lg_out, DEPTH)
                for p in range(2):
                    act.sem_inc(xT_st[p], 16)
                act.dma_start(se13[:, :, :], se_w13.rearrange("(j p) n -> p j n", p=P)).then_inc(s_se, 16)
                act.dma_start(se2[:, :, :], se_w2.rearrange("(j p) n -> p j n", p=IH)).then_inc(s_se, 16)
                act.wait_ge(r5_in, 1)
                nc.scalar.activation(rstd[:, :], rstd[:, :], ACT.Sqrt).then_inc(r5_sq, 1)

                def copy_xT(t, p, rounds):
                    act.wait_ge(xT_done, done(t))
                    act.wait_ge(lg_done, freed(t))
                    act.wait_ge(xT_st[p], rounds * 16)
                    nc.scalar.activation(qkT[p][:, 0:KC, :], bank[:, 4 + p, 0:E].rearrange("p (c s) -> p c s", s=P),
                                         ACT.Copy).then_inc(xT_copied, 1)

                def copy_lg(t, p):
                    act.wait_ge(lg_done, done(t))
                    nc.scalar.activation(lg_all[:, bass.ds(t * NR, NR)], bank[:, 6 + p, 0:NR], ACT.Copy).then_inc(lg_out, 1)
                copy_xT(0, 0, 1)
                with act.Fori(0, T // 2 - 1) as it:
                    copy_xT(it * 2 + 1, 1, it + 1)
                    copy_lg(it * 2, 0)
                    copy_xT(it * 2 + 2, 0, it + 2)
                    copy_lg(it * 2 + 1, 1)
                copy_xT(T - 1, 1, T // 2)
                copy_lg(T - 2, 0)
                copy_lg(T - 1, 1)

            @block.sync
            def _(sp):
                with sp.Fori(0, T // 2) as it:
                    for p in range(2):
                        t = it * 2 + p
                        sp.wait_ge(xT_copied, done(t))
                        sp.dma_start(xT_all[:, bass.ds(t * E, E)], qkT[p][:, 0:KC, :].rearrange("p c s -> p (c s)")).then_inc(xT_st[p], 16)
                for p in range(2):
                    sp.wait_ge(xT_st[p], 16 * (T // 2) + 16)

            @block.tensor
            def _(pe):
                pe.sem_inc(xT_done, DEPTH)
                pe.sem_inc(lg_done, DEPTH)
                pe.wait_ge(s_r, 32)

                def transposes(t, p):
                    pe.wait_ge(xn_ready, done(t))
                    pe.wait_ge(xT_copied, freed(t))
                    for c in range(KC):
                        ins = nc.tensor.transpose(bank[:, 4 + p, c * P:(c + 1) * P], qn[p][:, c * P:(c + 1) * P], ident)
                    ins.then_inc(xT_done, 1)

                def logits(t, p):
                    pe.wait_ge(xT_copied, done(t))
                    pe.wait_ge(lg_out, freed(t))
                    for c in range(KC):
                        ins = nc.tensor.matmul(bank[:, 6 + p, 0:NR], qkT[p][:, c, :], rw[:, c, :], start=(c == 0), stop=(c == KC - 1))
                    ins.then_inc(lg_done, 1)

                def step(t, p):
                    transposes(t + 1, 1 - p)
                    logits(t, p)
                transposes(0, 0)
                paired(pe, step, 0, T - 2)
                step(T - 2, 0)
                logits(T - 1, 1)

        def up(p, xt_buf, w, at_w):
            for c in range(KC):
                ins = nc.tensor.matmul(bank[:, p, 0:I2], xt_buf[:, c, :], w[:, at_w + c * I2:at_w + (c + 1) * I2],
                                       start=(c == 0), stop=(c == KC - 1))
            return ins

        def turn(p):
            for c in range(2):
                ins = nc.tensor.transpose(bank[0:IH, 4 + p, c * P:(c + 1) * P], hb[p][:, c * IH:(c + 1) * IH], ident)
            return ins

        def down(p, ybank, w, at_w, first, last):
            for c in range(2):
                ins = nc.tensor.matmul(bank[:, ybank, 0:E], hT[p][:, c, :], w[:, at_w + c * E:at_w + (c + 1) * E],
                                       start=(first and c == 0), stop=(last and c == 1))
            return ins

        def shared_sems(stage):
            return SharedSems(lambda name: sem(f"{name}_{stage}"))

        R = 2 * SUB

        def shared_loads(sp, f, first, tiles):
            def load(t, p):
                sp.dma_start(xT[p][:, :, :].rearrange("p c s -> p (c s)"), xT_all[:, bass.ds((t + first) * E, E)]).then_inc(f.xs_in[p], 16)
            load(0, 0)
            load(1, 1)
            if tiles == 2:
                return
            with sp.Fori(1, tiles // 2) as it:
                for p in range(2):
                    sp.wait_ge(f.sgu_done, (it - 1) * R + p * SUB + SUB + DEPTH)
                    load(it * 2 + p, p)

        def shared_start(pe, f):
            pe.sem_inc(f.sgu_done, DEPTH)
            pe.sem_inc(f.shT_done, DEPTH)
            pe.sem_inc(f.sy_done, DEPTH)

        def pe_up(pe, f, s, j, rounds):
            if j % SUB == 0:
                pe.wait_ge(f.xs_in[j // SUB], rounds * 16)
            pe.wait_ge(f.sh_ready, freed(s))
            up(j % 2, xT[j // SUB], se13[:, j % SUB, :], 0).then_inc(f.sgu_done, 1)

        def pe_turn(pe, f, s, j):
            pe.wait_ge(f.sh_ready, done(s))
            pe.wait_ge(f.shT_ready, freed(s))
            turn(j % 2).then_inc(f.shT_done, 1)

        def pe_down(pe, f, s, t, j):
            if j % SUB == 0:
                pe.wait_ge(f.sy_out, freed(t))
            pe.wait_ge(f.shT_ready, done(s))
            ins = down(j % 2, 6 + j // SUB, se2[:, j % SUB, :], 0, j % SUB == 0, j % SUB == SUB - 1)
            ins.then_inc(f.sy_done, 1)

        def shared_step(pe, f, it, j, lag):
            s = it * R + j
            pe_up(pe, f, s, j, it + 1)
            if lag or j >= 1:
                pe_turn(pe, f, s - 1, (j - 1) % R)
            if lag or j >= 2:
                t2 = it * 2 + (j - 2) // SUB if j >= 2 else it * 2 - 1
                pe_down(pe, f, s - 2, t2, (j - 2) % R)

        def shared_end(pe, f, tiles):
            n = tiles * SUB
            pe_turn(pe, f, n - 1, R - 1)
            pe_down(pe, f, n - 2, tiles - 1, R - 2)
            pe_down(pe, f, n - 1, tiles - 1, R - 1)

        def shared_products(pe, f, tiles):
            shared_start(pe, f)
            for j in range(R):
                shared_step(pe, f, 0, j, False)
            with pe.Fori(1, tiles // 2) as it:
                for j in range(R):
                    shared_step(pe, f, it, j, True)
            shared_end(pe, f, tiles)

        def silu(act, f, s, p):
            act.wait_ge(f.sgu_done, done(s))
            act.wait_ge(f.sh_ready, freed(s))
            nc.scalar.activation(sg[p][:, :], bank[:, p, 0:I], ACT.Silu).then_inc(f.ssg_ready, 1)

        def copy_hT(act, f, s, p):
            act.wait_ge(f.shT_done, done(s))
            act.wait_ge(f.sy_done, freed(s))
            nc.scalar.activation(hT[p][:, :, :], bank[0:IH, 4 + p, 0:2 * P].rearrange("p (c s) -> p c s", s=P),
                                 ACT.Copy).then_inc(f.shT_ready, 1)

        def shared_copies(act, f, tiles):
            n = tiles * SUB
            act.sem_inc(f.ssg_ready, DEPTH)
            act.sem_inc(f.shT_ready, DEPTH)

            def step(s, p):
                silu(act, f, s + 1, 1 - p)
                copy_hT(act, f, s, p)
            silu(act, f, 0, 0)
            paired(act, step, 0, n - 2)
            step(n - 2, 0)
            copy_hT(act, f, n - 1, 1)

        def gate_up(eng, f, s, p, up_half):
            eng.wait_ge(f.ssg_ready, done(s))
            eng.wait_ge(f.shT_done, freed(s))
            eng.tensor_tensor(hb[p][:, :], sg[p][:, :], up_half, ALU.mult).then_inc(f.sh_ready, 1)

        def keep(dve, f, t, p, first):
            dve.wait_ge(f.sy_done, done(t * SUB + SUB - 1))
            xs = x_all[:, bass.ds((t + first) * E, E)]
            return nc.vector.scalar_tensor_tensor(xs, bank[:, 6 + p, 0:E], sgate[:, bass.ds(t + first, 1)], xs, ALU.mult, ALU.add).then_inc(f.sy_out, 1)

        def tn(v, n=NE):
            return v.rearrange("p (t n) -> p t n", n=n)

        e_in, e_out, oh_ready, count_done, count_out, rank_done, rank_out, eob_ready, eobT_done, slots_ready = (
            sem(n) for n in ("e_in", "e_out", "oh_ready", "count_done", "count_out", "rank_done", "rank_out", "eob_ready", "eobT_done", "slots_ready"))
        f6 = shared_sems(6)
        HB = T // 2
        with nc.Block() as block:
            @block.vector
            def _(dve):
                step = lambda ins: after(dve, dve_step, ins)
                lg = tn(lg_all, NR)
                for t in range(T):
                    ins = nc.vector.max(top[:, t, :], lg_all[:, t * NR:t * NR + NE])
                step(ins)
                for t in range(T):
                    ins = nc.vector.max_index(topi[:, t, :], top[:, t, :], lg_all[:, t * NR:t * NR + NE])
                step(ins)
                nc.vector.tensor_tensor(tn(prob), lg[:, :, 0:NE], top[:, :, 0].unsqueeze(2).to_broadcast([P, T, NE]), ALU.subtract)
                step(nc.vector.tensor_copy(topf[:, :, :], topi[:, :, 0:K4]))
                nc.vector.tensor_copy(sgate[:, :], lg[:, :, NE])
                nc.vector.tensor_tensor(tn(wk[:, :], K4), top[:, :, 0:K4], top[:, :, 0].unsqueeze(2).to_broadcast([P, T, K4]), ALU.subtract).then_inc(e_in, 1)
                for k in range(K4):
                    ins = nc.vector.tensor_tensor(tn(oh[k]), iota_e.unsqueeze(1).to_broadcast([P, T, NE]),
                                                  topf[:, :, k].unsqueeze(2).to_broadcast([P, T, NE]), ALU.is_equal)
                ins.then_inc(oh_ready, 1)
                dve.wait_ge(e_out, 1)
                step(nc.vector.tensor_reduce(zsum[:, :], tn(prob), AX.X, ALU.add))
                nc.vector.tensor_scalar(sgate[:, :], sgate[:, :], 1.0, None, ALU.add)
                step(nc.vector.reciprocal(zsum[:, :], zsum[:, :]))
                nc.vector.tensor_scalar(zsum[:, :], zsum[:, :], gf[:, 0:1], None, ALU.mult)
                step(nc.vector.reciprocal(sgate[:, :], sgate[:, :]))
                nc.vector.tensor_scalar(sgate[:, :], sgate[:, :], gf[:, 0:1], None, ALU.mult)
                step(nc.vector.tensor_tensor(tn(wk[:, :], K4), tn(wk[:, :], K4), zsum[:, :].unsqueeze(2).to_broadcast([P, T, K4]), ALU.mult))
                dve.wait_ge(count_done, 1)
                pad = 8 * NE
                for b in range(2):
                    nc.vector.tensor_copy(tcum[0][:, pad + (1 + b * HB) * NE:pad + min((1 + (b + 1) * HB), T) * NE] if b == 0 else
                                          tcum[0][:, pad + (1 + HB) * NE:pad + T * NE],
                                          bank[:, 2 + b, 0:HB * NE] if b == 0 else bank[:, 2 + b, 0:(HB - 1) * NE])
                nc.vector.tensor_copy(cnt[:, :], bank[:, 3, (HB - 1) * NE:HB * NE]).then_inc(count_out, 1)
                nc.vector.memset(ecum[0][:, 0:EP], 0.0)
                nc.vector.memset(ecum[1][:, 0:EP], 0.0)
                nc.vector.memset(tcum[1][:, 0:pad], 0.0)
                step(nc.vector.memset(tcum[0][:, 0:pad + NE], 0.0))
                k, sh = 0, 1
                while sh < T:
                    step(nc.vector.tensor_tensor(tcum[1 - k][:, pad:], tcum[k][:, pad:], tcum[k][:, pad - sh * NE:pad + (T - sh) * NE], ALU.add))
                    k, sh = 1 - k, 2 * sh
                tex = tcum[k][:, pad:]
                step(nc.vector.tensor_tensor(cnt[:, :], cnt[:, :], tex[:, (T - 1) * NE:T * NE], ALU.add))
                step(nc.vector.tensor_tensor(cmp[:, :, :], cnt[:, :].unsqueeze(2).to_broadcast([P, NE, T]),
                                             fills.unsqueeze(1).to_broadcast([P, NE, T]), ALU.is_gt))
                step(nc.vector.tensor_reduce(nblk[:, :], cmp[:, :, :], AX.X, ALU.add))
                step(nc.vector.tensor_copy(ecum[0][:, EP:], nblk[:, :]))
                k, sh = 0, 1
                while sh < NE:
                    step(nc.vector.tensor_tensor(ecum[1 - k][:, EP:], ecum[k][:, EP:], ecum[k][:, EP - sh:EP + NE - sh], ALU.add))
                    k, sh = 1 - k, 2 * sh
                ends = ecum[k][:, EP:]
                nc.vector.tensor_tensor(nblk[:, :], ends, nblk[:, :], ALU.subtract)
                step(nc.vector.tensor_scalar(cmp[:, :, 0], ends, iota_p, None, ALU.is_le))
                step(nc.vector.tensor_reduce(eob[:, :], cmp[:, :, 0], AX.X, ALU.add))
                nc.vector.tensor_scalar(eob[:, :], eob[:, :], float(NE - 1), None, ALU.min).then_inc(eob_ready, 1)
                step(nc.vector.tensor_scalar(last_f[:, :], ends[:, NE - 1:NE], 1.0 / WB, -1.0, ALU.mult, ALU.add))
                step(nc.vector.tensor_scalar(cmp[:, :, 1], iota_e, last_f[:, 0:1], None, ALU.is_lt))
                step(nc.vector.tensor_reduce(last_f[:, :], cmp[:, :, 1], AX.X, ALU.add))
                nc.vector.tensor_copy(eob_row[0:1, P:P + 1], last_f[0:1, :])
                step(nc.vector.tensor_scalar(nblk[:, :], nblk[:, :], float(P), None, ALU.mult))
                step(nc.vector.tensor_tensor(tn(pos), tn(tex), nblk[:, :].unsqueeze(1).to_broadcast([P, T, NE]), ALU.add))
                dve.wait_ge(rank_done, 1)
                for b in range(2):
                    r = slice(b * HB * NE, (b + 1) * HB * NE)
                    ins = nc.vector.tensor_tensor(pos[:, r], pos[:, r], bank[:, 2 + b, 0:HB * NE], ALU.add)
                ins.then_inc(rank_out, 1)
                dve.wait_ge(rank_out, 1)
                for kk in range(K4):
                    step(nc.vector.tensor_tensor(prob, pos, oh[kk], ALU.mult))
                    step(nc.vector.tensor_reduce(slotf[:, :, kk], tn(prob), AX.X, ALU.add))
                nc.vector.tensor_copy(tn(slotu[:, :], K4), slotf[:, :, :]).then_inc(slots_ready, 1)
                dve.wait_ge(eobT_done, 1)
                nc.vector.tensor_copy(eob_row[0:1, 0:P], bank[0:1, 2, 0:P])

            @block.sync
            def _(sp):
                shared_loads(sp, f6, 0, TA)

            @block.gpsimd
            def _(pool):
                pool.sem_inc(f6.sh_ready, DEPTH)
                paired(pool, lambda s, p: gate_up(pool, f6, s, p, ub[p][:, :]), 0, TA * SUB)

            @block.scalar
            def _(act):
                act.sem_inc(f6.ssg_ready, DEPTH)
                act.sem_inc(f6.shT_ready, DEPTH)
                act.sem_inc(f6.sy_out, DEPTH)

                def copy_y(t):
                    act.wait_ge(f6.sy_done, done(t * SUB + SUB - 1))
                    nc.scalar.activation(ysh[:, t * E:(t + 1) * E], bank[:, 6 + t % 2, 0:E], ACT.Copy).then_inc(f6.sy_out, 1)

                def silu_and_up(s, p):
                    act.wait_ge(f6.sgu_done, done(s))
                    act.wait_ge(f6.sh_ready, freed(s))
                    nc.scalar.activation(sg[p][:, :], bank[:, p, 0:I], ACT.Silu)
                    nc.scalar.activation(ub[p][:, :], bank[:, p, I:I2], ACT.Copy).then_inc(f6.ssg_ready, 1)
                silu_and_up(0, 0)
                for s in range(TA * SUB):
                    if s + 1 < TA * SUB:
                        silu_and_up(s + 1, (s + 1) % 2)
                    if s == 3:
                        act.wait_ge(e_in, 1)
                        nc.scalar.activation(prob, prob, ACT.Exp)
                        nc.scalar.activation(wk[:, :], wk[:, :], ACT.Exp)
                        nc.scalar.activation(sgate[:, :], sgate[:, :], ACT.Exp, scale=-1.0)
                        nc.scalar.activation(gf[:, :], gf[:, :], ACT.Tanh).then_inc(e_out, 1)
                    copy_hT(act, f6, s, s % 2)
                    if s % SUB == 2 and s > SUB:
                        copy_y(s // SUB - 1)
                copy_y(TA - 1)

            @block.tensor
            def _(pe):
                def over_experts(lhs):
                    for b in range(2):
                        for q in range(K4):
                            ins = nc.tensor.matmul(bank[:, 2 + b, 0:HB * NE], lhs[:, :], oh[q][:, b * HB * NE:(b + 1) * HB * NE],
                                                   start=(q == 0), stop=(q == K4 - 1))
                    return ins
                pe.wait_ge(s_se, 32)
                shared_start(pe, f6)
                for it in range(TA // 2):
                    for j in range(R):
                        shared_step(pe, f6, it, j, it > 0)
                        if it * R + j == 4:
                            pe.wait_ge(oh_ready, 1)
                            over_experts(ones_b).then_inc(count_done, 1)
                        if it * R + j == 7:
                            pe.wait_ge(count_out, 1)
                            over_experts(tri_b).then_inc(rank_done, 1)
                shared_end(pe, f6, TA)
                pe.wait_ge(eob_ready, 1)
                pe.wait_ge(rank_out, 1)
                nc.tensor.matmul(bank[0:1, 2, 0:P], eob[:, 0:1], ident, start=True, stop=True).then_inc(eobT_done, 1)

        scattered, rest_cleared = sem("scattered"), sem("rest_cleared")
        w_in = [sem(f"w_in{b}") for b in range(WB)]
        f7 = shared_sems(7)
        with nc.Block() as block:
            @block.gpsimd
            def _(pool):
                pool.wait_ge(cleared, 16 * NZ)
                pool.wait_ge(slots_ready, 1)
                for t in range(T):
                    for k in range(K4):
                        c = t * K4 + k
                        pool.indirect_dma_start(slot_x[:, :], bass.IndirectOffsetOnAxis(slotu[:, c:c + 1], 0),
                                                xn_all[:, t * E:(t + 1) * E], None).then_inc(scattered, 16)
                pool.wait_ge(scattered, 16 * T * K4)

            @block.sync
            def _(sp):
                shared_loads(sp, f7, TA, TB)
                for b in range(WB):
                    e = sp.value_load(eob_row[0:1, b:b + 1], min_val=0, max_val=NE - 1)
                    sp.dma_start(wa[b][:, :], w13[bass.ds(e * P, P), :]).then_inc(w_in[b], 16)
                last = sp.value_load(eob_row[0:1, P:P + 1], min_val=N * K4 // P // WB - 1, max_val=NB // WB - 1)
                with sp.Fori(N * K4 // P // WB, NB // WB) as it:
                    with sp.If(it <= last):
                        sp.sem_inc(rest_cleared, 16)
                    with sp.Else():
                        sp.dma_start(slot_y[bass.ds(it * (WB * P), WB * P), :].rearrange("(p n) e -> p (n e)", p=P),
                                     zeros[:, 0:WB * E]).then_inc(rest_cleared, 16)
                sp.wait_ge(rest_cleared, 16 * (NB - N * K4 // P) // WB)

            @block.tensor
            def _(pe):
                shared_products(pe, f7, TB)

            @block.scalar
            def _(act):
                shared_copies(act, f7, TB)

            @block.vector
            def _(dve):
                dve.sem_inc(f7.sh_ready, DEPTH)
                dve.sem_inc(f7.sy_out, DEPTH)

                def tile(t, p, lag):
                    for j in range(SUB):
                        gate_up(dve, f7, t * SUB + j, j % 2, bank[:, j % 2, I:I2])
                        if j == 2 and lag:
                            keep(dve, f7, t - 1, 1 - p, TA)
                tile(0, 0, False)
                for t in range(TA):
                    xs = x_all[:, t * E:(t + 1) * E]
                    nc.vector.scalar_tensor_tensor(xs, ysh[:, t * E:(t + 1) * E], sgate[:, t:t + 1], xs, ALU.mult, ALU.add)
                tile(1, 1, True)
                with dve.Fori(1, TB // 2) as it:
                    for p in range(2):
                        tile(it * 2 + p, p, True)
                keep(dve, f7, TB - 1, 1, TA)

        v_in = [sem(f"v_in{b}") for b in range(WB)]
        r_in = [sem(f"r_in{b}") for b in range(WB)]
        y_st = [sem(f"y_st{b}") for b in range(WB)]
        bx_done, bx_ready, bgu_done, bsg_ready, bh_ready, bhT_done, bhT_ready, by_done, by_ready = (
            sem(n) for n in ("bx_done", "bx_ready", "bgu_done", "bsg_ready", "bh_ready", "bhT_done", "bhT_ready", "by_done", "by_ready"))

        def in_use(eng, first, step):
            last = eng.value_load(eob_row[0:1, P:P + 1], min_val=N * K4 // P // WB - 1, max_val=NB // WB - 1)
            with eng.Fori(first, NB // WB) as it:
                with eng.If(it <= last):
                    step(it, last)
            return last

        with nc.Block() as block:
            @block.sync
            def _(sp):
                def load(i, b):
                    e = sp.value_load(eob_row[0:1, bass.ds(i, 1)], min_val=0, max_val=NE - 1)
                    sp.wait_ge(bx_done, i - WB + 1 + DEPTH)
                    sp.dma_start(xg[b][:, :], slot_x[bass.ds(i * P, P), :]).then_inc(r_in[b], 16)
                    sp.wait_ge(bgu_done, i - WB + 1 + DEPTH)
                    sp.dma_start(wa[b][:, :], w13[bass.ds(e * P, P), :]).then_inc(w_in[b], 16)
                for b in range(WB):
                    sp.dma_start(xg[b][:, :], slot_x[b * P:(b + 1) * P, :]).then_inc(r_in[b], 16)

                def round_(it, _):
                    for b in range(WB):
                        load(it * WB + b, b)
                in_use(sp, 1, round_)

            @block.gpsimd
            def _(pool):
                def load(i, b):
                    e = pool.value_load(eob_row[0:1, bass.ds(i, 1)], min_val=0, max_val=NE - 1)
                    pool.dma_start(wb[b][:, :], w2[bass.ds(e * IH, IH), :]).then_inc(v_in[b], 16)

                def store(i, b):
                    pool.wait_ge(by_ready, done(i))
                    pool.dma_start(slot_y[bass.ds(i * P, P), :], yb[b][:, :]).then_inc(y_st[b], 16)
                for b in range(WB):
                    load(b, b)

                def round_(it, _):
                    for b in range(WB):
                        pool.wait_ge(by_done, (it - 1) * WB + b + 1 + DEPTH)
                        load(it * WB + b, b)
                        store((it - 1) * WB + b, b)
                last = in_use(pool, 1, round_)
                for b in range(WB):
                    store(last * WB + b, b)
                for b in range(WB):
                    pool.wait_ge(y_st[b], last * 16 + 16)

            @block.tensor
            def _(pe):
                pe.sem_inc(bx_done, DEPTH)
                pe.sem_inc(bgu_done, DEPTH)
                pe.sem_inc(bhT_done, DEPTH)
                pe.sem_inc(by_done, DEPTH)

                def rows(i, b, rounds):
                    pe.wait_ge(r_in[b], rounds * 16)
                    pe.wait_ge(bx_ready, freed(i))
                    for c in range(KC):
                        ins = nc.tensor.transpose(bank[:, 2 + b % 2, c * P:(c + 1) * P], xg[b][:, c * P:(c + 1) * P], ident)
                    ins.then_inc(bx_done, 1)

                def pe_up(i, b, rounds):
                    pe.wait_ge(w_in[b], rounds * 16)
                    pe.wait_ge(bx_ready, done(i))
                    pe.wait_ge(bh_ready, freed(i))
                    up(b % 2, xT[b % 2], wa[b], 0).then_inc(bgu_done, 1)

                def pe_turn(i, b):
                    pe.wait_ge(bh_ready, done(i))
                    pe.wait_ge(bhT_ready, freed(i))
                    turn(b % 2).then_inc(bhT_done, 1)

                def pe_down(i, b, rounds):
                    pe.wait_ge(v_in[b], rounds * 16)
                    pe.wait_ge(bhT_ready, done(i))
                    pe.wait_ge(by_ready, freed(i))
                    down(b % 2, 6 + b % 2, wb[b], 0, True, True).then_inc(by_done, 1)

                def body(it, lag, last):
                    for b in range(WB):
                        i = it * WB + b
                        if b < WB - 1:
                            rows(i + 1, b + 1, it + 1)
                        elif last is None:
                            rows(i + 1, 0, it + 2)
                        else:
                            with pe.If(it < last):
                                rows(i + 1, 0, it + 2)
                        pe_up(i, b, it + 1)
                        if lag or b >= 1:
                            pe_turn(i - 1, (b - 1) % WB)
                        if lag or b >= 2:
                            pe_down(i - 2, (b - 2) % WB, it + 1 if b >= 2 else it)
                rows(0, 0, 1)
                body(0, False, None)
                last = in_use(pe, 1, lambda it, last: body(it, True, last))
                pe_turn(last * WB + WB - 1, WB - 1)
                pe_down(last * WB + WB - 2, WB - 2, last + 1)
                pe_down(last * WB + WB - 1, WB - 1, last + 1)

            @block.scalar
            def _(act):
                act.sem_inc(bsg_ready, DEPTH)
                act.sem_inc(bhT_ready, DEPTH)
                act.sem_inc(by_ready, DEPTH)

                def silu(i, b):
                    act.wait_ge(bgu_done, done(i))
                    act.wait_ge(bh_ready, freed(i))
                    nc.scalar.activation(sg[b % 2][:, :], bank[:, b % 2, 0:I], ACT.Silu).then_inc(bsg_ready, 1)

                def copy_hT(i, b):
                    act.wait_ge(bhT_done, done(i))
                    act.wait_ge(by_done, freed(i))
                    nc.scalar.activation(hT[b % 2][:, :, :], bank[0:IH, 4 + b % 2, 0:2 * P].rearrange("p (c s) -> p c s", s=P),
                                         ACT.Copy).then_inc(bhT_ready, 1)

                def copy_y(i, b, rounds):
                    act.wait_ge(by_done, done(i))
                    if rounds is not None:
                        act.wait_ge(y_st[b], rounds * 16)
                    nc.scalar.activation(yb[b][:, :], bank[:, 6 + b % 2, 0:E], ACT.Copy).then_inc(by_ready, 1)

                def body(it, lag, again):
                    for b in range(WB):
                        i = it * WB + b
                        silu(i, b)
                        if lag or b >= 1:
                            copy_hT(i - 1, (b - 1) % WB)
                        if lag or b >= 2:
                            rounds = (it if b >= 2 else it - 1) if again or b >= 2 and lag else None
                            copy_y(i - 2, (b - 2) % WB, rounds)
                body(0, False, False)
                body(1, True, False)
                last = in_use(act, 2, lambda it, _: body(it, True, True))
                copy_hT(last * WB + WB - 1, WB - 1)
                copy_y(last * WB + WB - 2, WB - 2, last)
                copy_y(last * WB + WB - 1, WB - 1, last)

            @block.vector
            def _(dve):
                dve.sem_inc(bx_ready, DEPTH)
                dve.sem_inc(bh_ready, DEPTH)

                def copy_x(i, b):
                    dve.wait_ge(bx_done, done(i))
                    dve.wait_ge(bgu_done, freed(i))
                    nc.vector.tensor_copy(xT[b % 2][:, :, :], bank[:, 2 + b % 2, 0:E].rearrange("p (c s) -> p c s", s=P)).then_inc(bx_ready, 1)

                def mul(i, b):
                    dve.wait_ge(bsg_ready, done(i))
                    dve.wait_ge(bhT_done, freed(i))
                    nc.vector.tensor_tensor(hb[b % 2][:, :], sg[b % 2][:, :], bank[:, b % 2, I:I2], ALU.mult).then_inc(bh_ready, 1)

                def round_(it, last):
                    for b in range(WB):
                        i = it * WB + b
                        if b < WB - 1:
                            copy_x(i + 1, b + 1)
                        else:
                            with dve.If(it < last):
                                copy_x(i + 1, 0)
                        mul(i, b)
                copy_x(0, 0)
                in_use(dve, 0, round_)

        YB = 8
        yg = [b[:, i * E:(i + 1) * E] for b in (dd[2], dd[3]) for i in range(4)]
        yg_in = [sem(f"yg_in{b}") for b in range(YB)]
        added, s_out = sem("added"), sem("s_out")
        f9 = shared_sems(9)
        with nc.Block() as block:
            @block.gpsimd
            def _(pool):
                for c in range(T * K4):
                    if c >= YB:
                        pool.wait_ge(added, c - YB + 1)
                    pool.indirect_dma_start(yg[c % YB], None, slot_y[:, :],
                                            bass.IndirectOffsetOnAxis(slotu[:, c:c + 1], 0)).then_inc(yg_in[c % YB], 16)

            @block.tensor
            def _(pe):
                shared_products(pe, f9, TC)

            @block.scalar
            def _(act):
                shared_copies(act, f9, TC)

            @block.vector
            def _(dve):
                dve.sem_inc(f9.sh_ready, DEPTH)
                dve.sem_inc(f9.sy_out, DEPTH)

                def add(c):
                    t = c // K4
                    if t >= TA + TB:
                        dve.wait_ge(f9.sy_out, done(t - TA - TB))
                    dve.wait_ge(yg_in[c % YB], 16 * (c // YB + 1))
                    if c:
                        dve.wait_ge(added, c)
                    xs = x_all[:, t * E:(t + 1) * E]
                    nc.vector.scalar_tensor_tensor(xs, yg[c % YB], wk[:, c:c + 1], xs, ALU.mult, ALU.add).then_inc(added, 1)

                for s in range(TC * SUB):
                    gate_up(dve, f9, s, s % 2, bank[:, s % 2, I:I2])
                    add(2 * s)
                    if s % SUB == 2 and s > SUB:
                        keep(dve, f9, s // SUB - 1, (s // SUB - 1) % 2, TA + TB)
                    add(2 * s + 1)
                keep(dve, f9, TC - 1, (TC - 1) % 2, TA + TB)
                for c in range(2 * TC * SUB, T * K4):
                    add(c)

            @block.sync
            def _(sp):
                shared_loads(sp, f9, TA + TB, TC)
                for t in range(T):
                    sp.wait_ge(added, K4 * (t + 1))
                    sp.dma_start(out[t * P:(t + 1) * P, :], x_all[:, t * E:(t + 1) * E]).then_inc(s_out, 16)
                sp.wait_ge(s_out, 16 * T)


def kernel(x, ctx_2048, g_xattn, g_ffn, L0_xattn_Wi, L0_xattn_bi, L0_xattn_Wf, L0_xattn_bf, L0_xattn_ln_scale,
           L0_ffn_gate_w, L0_ffn_shared_gate_w, L0_ffn_w13, L0_ffn_w2, L0_ffn_se_gate_up_w, L0_ffn_se_down_w):
    import numpy as np
    import concourse.bacc as bacc
    from concourse.bass_utils import run_bass_kernel_spmd

    P, S, DH = 128, 64, 16
    row, col = np.arange(P)[:, None], np.arange(P)[None, :]
    same = row // S == col // S
    consts = np.concatenate([
        row == col,
        (row <= col) & same,
        row < col,
        (row // DH == np.arange(P // DH)[None, :]) * DH ** -0.5,
        np.where(row % S > np.arange(S)[None, :], -1.0e30, 0.0),
        np.arange(L0_ffn_w2.shape[0])[None, :] + 0 * row,
        row,
        P * np.arange(x.size // x.shape[-1] // P)[None, :] + 0 * row,
        row // S == np.arange(P // S)[None, :],
    ], axis=1).astype(np.float32)

    def swapped(a):
        return np.ascontiguousarray(np.swapaxes(a, -1, -2))

    def width_first(w):
        e, n, k = w.shape
        return swapped(w).reshape(e, k // P, P, n).transpose(0, 2, 1, 3).reshape(e * P, -1)

    def inner_first(w):
        e, k, n = w.shape
        return swapped(w).reshape(e, 2, n // 2, k).transpose(0, 2, 1, 3).reshape(e * n // 2, -1)

    I = L0_ffn_w2.shape[2]
    se_gu = L0_ffn_se_gate_up_w.reshape(2, -1, I, L0_ffn_se_gate_up_w.shape[1])
    se_d = L0_ffn_se_down_w

    arrays = {
        "x": np.ascontiguousarray(x).reshape(-1, x.shape[-1]),
        "ctx": np.ascontiguousarray(ctx_2048).reshape(-1, x.shape[-1]),
        "w_i": L0_xattn_Wi, "b_i": L0_xattn_bi, "w_f": L0_xattn_Wf, "b_f": L0_xattn_bf,
        "ln_scale": L0_xattn_ln_scale, "g_x": g_xattn, "g_f": g_ffn,
        "router_w": np.concatenate([swapped(L0_ffn_gate_w), swapped(L0_ffn_shared_gate_w)], axis=1),
        "w13": width_first(L0_ffn_w13), "w2": inner_first(L0_ffn_w2),
        "se_w13": width_first(np.concatenate([se_gu[0], se_gu[1]], axis=1)),
        "se_w2": inner_first(np.swapaxes(se_d.reshape(se_d.shape[0], -1, I), 0, 1)),
        "consts": consts,
    }
    nc = bacc.Bacc("TRN2", target_bir_lowering=False, num_devices=1)
    arrays = {k: np.ascontiguousarray(v) for k, v in arrays.items()}
    aps = {k: nc.dram_tensor(f"in_{k}", v.shape, mybir.dt.from_np(v.dtype), kind="ExternalInput").ap() for k, v in arrays.items()}
    out = nc.dram_tensor("out_0", arrays["x"].shape, mybir.dt.float32, kind="ExternalOutput").ap()
    flamingo_layer(nc, out=out, **aps)
    r = run_bass_kernel_spmd(nc, [{f"in_{k}": v for k, v in arrays.items()}], core_ids=[0])
    return r.results[0]["out_0"].reshape(x.shape)
```
